# Optimizing a Trainium2 kernel written in Bass

```python
import numpy as np
import jax
import jax.numpy as jnp

def _softmax(x, axis=-1):
    return jax.nn.softmax(x, axis=axis)

def _gelu(x):
    return jax.nn.gelu(x, approximate=True)

def _silu(x):
    return jax.nn.silu(x)

def _sigmoid(x):
    return jax.nn.sigmoid(x)

def _layernorm(x, axis=-1, eps=1e-05):
    m = jnp.mean(x, axis=axis, keepdims=True)
    v = jnp.var(x, axis=axis, keepdims=True)
    return (x - m) / jnp.sqrt(v + eps)

def _scatter_add(tgt, idx, src, axis=0):
    return tgt.at[idx].add(src)

def _segment_sum(src, seg, n):
    return jax.ops.segment_sum(src, seg, n)
kernel_name = 'mk_vit_tower_d2_tok_img1024_r4_03b696'

def setup_inputs(seed: int=0):
    np.random.seed(seed)
    _w = jnp.asarray

    def _rec_inputs():
        import jax
        import jax.numpy as jnp
        _rk = jax.random.key(seed)
        x = -0.00150118 + 0.499729 * jax.random.normal(jax.random.fold_in(_rk, 1), (8, 256, 64, 2), jnp.float32)
        return x
    x = _rec_inputs()

    def _L0_tok_setup():
        import jax, jax.numpy as jnp
        import numpy as np
        import math
        H = 256
        N = 64
        CH = 1
        SEQ_L = 256
        key = jax.random.key(seed)
        k1, k2, k3, k4 = jax.random.split(key, 4)
        log_dt = jax.random.uniform(k1, (H,), dtype=jnp.float32, minval=math.log(0.001), maxval=math.log(0.1))
        inv_A_real = jnp.log(0.5 * jnp.ones((H, N), jnp.float32)) + 0.1 * jax.random.normal(k2, (H, N), dtype=jnp.float32)
        A_imag = jnp.broadcast_to(math.pi * jnp.arange(N, dtype=jnp.float32), (H, N)).copy()
        B_ri = jax.random.normal(k3, (H, N, 2), dtype=jnp.float32) * 0.5
        C_ri = jax.random.normal(k4, (CH, H, N, 2), dtype=jnp.float32) * 0.5
        return {'log_dt': log_dt, 'inv_A_real': inv_A_real, 'A_imag': A_imag, 'B_ri': B_ri, 'C_ri': C_ri, 'L': SEQ_L}
    _L0_tok_all = _L0_tok_setup()
    _L0_tok_in = {k: v for k, v in _L0_tok_all.items() if k in ('log_dt', 'inv_A_real', 'A_imag', 'B_ri')}
    del _L0_tok_all

    def _L0_attn_setup():
        import jax, jax.numpy as jnp
        import numpy as np
        NUM_HEADS = 1
        LN_EPS = 1e-05
        key = jax.random.key(seed)
        ks = jax.random.split(key, 4)
        B, L, D = (8, 1024, 256)
        x = jax.random.normal(ks[0], (B, L, D), dtype=jnp.float32)
        qkv_w = jax.random.normal(ks[1], (3 * D, D), dtype=jnp.float32) * np.float32(np.sqrt(1.0 / D))
        qkv_b = jnp.zeros((3 * D,), dtype=jnp.float32)
        proj_w = jax.random.normal(ks[2], (D, D), dtype=jnp.float32) * np.float32(np.sqrt(1.0 / D))
        proj_b = jnp.zeros((D,), dtype=jnp.float32)
        return {'x': x, 'norm_w': jnp.ones((D,), dtype=jnp.float32), 'norm_b': jnp.zeros((D,), dtype=jnp.float32), 'qkv_w': qkv_w, 'qkv_b': qkv_b, 'proj_w': proj_w, 'proj_b': proj_b}
    _L0_attn_all = _L0_attn_setup()
    _L0_attn_in = {k: v for k, v in _L0_attn_all.items() if k in ('norm_w', 'norm_b', 'qkv_w', 'qkv_b', 'proj_w', 'proj_b')}
    del _L0_attn_all

    def _L0_ffn_setup():
        import jax, jax.numpy as jnp
        import numpy as np
        DIM = 256

        def _reference_tuple_inner(x, W_r, W_k, W_v, mu_r, mu_k):
            B, T, C = x.shape
            x_prev = jnp.concatenate([jnp.zeros((B, 1, C), x.dtype), x[:, :-1, :]], axis=1)
            xr = mu_r * x + (1.0 - mu_r) * x_prev
            xk = mu_k * x + (1.0 - mu_k) * x_prev
            r = jax.nn.sigmoid(jnp.einsum('btc,dc->btd', xr, W_r))
            k = jnp.einsum('btc,dc->btd', xk, W_k)
            k_act = jnp.square(jax.nn.relu(k))
            out = r * jnp.einsum('btc,dc->btd', k_act, W_v)
            new_state = x[:, -1, :]
            return (out, new_state)
        key = jax.random.key(seed)
        ks = jax.random.split(key, 6)
        B, T, C = (8, 512, DIM)
        x = jax.random.normal(ks[0], (B, T, C), dtype=jnp.float32)
        s = 1.0 / np.sqrt(C)
        W_r = jax.random.uniform(ks[1], (C, C), jnp.float32, -s, s)
        W_k = jax.random.uniform(ks[2], (C, C), jnp.float32, -s, s)
        W_v = jax.random.uniform(ks[3], (C, C), jnp.float32, -s, s)
        mu_r = jax.random.uniform(ks[4], (C,), jnp.float32)
        mu_k = jax.random.uniform(ks[5], (C,), jnp.float32)
        return {'x': x, 'W_r': W_r, 'W_k': W_k, 'W_v': W_v, 'mu_r': mu_r, 'mu_k': mu_k}
    _L0_ffn_all = _L0_ffn_setup()
    _L0_ffn_in = {k: v for k, v in _L0_ffn_all.items() if k in ('W_r', 'W_k', 'W_v', 'mu_r', 'mu_k')}
    del _L0_ffn_all

    def _L1_attn_setup():
        import jax, jax.numpy as jnp
        import numpy as np
        D = 256
        H = 16
        K = 64
        B = 4
        T = 256
        LAYER_ID = 12
        NUM_LAYERS = 24
        D_MIX = 32
        D_DECAY = 64

        def _bidir_shift(x):
            left = jnp.pad(x[:, :-1, :], ((0, 0), (1, 0), (0, 0)))
            right = jnp.pad(x[:, 1:, :], ((0, 0), (0, 1), (0, 0)))
            return 0.5 * (left + right)

        def _lion_attention(r, k, v, w):
            Tn = r.shape[2]
            cs = jnp.cumsum(w, axis=2)
            cs_b = cs - w
            shift_f = cs[:, :, Tn // 2:Tn // 2 + 1, :]
            shift_b = cs_b[:, :, Tn // 2:Tn // 2 + 1, :]
            cf = jnp.clip(cs - shift_f, -60.0, 60.0)
            cb = jnp.clip(cs_b - shift_b, -60.0, 60.0)
            A_f = jnp.einsum('bhik,bhjk->bhij', r * jnp.exp(cf), k * jnp.exp(-cf))
            A_b = jnp.einsum('bhik,bhjk->bhij', r * jnp.exp(-cb), k * jnp.exp(cb))
            idx = jnp.arange(Tn)
            lower = idx[:, None] >= idx[None, :]
            A = jnp.where(lower, A_f, A_b)
            return jnp.einsum('bhij,bhjk->bhik', A, v)
        key = jax.random.key(seed)
        ks = jax.random.split(key, 12)
        r01 = LAYER_ID / (NUM_LAYERS - 1)
        r10 = 1.0 - LAYER_ID / NUM_LAYERS
        ddd = jnp.arange(D, dtype=jnp.float32) / D
        maa = lambda p: (1.0 - ddd ** p).reshape(1, 1, D)
        inp = {}
        inp['x'] = jax.random.normal(ks[0], (B, T, D), jnp.float32)
        inp['time_maa_x'] = maa(r10)
        inp['time_maa_w'] = maa(r10)
        inp['time_maa_k'] = maa(r10)
        inp['time_maa_v'] = (1.0 - (ddd ** r10 + 0.3 * r01)).reshape(1, 1, D)
        inp['time_maa_r'] = maa(0.5 * r10)
        inp['time_maa_g'] = maa(0.5 * r10)
        inp['time_maa_w1'] = jax.random.uniform(ks[1], (D, D_MIX * 5), jnp.float32, -0.01, 0.01)
        inp['time_maa_w2'] = jax.random.uniform(ks[2], (5, D_MIX, D), jnp.float32, -0.01, 0.01)
        n = jnp.arange(D, dtype=jnp.float32)
        inp['time_decay'] = (-6.0 + 5.0 * (n / (D - 1)) ** (0.7 + 1.3 * r01)).reshape(1, 1, D)
        inp['time_decay_w1'] = jax.random.uniform(ks[3], (D, D_DECAY), jnp.float32, -0.01, 0.01)
        inp['time_decay_w2'] = jax.random.uniform(ks[4], (D_DECAY, D), jnp.float32, -0.01, 0.01)
        for nm, kk in zip(['W_r', 'W_k', 'W_v', 'W_g', 'W_o'], ks[5:10]):
            inp[nm] = jax.random.normal(kk, (D, D), jnp.float32) * 0.02
        inp['ln_w'] = jnp.ones((D,), jnp.float32)
        inp['ln_b'] = jnp.zeros((D,), jnp.float32)
        return inp
    _L1_attn_all = _L1_attn_setup()
    _L1_attn_in = {k: v for k, v in _L1_attn_all.items() if k in ('time_maa_x', 'time_maa_w', 'time_maa_k', 'time_maa_v', 'time_maa_r', 'time_maa_g', 'time_maa_w1', 'time_maa_w2', 'time_decay', 'time_decay_w1', 'time_decay_w2', 'W_r', 'W_k', 'W_v', 'W_g', 'W_o', 'ln_w', 'ln_b')}
    del _L1_attn_all

    def _L1_ffn_setup():
        import jax, jax.numpy as jnp
        import numpy as np
        DIM = 256
        HIDDEN = 768
        SCALE = 1.0 / 127.0

        def _dequant(w_int, dtype):
            return w_int.astype(dtype) * jnp.asarray(SCALE, dtype)
        key = jax.random.key(seed)
        k_x, k_g, k_u, k_d = jax.random.split(key, 4)
        x = jax.random.normal(k_x, (4, 512, DIM), dtype=jnp.float32)
        w_gate = jax.random.randint(k_g, (HIDDEN, DIM), -127, 128, dtype=jnp.int32)
        w_up = jax.random.randint(k_u, (HIDDEN, DIM), -127, 128, dtype=jnp.int32)
        w_down = jax.random.randint(k_d, (DIM, HIDDEN), -127, 128, dtype=jnp.int32)
        return {'x': x, 'w_gate': w_gate, 'w_up': w_up, 'w_down': w_down}
    _L1_ffn_all = _L1_ffn_setup()
    _L1_ffn_in = {k: v for k, v in _L1_ffn_all.items() if k in ('w_gate', 'w_up', 'w_down')}
    del _L1_ffn_all
    return {'x': x, 'L0_tok_log_dt': _L0_tok_in['log_dt'], 'L0_tok_inv_A_real': _L0_tok_in['inv_A_real'], 'L0_tok_A_imag': _L0_tok_in['A_imag'], 'L0_tok_B_ri': _L0_tok_in['B_ri'], 'L0_attn_norm_w': _L0_attn_in['norm_w'], 'L0_attn_norm_b': _L0_attn_in['norm_b'], 'L0_attn_qkv_w': _L0_attn_in['qkv_w'], 'L0_attn_qkv_b': _L0_attn_in['qkv_b'], 'L0_attn_proj_w': _L0_attn_in['proj_w'], 'L0_attn_proj_b': _L0_attn_in['proj_b'], 'L0_ffn_W_r': _L0_ffn_in['W_r'], 'L0_ffn_W_k': _L0_ffn_in['W_k'], 'L0_ffn_W_v': _L0_ffn_in['W_v'], 'L0_ffn_mu_r': _L0_ffn_in['mu_r'], 'L0_ffn_mu_k': _L0_ffn_in['mu_k'], 'L1_attn_time_maa_x': _L1_attn_in['time_maa_x'], 'L1_attn_time_maa_w': _L1_attn_in['time_maa_w'], 'L1_attn_time_maa_k': _L1_attn_in['time_maa_k'], 'L1_attn_time_maa_v': _L1_attn_in['time_maa_v'], 'L1_attn_time_maa_r': _L1_attn_in['time_maa_r'], 'L1_attn_time_maa_g': _L1_attn_in['time_maa_g'], 'L1_attn_time_maa_w1': _L1_attn_in['time_maa_w1'], 'L1_attn_time_maa_w2': _L1_attn_in['time_maa_w2'], 'L1_attn_time_decay': _L1_attn_in['time_decay'], 'L1_attn_time_decay_w1': _L1_attn_in['time_decay_w1'], 'L1_attn_time_decay_w2': _L1_attn_in['time_decay_w2'], 'L1_attn_W_r': _L1_attn_in['W_r'], 'L1_attn_W_k': _L1_attn_in['W_k'], 'L1_attn_W_v': _L1_attn_in['W_v'], 'L1_attn_W_g': _L1_attn_in['W_g'], 'L1_attn_W_o': _L1_attn_in['W_o'], 'L1_attn_ln_w': _L1_attn_in['ln_w'], 'L1_attn_ln_b': _L1_attn_in['ln_b'], 'L1_ffn_w_gate': _L1_ffn_in['w_gate'], 'L1_ffn_w_up': _L1_ffn_in['w_up'], 'L1_ffn_w_down': _L1_ffn_in['w_down']}

def reference(x, L0_tok_log_dt, L0_tok_inv_A_real, L0_tok_A_imag, L0_tok_B_ri, L0_attn_norm_w, L0_attn_norm_b, L0_attn_qkv_w, L0_attn_qkv_b, L0_attn_proj_w, L0_attn_proj_b, L0_ffn_W_r, L0_ffn_W_k, L0_ffn_W_v, L0_ffn_mu_r, L0_ffn_mu_k, L1_attn_time_maa_x, L1_attn_time_maa_w, L1_attn_time_maa_k, L1_attn_time_maa_v, L1_attn_time_maa_r, L1_attn_time_maa_g, L1_attn_time_maa_w1, L1_attn_time_maa_w2, L1_attn_time_decay, L1_attn_time_decay_w1, L1_attn_time_decay_w2, L1_attn_W_r, L1_attn_W_k, L1_attn_W_v, L1_attn_W_g, L1_attn_W_o, L1_attn_ln_w, L1_attn_ln_b, L1_ffn_w_gate, L1_ffn_w_up, L1_ffn_w_down):
    import jax
    import jax.numpy as jnp

    def _L0_tok_ref(log_dt, inv_A_real, A_imag, B_ri, C_ri, L):
        import jax, jax.numpy as jnp
        import numpy as np
        import math
        H = 256
        N = 64
        CH = 1
        SEQ_L = 256
        dt = jnp.exp(log_dt)
        A = -jnp.exp(inv_A_real) + 1j * A_imag
        B = B_ri[..., 0] + 1j * B_ri[..., 1]
        C = C_ri[..., 0] + 1j * C_ri[..., 1]
        dtA = A * dt[:, None]
        dA = (1.0 + dtA / 2) / (1.0 - dtA / 2)
        C_term = C * B[None]
        log_dA = jnp.log(dA)
        V = jnp.exp(log_dA[:, :, None] * jnp.arange(L))
        K = 2.0 * jnp.einsum('chn,hnl->chl', C_term, V).real
        return K.astype(jnp.float32)

    def _L0_attn_ref(x, norm_w, norm_b, qkv_w, qkv_b, proj_w, proj_b):
        import jax, jax.numpy as jnp
        import numpy as np
        NUM_HEADS = 1
        LN_EPS = 1e-05
        B, L, D = x.shape
        H = NUM_HEADS
        mu = jnp.mean(x, axis=-1, keepdims=True)
        var = jnp.mean(jnp.square(x - mu), axis=-1, keepdims=True)
        h = (x - mu) / jnp.sqrt(var + LN_EPS) * norm_w + norm_b
        qkv = h @ qkv_w.T + qkv_b
        qkv = qkv.reshape(B * H, L // H, 3, D)
        q, k, v = (qkv[..., 0, :], qkv[..., 1, :], qkv[..., 2, :])
        scale = np.float32(1.0 / np.sqrt(L // H))
        w = jax.nn.softmax(jnp.einsum('ncq,nck->nqk', q, k * scale), axis=2)
        a = jnp.einsum('nqk,nck->ncq', w, v)
        a = a.reshape(B, L, D)
        return a @ proj_w.T + proj_b + x

    def _L0_ffn_ref(x, W_r, W_k, W_v, mu_r, mu_k):
        import jax, jax.numpy as jnp
        import numpy as np
        DIM = 256

        def _reference_tuple_inner(x, W_r, W_k, W_v, mu_r, mu_k):
            B, T, C = x.shape
            x_prev = jnp.concatenate([jnp.zeros((B, 1, C), x.dtype), x[:, :-1, :]], axis=1)
            xr = mu_r * x + (1.0 - mu_r) * x_prev
            xk = mu_k * x + (1.0 - mu_k) * x_prev
            r = jax.nn.sigmoid(jnp.einsum('btc,dc->btd', xr, W_r))
            k = jnp.einsum('btc,dc->btd', xk, W_k)
            k_act = jnp.square(jax.nn.relu(k))
            out = r * jnp.einsum('btc,dc->btd', k_act, W_v)
            new_state = x[:, -1, :]
            return (out, new_state)
        return _reference_tuple_inner(x, W_r, W_k, W_v, mu_r, mu_k)[0]

    def _L1_attn_ref(x, time_maa_x, time_maa_w, time_maa_k, time_maa_v, time_maa_r, time_maa_g, time_maa_w1, time_maa_w2, time_decay, time_decay_w1, time_decay_w2, W_r, W_k, W_v, W_g, W_o, ln_w, ln_b):
        import jax, jax.numpy as jnp
        import numpy as np
        D = 256
        H = 16
        K = 64
        B = 4
        T = 256
        LAYER_ID = 12
        NUM_LAYERS = 24
        D_MIX = 32
        D_DECAY = 64

        def _bidir_shift(x):
            left = jnp.pad(x[:, :-1, :], ((0, 0), (1, 0), (0, 0)))
            right = jnp.pad(x[:, 1:, :], ((0, 0), (0, 1), (0, 0)))
            return 0.5 * (left + right)

        def _lion_attention(r, k, v, w):
            Tn = r.shape[2]
            cs = jnp.cumsum(w, axis=2)
            cs_b = cs - w
            shift_f = cs[:, :, Tn // 2:Tn // 2 + 1, :]
            shift_b = cs_b[:, :, Tn // 2:Tn // 2 + 1, :]
            cf = jnp.clip(cs - shift_f, -60.0, 60.0)
            cb = jnp.clip(cs_b - shift_b, -60.0, 60.0)
            A_f = jnp.einsum('bhik,bhjk->bhij', r * jnp.exp(cf), k * jnp.exp(-cf))
            A_b = jnp.einsum('bhik,bhjk->bhij', r * jnp.exp(-cb), k * jnp.exp(cb))
            idx = jnp.arange(Tn)
            lower = idx[:, None] >= idx[None, :]
            A = jnp.where(lower, A_f, A_b)
            return jnp.einsum('bhij,bhjk->bhik', A, v)
        Bn, Tn, Dn = x.shape
        Hh, Kk = (H, Dn // H)
        dxprev = _bidir_shift(x) - x
        xxx = jnp.tanh((x + dxprev * time_maa_x) @ time_maa_w1)
        mm = jnp.einsum('btfm,fmd->fbtd', xxx.reshape(Bn, Tn, 5, D_MIX), time_maa_w2)
        mw, mk, mv, mr, mg = (mm[0], mm[1], mm[2], mm[3], mm[4])
        xw = x + dxprev * (time_maa_w + mw)
        xk = x + dxprev * (time_maa_k + mk)
        xv = x + dxprev * (time_maa_v + mv)
        xr = x + dxprev * (time_maa_r + mr)
        xg = x + dxprev * (time_maa_g + mg)
        r = xr @ W_r.T
        k = xk @ W_k.T
        v = xv @ W_v.T
        g = jax.nn.silu(xg @ W_g.T)
        w = time_decay + jnp.tanh(xw @ time_decay_w1) @ time_decay_w2
        to_h = lambda t: t.reshape(Bn, Tn, Hh, Kk).transpose(0, 2, 1, 3)
        y = _lion_attention(to_h(r), to_h(k), to_h(v), -jnp.exp(to_h(w)))
        y = y.transpose(0, 2, 1, 3).reshape(Bn * Tn, Dn)
        eps = 1e-05 * 64.0
        yg = y.reshape(Bn * Tn, Hh, Kk)
        mu = jnp.mean(yg, axis=-1, keepdims=True)
        var = jnp.var(yg, axis=-1, keepdims=True)
        yn = ((yg - mu) * jax.lax.rsqrt(var + eps)).reshape(Bn * Tn, Dn) * ln_w + ln_b
        y = yn.reshape(Bn, Tn, Dn)
        return y * g @ W_o.T

    def _L1_ffn_ref(x, w_gate, w_up, w_down):
        import jax, jax.numpy as jnp
        import numpy as np
        DIM = 256
        HIDDEN = 768
        SCALE = 1.0 / 127.0

        def _dequant(w_int, dtype):
            return w_int.astype(dtype) * jnp.asarray(SCALE, dtype)
        wg = _dequant(w_gate, x.dtype)
        wu = _dequant(w_up, x.dtype)
        wd = _dequant(w_down, x.dtype)
        gate = jnp.einsum('bsd,hd->bsh', x, wg)
        up = jnp.einsum('bsd,hd->bsh', x, wu)
        h = jax.nn.silu(gate) * up
        return jnp.einsum('bsh,dh->bsd', h, wd)
    h = _L0_tok_ref(L0_tok_log_dt, L0_tok_inv_A_real, L0_tok_A_imag, L0_tok_B_ri, x, 256)
    h = h + _L0_attn_ref(_layernorm(h, axis=-1), L0_attn_norm_w, L0_attn_norm_b, L0_attn_qkv_w, L0_attn_qkv_b, L0_attn_proj_w, L0_attn_proj_b)
    h = h + _L0_ffn_ref(_layernorm(h, axis=-1), L0_ffn_W_r, L0_ffn_W_k, L0_ffn_W_v, L0_ffn_mu_r, L0_ffn_mu_k)
    h = h + _L1_attn_ref(_layernorm(h, axis=-1), L1_attn_time_maa_x, L1_attn_time_maa_w, L1_attn_time_maa_k, L1_attn_time_maa_v, L1_attn_time_maa_r, L1_attn_time_maa_g, L1_attn_time_maa_w1, L1_attn_time_maa_w2, L1_attn_time_decay, L1_attn_time_decay_w1, L1_attn_time_decay_w2, L1_attn_W_r, L1_attn_W_k, L1_attn_W_v, L1_attn_W_g, L1_attn_W_o, L1_attn_ln_w, L1_attn_ln_b)
    h = h + _L1_ffn_ref(_layernorm(h, axis=-1), L1_ffn_w_gate, L1_ffn_w_up, L1_ffn_w_down)
    return h

_drawn_inputs = setup_inputs


def setup_inputs(seed=0):
    import zlib

    import numpy as np

    out = dict(_drawn_inputs(seed))
    spreads = {'L0_attn_norm_w': (1.0, 0.2),
     'L0_attn_norm_b': (0.0, 0.374),
     'L0_attn_qkv_b': (0.0, 0.39),
     'L0_attn_proj_b': (0.0, 0.272),
     'L1_attn_ln_w': (1.0, 0.6),
     'L1_attn_ln_b': (0.0, 0.8)}
    factors = {'L0_ffn_W_r': 8.0,
     'L0_ffn_mu_r': 8.0,
     'L0_ffn_mu_k': 4.383,
     'L1_attn_time_maa_x': 8.0,
     'L1_attn_time_maa_w': 64.0,
     'L1_attn_time_maa_k': 8.0,
     'L1_attn_time_maa_v': 8.0,
     'L1_attn_time_maa_r': 8.0,
     'L1_attn_time_maa_g': 8.0,
     'L1_attn_time_maa_w1': 8.0,
     'L1_attn_time_maa_w2': 8.0,
     'L1_attn_time_decay': 64.0,
     'L1_attn_time_decay_w1': 64.0,
     'L1_attn_time_decay_w2': 64.0,
     'L1_attn_W_r': 4.588,
     'L1_attn_W_k': 4.57,
     'L1_attn_W_v': 4.646,
     'L1_attn_W_g': 4.592,
     'L1_attn_W_o': 4.573}
    for name, (base, spread) in spreads.items():
        noise = np.random.default_rng([zlib.crc32(name.encode()), seed]).standard_normal(out[name].shape)
        drawn = base * np.exp(spread * noise) if base else spread * noise
        out[name] = jnp.asarray(drawn.astype(out[name].dtype))
    for name, factor in factors.items():
        out[name] = (out[name] * factor).astype(out[name].dtype)
    return out
```

```python
import concourse.bass as bass
from concourse import mybir
from contextlib import ExitStack

f32 = mybir.dt.float32
i32 = mybir.dt.int32
ALU = mybir.AluOpType
ACT = mybir.ActivationFunctionType
AX = mybir.AxisListType

B, T, D, NS = 8, 256, 256, 64
P = 128
TT = T // P
FT = D // P
HD = 16
NH = D // HD
MIX, NMIX, DEC = 32, 5, 64
HID = 768
HT = HID // P
LN_EPS = 1e-5
GN_EPS = 1e-5 * 64.0
CLIP = 60.0
QK_SCALE = 1.0 / 16.0
DEQUANT = 1.0 / 127.0

LO, HI = 32, 8
TC = 32
CHUNKS = T // TC
STREAMS = 2
ROUNDS = B // STREAMS

WEIGHTS = [("qkv", 3 * D, D), ("proj", D, D), ("ffn_r", D, D), ("ffn_k", D, D), ("ffn_v", D, D),
           ("r", D, D), ("k", D, D), ("v", D, D), ("g", D, D), ("o", D, D),
           ("gate", HID, D), ("up", HID, D), ("down", D, HID)]
W_AT = {}
_at = 0
for _n, _o, _i in WEIGHTS:
    W_AT[_n] = _at
    _at += (_o // P) * (_i // P)
W_BLOCKS = _at
W_GROUPS = W_BLOCKS // 4

NB = 8
STAGES = [("hT", 1), ("qkv", 3), ("scores", 1), ("probsT", 1), ("attT", 1), ("attn_out", 1),
          ("xT0", 1), ("ffn_kr", 2), ("ffn_v", 1),
          ("xT1", 1), ("lowrank", 1), ("mix", 5), ("low_v_g", 3), ("decay", 1), ("keys_queries", 2),
          ("keys", 1), ("state", 1), ("blocks", 16), ("y", 1), ("gatedT", 1), ("mix_out", 1),
          ("xT2", 1), ("gate_up", 6), ("down", 1)]
FIRST = {}
_n = 0
for _s, _c in STAGES:
    for _u in range(STREAMS):
        FIRST[_s, _u] = _n
        _n += _c
USES = [sum(1 for _k in range(_n) if _k % NB == b) for b in range(NB)]

PRE_VEC = 1
PRE_POLE = 1
PRE_CB = 2 * 2 * B // 4
PRE_A = PRE_VEC + PRE_POLE + PRE_CB
PRE_W = W_GROUPS
CHUNK_BANKS = 4
GEN_ROUNDS = CHUNKS // 2


def _pre_uses():
    a = [0] * NB
    for n in range(PRE_A + PRE_W):
        a[n % NB] += 1
    m = [a[b] + (GEN_ROUNDS if b < CHUNK_BANKS else 0) for b in range(NB)]
    return a, m


USED_A, USED_M = _pre_uses()


def result(stage, u, k, r):
    n = FIRST[stage, u] + k
    b = n % NB
    return b, r * USES[b] + (USED_M[b] + n // NB + 1)


def mk_vit_tower(nc, t_in, out):
    kd = nc.dram_tensor("generated_tokens", (B * HI, T, LO), f32, kind="Internal").ap()
    ctx = ExitStack()
    with ctx:
        def sb(name, shape, dt=f32):
            return ctx.enter_context(nc.sbuf_tensor(name, shape, dt))

        def sem(name):
            return ctx.enter_context(nc.semaphore(name))

        wt = sb("weightsT", [P, W_BLOCKS * P])
        ident = sb("ident", [P, P])
        w1 = sb("maa_w1", [P, FT, NMIX * MIX])
        w2a = sb("maa_w2a", [P, D])
        w2b = sb("maa_w2b", [MIX, D])
        dw1 = sb("decay_w1", [P, FT, DEC])
        dw2 = sb("decay_w2", [DEC, D])
        qk_bias = sb("qk_bias", [P, 2 * D])
        pj_bias = sb("proj_bias", [P, D])
        lnw = sb("ln_w", [P, D])
        lnb = sb("ln_b", [P, D])
        vec_rows = sb("vec_rows", [24, P])
        vec = sb("vec", [P, 24])
        blockdiag = sb("blockdiag", [P, P])
        above = sb("above", [P, 2, P])
        heads4 = sb("heads4", [P, 4])
        parity = sb("parity", [P, 2])
        ones = sb("ones", [P, T])
        neg_half = sb("neg_half", [P, 2 * NH])
        VEC = {n: i for i, n in enumerate(["norm_w", "norm_b", "v_bias", "mu_r", "mu_k", "maa_x", "maa_w",
                                           "maa_k", "maa_v", "maa_r", "maa_g", "decay"])}

        def vcol(name, ft):
            c = FT * VEC[name] + ft
            return vec[:, c:c + 1]

        def w(name, kt, c0, cn):
            width = next(o for n, o, _ in WEIGHTS if n == name)
            c = W_AT[name] * P + kt * width + c0
            return wt[:, c:c + cn]

        SLOTS = 32
        arena = [sb(f"arena{u}", [P, SLOTS * 512]) for u in range(STREAMS)]
        xT = [sb(f"xT{u}", [P, FT, T + 2]) for u in range(STREAMS)]
        k_in = [sb(f"tokens_in{u}", [P, TT, D]) for u in range(STREAMS)]
        out_sb = [sb(f"out_sb{u}", [P, TT, D]) for u in range(STREAMS)]
        stats = [sb(f"stats{u}", [P, TT, 6]) for u in range(STREAMS)]
        meanvar = [sb(f"meanvar{u}", [P, TT, 2]) for u in range(STREAMS)]
        rstd = [sb(f"rstd{u}", [P, TT]) for u in range(STREAMS)]
        smax = [sb(f"smax{u}", [P, 4]) for u in range(STREAMS)]
        ssum = [sb(f"ssum{u}", [P, 4]) for u in range(STREAMS)]
        gn = [sb(f"gn{u}", [P, 3, TT * NH]) for u in range(STREAMS)]

        def slot(u, s, n=1):
            return arena[u][:, s * 512:(s + n) * 512]

        def two(u, s):
            return slot(u, s).rearrange("p (a b) -> p a b", a=2)

        H, XN, N0, BASE = 0, 1, 2, 3
        HTs, QK, VT, EX, PT, AT_ = 5, 6, 8, 9, 10, 11
        DIFF, XR, XK, RELU, KSQ, TANH, GATED = 5, 6, 7, 8, 9, 10, 11
        DX, XM, TMP, XF, XXX, ZT = 5, 6, (7, 4), 8, 13, 14
        EW, CS, CSB, CF, CB, EFN, EBN = 15, 16, 17, 18, 19, 20, 21
        RF, RB, KF, KB, RFM, RBM, VV, G2 = 22, 23, 24, 25, 26, 28, 30, 31
        THG, KTM, SBD, AB = 3, 13, 14, 5
        YC, SQ, ZN, ZG, ZTs = 15, 16, 17, 18, 19
        THF, SF, HM = 5, 8, 11

        banks = [ctx.enter_context(nc.psum_tensor(f"bank{b}", [P, 512], f32)) for b in range(NB)]

        def bank2(b):
            return banks[b][:, :].rearrange("p (a b) -> p a b", a=2)

        full = [sem(f"bank{b}_full") for b in range(NB)]
        emptied = [sem(f"bank{b}_emptied") for b in range(NB)]
        inputs_in = sem("inputs_in")
        c_in = sem("c_in")
        vec_in = sem("vec_in")
        small_in = sem("small_in")
        weights_in = [sem(f"weights_in_{n}") for n, _, _ in WEIGHTS]
        ident_made = sem("ident_made")
        consts_made = sem("consts_made")
        parity_made = sem("parity_made")
        dequantized = sem("dequantized")
        act_dt = sem("act_dt")
        poles_made = sem("poles_made")
        cb_made = sem("cb_made")
        powers_made = sem("powers_made")
        q_start = sem("q_start")
        hi_made = sem("high_powers_made")
        cross_made = sem("cross_made")
        p_made = sem("p_made")
        k_copied = sem("k_copied")
        k_stored = [sem(f"k_stored{i}") for i in range(2)]
        k_loaded = [sem(f"k_loaded{u}") for u in range(STREAMS)]
        out_free = [sem(f"out_free{u}") for u in range(STREAMS)]
        dve_chain = sem("dve_chain")
        pool_chain = sem("pool_chain")
        act_chain = sem("act_chain")
        main_dve_chain = sem("main_dve_chain")
        main_pool_chain = sem("main_pool_chain")

        NAMES = {}

        def product(name, per_batch=1):
            NAMES[name] = (sem(name), per_batch)
            return NAMES[name][0]

        def at(name, g, k=None):
            s, n = NAMES[name]
            return s, g * n + (n if k is None else k)

        var_ready = [sem(f"var_ready{u}") for u in range(STREAMS)]
        rstd_ready = [sem(f"rstd_ready{u}") for u in range(STREAMS)]
        normed = [sem(f"normed{u}") for u in range(STREAMS)]

        for name, n in [("base_ready", 1), ("max_ready", 1),
                        ("diff_ready", 1), ("xr_ready", 1), ("xk_ready", 1), ("ksq_ready", 1),
                        ("xm_ready", 1), ("mixed", NMIX), ("tanh_low", 1), ("tanh_r", 1),
                        ("tanh_g", 1), ("cs_ready", 1), ("csb_ready", 1), ("cf_ready", 1), ("cb_ready", 1),
                        ("ef_ready", 1), ("eb_ready", 1), ("rf_ready", 1), ("kf_ready", 1),
                        ("rfm_ready", 1), ("rbm_ready", 1), ("low_copied", 16), ("centred", 1), ("squared", 1),
                        ("gvar_ready", 1), ("grstd_ready", 1), ("yn_ready", 1), ("affine_ready", 1),
                        ("gated_ready", 1), ("tanh_gate", 3), ("out_ready", 1)]:
            product(name, n)

        waits_apart = {e: sem(f"waits_apart_{e}") for e in ("pool", "dve")}

        def apart(eng, name):
            eng.sem_inc(waits_apart[name], 1)

        block = ctx.enter_context(nc.Block())

        flat = {0: 0, 1: 0}

        def carve(a, n):
            c = flat[a]
            flat[a] += n
            assert flat[a] <= SLOTS * 512
            return arena[a][:, c:c + n]

        nat = {}
        for name, o, i in WEIGHTS:
            nat[name] = carve(0, (o // P) * i)
        pole = carve(1, 2 * TT * 2 * NS).rearrange("p (c t d n) -> p c t d n", c=2, t=TT, d=2)
        b_nat = carve(1, TT * NS * 2).rearrange("p (t n c) -> p t n c", t=TT, c=2)
        c_nat = carve(1, B * TT * NS * 2).rearrange("p (b t n c) -> p b t n c", b=B, t=TT, c=2)
        cb_nat = carve(1, 2 * B * TT * 2 * NS).rearrange("p (c b t d n) -> p c b t d n", c=2, b=B, t=TT, d=2)
        cbT = carve(1, 2 * B * T).rearrange("p (c b t) -> p c b t", c=2, b=B)
        zp = carve(1, 8 * 2 * T).rearrange("p (k c t) -> p k c t", k=8, c=2)
        pbuf = cb_nat.rearrange("p c b t d n -> p (c b t d n)")
        pb = [pbuf[:, i * 2048:(i + 1) * 2048].rearrange("p (t b a) -> p t b a", t=TC, b=B) for i in range(2)]
        cross = c_nat.rearrange("p b t n c -> p (b t n c)").rearrange("p (t b a) -> p t b a", t=TC, b=B)
        q1 = [carve(0, TC * LO).rearrange("p (t l) -> p t l", t=TC) for _ in range(2)]
        q2 = carve(1, TC * LO).rearrange("p (t l) -> p t l", t=TC)
        tmp1 = carve(0, TC * LO // 2)
        tmp2 = carve(0, TC * LO // 2)
        e1 = [sb(f"high_re{i}", [P, TC * HI])[:, :].rearrange("p (t a) -> p t a", t=TC) for i in range(2)]
        e2 = [carve(a, TC * HI).rearrange("p (t a) -> p t a", t=TC) for a in range(2)]
        etmp = [carve(0, TC * HI // 2) for _ in range(2)]
        ks = [carve(0, TC * LO) for _ in range(2)]
        work = [k_in[i // 4][:, :, :].rearrange("p t d -> p (t d)")[:, (i % 4) * P:(i % 4 + 1) * P] for i in range(8)]
        inv_nat, aim_nat = work[6], work[7]
        logdt = sb("log_dt", [P, TT])
        halfdt = sb("half_dt", [P, TT])
        sqt = [wt[:, i * 256:(i + 1) * 256] for i in range(4)]

        @block.sync
        def _(sp):
            with nc.allow_non_contiguous_dma(reason="per-token scalars"):
                sp.dma_start(logdt[:, :], t_in["L0_tok_log_dt"].rearrange("(t p) -> p t", p=P)).then_inc(inputs_in, 16)
            sp.dma_start(inv_nat.rearrange("p (t n) -> p t n", t=TT),
                         t_in["L0_tok_inv_A_real"].rearrange("(t p) n -> p t n", p=P)).then_inc(inputs_in, 16)
            sp.dma_start(aim_nat.rearrange("p (t n) -> p t n", t=TT),
                         t_in["L0_tok_A_imag"].rearrange("(t p) n -> p t n", p=P)).then_inc(inputs_in, 16)
            sp.dma_start(b_nat, t_in["L0_tok_B_ri"].rearrange("(t p) n c -> p t n c", p=P)).then_inc(inputs_in, 16)
            for tt in range(TT):
                sp.dma_start(c_nat[:, :, tt].rearrange("p b n c -> p b (n c)"),
                             t_in["x"][:, tt * P:(tt + 1) * P].rearrange("b p n c -> p b (n c)")).then_inc(c_in, 16)
            src = {"qkv": "L0_attn_qkv_w", "proj": "L0_attn_proj_w", "ffn_r": "L0_ffn_W_r", "ffn_k": "L0_ffn_W_k",
                   "ffn_v": "L0_ffn_W_v", "r": "L1_attn_W_r", "k": "L1_attn_W_k", "v": "L1_attn_W_v",
                   "g": "L1_attn_W_g", "o": "L1_attn_W_o", "gate": "L1_ffn_w_gate", "up": "L1_ffn_w_up",
                   "down": "L1_ffn_w_down"}
            for (name, o, i), s in zip(WEIGHTS, weights_in):
                dst = nat[name].bitcast(i32) if name in ("gate", "up", "down") else nat[name]
                sp.dma_start(dst.rearrange("p (o i) -> p o i", i=i),
                             t_in[src[name]].rearrange("(o p) i -> p o i", p=P)).then_inc(s, 16)

            with sp.Fori(0, GEN_ROUNDS) as r:
                for c in range(2):
                    sp.wait_ge(k_copied, (r * 2 + c) * 2 + 2)
                    sp.dma_start(kd[:, bass.ds((r * 2 + c) * TC, TC), :],
                                 ks[c][0:B * HI, :].rearrange("p (t l) -> p t l", t=TC)).then_inc(k_stored[c], 16)
            for c in range(2):
                sp.wait_ge(k_stored[c], 16 * (GEN_ROUNDS + 1))

            def load(g, u):
                for tt in range(TT):
                    sp.dma_start(k_in[u][:, tt, :].rearrange("p (a l) -> p a l", a=HI),
                                 kd[bass.ds(g * HI, HI), tt * P:(tt + 1) * P, :].rearrange("a p l -> p a l"))\
                      .then_inc(k_loaded[u], 16)

            def store(g, u):
                sp.wait_ge(*at("out_ready", g))
                sp.dma_start(out[bass.ds(g, 1), :, :].rearrange("o (t p) f -> p (o t) f", p=P), out_sb[u][:, :, :])\
                  .then_inc(out_free[u], 16)

            for u in range(STREAMS):
                load(u, u)
            with sp.Fori(0, ROUNDS - 1) as r:
                for u in range(STREAMS):
                    sp.wait_ge(*at("base_ready", r * 2 + u))
                    load(r * 2 + (STREAMS + u), u)
                for u in range(STREAMS):
                    store(r * 2 + u, u)
            for u in range(STREAMS):
                store((ROUNDS - 1) * STREAMS + u, u)
            for u in range(STREAMS):
                sp.wait_ge(out_free[u], 16 * (ROUNDS + 1))

        @block.gpsimd
        def _(pool):
            pl = nc.gpsimd
            chain = [0]

            def link(ins):
                chain[0] += 1
                ins.then_inc(pool_chain, 1)
                pool.wait_ge(pool_chain, chain[0])

            link(pl.memset(ident[:, :], 0.0))
            pl.affine_select(out=ident[:, :], in_=ident[:, :], compare_op=ALU.not_equal, fill=1.0, base=0,
                             pattern=[[-1, P]], channel_multiplier=1).then_inc(ident_made, 1)
            link(pl.memset(blockdiag[:, :], 1.0))
            bdv = blockdiag[:, :]
            link(pl.affine_select(out=bdv, in_=bdv, compare_op=ALU.is_ge, fill=0.0, base=0,
                                  pattern=[[-HD, P // HD], [0, HD]], channel_multiplier=1))
            link(pl.affine_select(out=bdv, in_=bdv, compare_op=ALU.is_ge, fill=0.0, base=HD - 1,
                                  pattern=[[HD, P // HD], [0, HD]], channel_multiplier=-1))
            link(pl.memset(above[:, :, :], 1.0))
            link(pl.affine_select(out=above[:, :, :], in_=above[:, :, :], compare_op=ALU.is_gt, fill=0.0, base=0,
                                  pattern=[[0, 2], [-1, P]], channel_multiplier=1))
            link(pl.memset(heads4[:, :], 1.0))
            link(pl.affine_select(out=heads4[:, :], in_=heads4[:, :], compare_op=ALU.is_ge, fill=0.0, base=0,
                                  pattern=[[-2 * HD, 4]], channel_multiplier=1))
            link(pl.affine_select(out=heads4[:, :], in_=heads4[:, :], compare_op=ALU.is_ge, fill=0.0, base=HD - 1,
                                  pattern=[[2 * HD, 4]], channel_multiplier=-1))
            link(pl.memset(ones[:, :], 1.0))
            for u in range(STREAMS):
                link(pl.memset(xT[u][:, :, :], 0.0))
            pl.memset(neg_half[:, :], -0.5).then_inc(consts_made, 1)
            for q in (q1[0], q1[1], q2):
                link(pl.memset(q[:, :, 0:1], 0.0))
            for q in (e1[0], e1[1], e2[0], e2[1]):
                link(pl.memset(q[:, :, 0:1], 0.0))
            for q in q1:
                link(pl.memset(q[0:NS, :, 0:1], 2.0))
            link(pl.memset(q2[NS:P, :, 0:1], 2.0))
            for q in e1:
                link(pl.memset(q[0:NS, :, 0:1], 1.0))
            for q in e2:
                link(pl.memset(q[NS:P, :, 0:1], 1.0))
            pl.memset(ks[0], 0.0).then_inc(k_stored[0], 16)
            pl.memset(ks[1], 0.0).then_inc(k_stored[1], 16)
            for u in range(STREAMS):
                pl.memset(out_sb[u][:, :, :], 0.0).then_inc(out_free[u], 16)
            link(pl.memset(etmp[0], 0.0))
            pl.memset(etmp[1], 0.0).then_inc(q_start, 1)
            pool.wait_ge(q_start, 1)

            pool.wait_ge(powers_made, 1)
            for c in range(2 * B * TT // 4):
                n = PRE_VEC + PRE_POLE + c
                pool.wait_ge(emptied[n % NB], n // NB + 1)
            gen_base = chain[0]
            GEN_LINKS = 2 * (4 + 4 + 3)
            with pool.Fori(0, GEN_ROUNDS) as r:
                local = [0]

                def glink(ins):
                    local[0] += 1
                    ins.then_inc(pool_chain, 1)
                    pool.wait_ge(pool_chain, r * GEN_LINKS + (gen_base + local[0]))
                    apart(pool, "pool")

                for c in range(2):
                    t0 = (r * 2 + c) * TC
                    pool.wait_ge(p_made, (r * 2 + c) + 1)
                    apart(pool, "pool")
                    for lv, m in enumerate((1, 2, 4)):
                        zr = zp[:, 5 + lv, 0, bass.ds(t0, TC)].unsqueeze(2).to_broadcast([P, TC, m])
                        zi = zp[:, 5 + lv, 1, bass.ds(t0, TC)].unsqueeze(2).to_broadcast([P, TC, m])
                        ta = etmp[0][:, 0:TC * m].rearrange("p (t a) -> p t a", t=TC)
                        tb = etmp[1][:, 0:TC * m].rearrange("p (t a) -> p t a", t=TC)
                        pl.tensor_tensor(ta, e1[c][:, :, 0:m], zr, ALU.mult)
                        glink(pl.tensor_tensor(tb, e2[c][:, :, 0:m], zi, ALU.mult))
                        glink(pl.tensor_tensor(e1[c][:, :, m:2 * m], ta, tb, ALU.add))
                        pl.tensor_tensor(ta, e2[c][:, :, 0:m], zr, ALU.mult)
                        glink(pl.tensor_tensor(tb, e1[c][:, :, 0:m], zi, ALU.mult))
                        last = pl.tensor_tensor(e2[c][:, :, m:2 * m], ta, tb, ALU.subtract)
                        if lv < 2:
                            glink(last)
                        else:
                            last.then_inc(hi_made, 1)
                            pool.wait_ge(hi_made, (r * 2 + c) + 1)
                    pool.wait_ge(p_made, (r * 2 + c) + 2)
                    apart(pool, "pool")
                    pl.tensor_tensor(cross, cbT[:, 1, :, bass.ds(t0, TC)].rearrange("p b t -> p t b").unsqueeze(3)
                                     .to_broadcast([P, TC, B, HI]),
                                     e2[c].unsqueeze(2).to_broadcast([P, TC, B, HI]), ALU.mult).then_inc(cross_made, 1)
                assert local[0] == GEN_LINKS, local[0]
            pool.wait_ge(weights_in[0], 16)

            def rstd_of(u, r, n):
                pool.wait_ge(var_ready[u], r * 5 + (n + 1))
                apart(pool, "pool")
                mlink(pl.tensor_scalar(rstd[u][:, :], meanvar[u][:, :, 1], LN_EPS, 1.0, ALU.add, ALU.mult))
                pl.tensor_tensor(rstd[u][:, :], rstd[u][:, :], neg_half[:, 0:TT], ALU.pow)\
                  .then_inc(rstd_ready[u], 1)

            MAIN_LINKS = STREAMS * (5 + 1 + 1 + 1)
            for n in range(PRE_A + PRE_W):
                pool.wait_ge(emptied[n % NB], n // NB + 1)
            with pool.Fori(0, ROUNDS) as r:
                mlocal = [0]

                def mlink(ins):
                    mlocal[0] += 1
                    ins.then_inc(main_pool_chain, 1)
                    pool.wait_ge(main_pool_chain, r * MAIN_LINKS + mlocal[0])

                for u in range(STREAMS):
                    g = r * 2 + u
                    rstd_of(u, r, 0)
                    rstd_of(u, r, 1)
                    pool.wait_ge(normed[u], r * 5 + 1)
                    mlink(pl.tensor_tensor(two(u, BASE), k_in[u][:, :, :], two(u, XN), ALU.add))
                    pl.tensor_tensor(two(u, BASE), two(u, BASE), pj_bias[:, :].unsqueeze(1).to_broadcast([P, TT, D]),
                                     ALU.add).then_inc(at("base_ready", g)[0], 1)
                for u in range(STREAMS):
                    rstd_of(u, r, 2)
                for u in range(STREAMS):
                    g = r * 2 + u
                    b, v = result("xT0", u, 0, r)
                    pool.wait_ge(emptied[b], v)
                    pl.tensor_tensor(two(u, DIFF), xT[u][:, :, 1:T + 1], xT[u][:, :, 0:T], ALU.subtract)\
                      .then_inc(at("diff_ready", g)[0], 1)
                for u in range(STREAMS):
                    g = r * 2 + u
                    b, v = result("ffn_kr", u, 0, r)
                    pool.wait_ge(emptied[b], v)
                    pl.tensor_tensor(two(u, KSQ), two(u, RELU), two(u, RELU), ALU.mult)\
                      .then_inc(at("ksq_ready", g)[0], 1)
                for u in range(STREAMS):
                    rstd_of(u, r, 3)
                for u in range(STREAMS):
                    g = r * 2 + u
                    for f in range(NMIX):
                        b, v = result("mix", u, f, r)
                        pool.wait_ge(emptied[b], v)
                        pl.tensor_tensor(two(u, XF + f), two(u, TMP[f % 2]), xT[u][:, :, 1:T + 1], ALU.add)\
                          .then_inc(at("mixed", g)[0], 1)
                for u in range(STREAMS):
                    g = r * 2 + u
                    pool.wait_ge(*at("cs_ready", g))
                    pl.tensor_tensor(two(u, CSB), two(u, CS), two(u, EW), ALU.add)\
                      .then_inc(at("csb_ready", g)[0], 1)
                    b, v = result("keys_queries", u, 1, r)
                    pool.wait_ge(emptied[b], v)
                    apart(pool, "pool")
                    for e in range(2):
                        last = pl.tensor_scalar(
                            slot(u, RBM, 2).rearrange("p (d j e i) -> p d j e i", d=FT, j=TT, e=2)[:, :, :, e, :],
                            slot(u, RB).rearrange("p (d j i) -> p d j i", d=FT, j=TT),
                            parity[:, e:e + 1], 1.0, ALU.mult, ALU.mult)
                    last.then_inc(at("rbm_ready", g)[0], 1)
                for u in range(STREAMS):
                    g = r * 2 + u
                    pool.wait_ge(*at("gvar_ready", g))
                    apart(pool, "pool")
                    mlink(pl.tensor_scalar(gn[u][:, 2, :], gn[u][:, 1, :], 1.0 / HD, GN_EPS, ALU.mult, ALU.add))
                    pl.tensor_tensor(gn[u][:, 2, :], gn[u][:, 2, :], neg_half[:, :], ALU.pow)\
                      .then_inc(at("grstd_ready", g)[0], 1)
                    pool.wait_ge(*at("yn_ready", g))
                    mlink(pl.tensor_tensor(two(u, ZN), two(u, ZN), lnw[:, :].unsqueeze(1).to_broadcast([P, TT, D]),
                                           ALU.mult))
                    pl.tensor_tensor(two(u, ZN), two(u, ZN), lnb[:, :].unsqueeze(1).to_broadcast([P, TT, D]),
                                     ALU.add).then_inc(at("affine_ready", g)[0], 1)
                for u in range(STREAMS):
                    rstd_of(u, r, 4)
                assert mlocal[0] == MAIN_LINKS, mlocal[0]

        @block.scalar
        def _(act):
            ac = nc.scalar
            rows = ["L0_attn_norm_w", "L0_attn_norm_b", None, "L0_ffn_mu_r", "L0_ffn_mu_k", "L1_attn_time_maa_x",
                    "L1_attn_time_maa_w", "L1_attn_time_maa_k", "L1_attn_time_maa_v", "L1_attn_time_maa_r",
                    "L1_attn_time_maa_g", "L1_attn_time_decay"]
            for i, name in enumerate(rows):
                if name is None:
                    src = t_in["L0_attn_qkv_b"][2 * D:3 * D]
                elif name.startswith("L1"):
                    src = t_in[name][0, 0, :]
                else:
                    src = t_in[name]
                act.dma_start(vec_rows[FT * i:FT * (i + 1), :], src.rearrange("(t p) -> t p", p=P)).then_inc(vec_in, 16)
            act.dma_start(w1[:, :, :], t_in["L1_attn_time_maa_w1"].rearrange("(t p) m -> p t m", p=P)).then_inc(small_in, 16)
            w2 = t_in["L1_attn_time_maa_w2"].rearrange("f m d -> (f m) d")
            act.dma_start(w2a[:, :], w2[0:P, :]).then_inc(small_in, 16)
            act.dma_start(w2b[:, :], w2[P:P + MIX, :]).then_inc(small_in, 16)
            act.dma_start(dw1[:, :, :], t_in["L1_attn_time_decay_w1"].rearrange("(t p) m -> p t m", p=P)).then_inc(small_in, 16)
            act.dma_start(dw2[:, :], t_in["L1_attn_time_decay_w2"]).then_inc(small_in, 16)
            for dst, src in ((qk_bias, t_in["L0_attn_qkv_b"][0:2 * D]), (pj_bias, t_in["L0_attn_proj_b"]),
                             (lnw, t_in["L1_attn_ln_w"]), (lnb, t_in["L1_attn_ln_b"])):
                act.dma_start(dst[:, :], src.partition_broadcast(P)).then_inc(small_in, 16)

            act.wait_ge(inputs_in, 64)
            ac.activation(halfdt[:, :], logdt[:, :], ACT.Exp).then_inc(act_dt, 1)
            ac.activation(work[0], inv_nat, ACT.Exp).then_inc(act_dt, 1)

            def copy_out(dst, b, v, src=None):
                act.wait_ge(full[b], v)
                ac.activation(dst, banks[b][:, :] if src is None else src, ACT.Copy).then_inc(emptied[b], 1)

            act.wait_ge(full[0], 1)
            ac.activation(vec[:, :], banks[0][:, 0:24], ACT.Copy).then_inc(emptied[0], 1)
            n = PRE_VEC
            copy_out(zp[:, 0].rearrange("p c t -> p (c t)"), n % NB, n // NB + 1)
            for k in range(PRE_CB):
                n = PRE_VEC + PRE_POLE + k
                copy_out(cbT.rearrange("p c b t -> p (c b t)")[:, k * 512:(k + 1) * 512], n % NB, n // NB + 1)
            act.wait_ge(powers_made, 1)
            for k in range(W_GROUPS):
                n = PRE_A + k
                copy_out(wt[:, k * 512:(k + 1) * 512], n % NB, n // NB + 1)
            with act.Fori(0, GEN_ROUNDS) as r:
                for c in range(2):
                    act.wait_ge(k_stored[c], r * 16 + 16)
                    for h in range(2):
                        b = 2 * c + h
                        act.wait_ge(full[b], r + (USED_A[b] + 1))
                        ac.activation(ks[c][0:B * HI, h * 512:(h + 1) * 512], banks[b][0:B * HI, :], ACT.Copy)\
                          .then_inc(emptied[b], 1)
                    act.wait_ge(emptied[2 * c + 1], r + (USED_A[2 * c + 1] + 1))
                    ac.activation(ssum[0][:, 2:3], ones[:, 0:1], ACT.Copy).then_inc(k_copied, 2)

            with act.Fori(0, ROUNDS) as r:
                def transposed(stage, u):
                    b, v = result(stage, u, 0, r)
                    act.wait_ge(full[b], v)
                    ac.activation(xT[u][:, :, 1:T + 1], bank2(b), ACT.Copy).then_inc(emptied[b], 1)

                for u in range(STREAMS):
                    b, v = result("hT", u, 0, r)
                    act.wait_ge(full[b], v)
                    for ft in range(FT):
                        last = ac.activation(two(u, HTs)[:, ft, :], bank2(b)[:, ft, :], ACT.Identity,
                                             bias=vcol("norm_b", ft), scale=vcol("norm_w", ft))
                    last.then_inc(emptied[b], 1)
                for u in range(STREAMS):
                    b, v = result("qkv", u, 2, r)
                    act.wait_ge(full[b], v)
                    for ft in range(FT):
                        last = ac.activation(two(u, VT)[:, ft, :], bank2(b)[:, ft, :], ACT.Identity,
                                             bias=vcol("v_bias", ft))
                    last.then_inc(emptied[b], 1)
                for u in range(STREAMS):
                    g = r * 2 + u
                    b, v = result("scores", u, 0, r)
                    act.wait_ge(*at("max_ready", g))
                    for qt in range(FT):
                        last = ac.activation(two(u, EX)[:, qt, :], bank2(b)[:, qt, :], ACT.Exp,
                                             bias=smax[u][:, 2 + qt:3 + qt], scale=QK_SCALE,
                                             accum_out=ssum[u][:, qt:qt + 1])
                    last.then_inc(emptied[b], 1)
                for u in range(STREAMS):
                    b, v = result("probsT", u, 0, r)
                    copy_out(slot(u, PT), b, v)
                for u in range(STREAMS):
                    transposed("xT0", u)
                for u in range(STREAMS):
                    g = r * 2 + u
                    b, v = result("ffn_kr", u, 0, r)
                    act.wait_ge(full[b], v)
                    ac.activation(slot(u, RELU), banks[b][:, :], ACT.Relu).then_inc(emptied[b], 1)
                    b, v = result("ffn_kr", u, 1, r)
                    act.wait_ge(full[b], v)
                    ac.activation(slot(u, TANH), banks[b][:, :], ACT.Tanh, scale=0.5).then_inc(emptied[b], 1)
                for u in range(STREAMS):
                    transposed("xT1", u)
                for u in range(STREAMS):
                    b, v = result("lowrank", u, 0, r)
                    act.wait_ge(full[b], v)
                    ac.activation(slot(u, XXX)[:, 0:T], banks[b][:, 0:T], ACT.Tanh)
                    ac.activation(slot(u, XXX)[0:MIX, T:2 * T], banks[b][0:MIX, T:2 * T], ACT.Tanh)\
                      .then_inc(emptied[b], 1)
                for u in range(STREAMS):
                    g = r * 2 + u
                    b, v = result("low_v_g", u, 0, r)
                    act.wait_ge(full[b], v)
                    ac.activation(slot(u, ZT)[0:DEC, 0:T], banks[b][0:DEC, 0:T], ACT.Tanh).then_inc(emptied[b], 1)
                    b, v = result("low_v_g", u, 1, r)
                    copy_out(slot(u, VV), b, v)
                    b, v = result("low_v_g", u, 2, r)
                    act.wait_ge(full[b], v)
                    ac.activation(slot(u, THG), banks[b][:, :], ACT.Tanh, scale=0.5).then_inc(at("tanh_g", g)[0], 1)
                for u in range(STREAMS):
                    b, v = result("decay", u, 0, r)
                    act.wait_ge(full[b], v)
                    for ft in range(FT):
                        last = ac.activation(two(u, EW)[:, ft, :], bank2(b)[:, ft, :], ACT.Exp,
                                             bias=vcol("decay", ft))
                    last.then_inc(emptied[b], 1)
                for u in range(STREAMS):
                    g = r * 2 + u
                    act.wait_ge(*at("cf_ready", g))
                    ac.activation(slot(u, EFN), slot(u, CF), ACT.Exp, scale=-1.0)
                    ac.activation(slot(u, CF), slot(u, CF), ACT.Exp).then_inc(at("ef_ready", g)[0], 1)
                    act.wait_ge(*at("cb_ready", g))
                    ac.activation(slot(u, EBN), slot(u, CB), ACT.Exp, scale=-1.0)
                    ac.activation(slot(u, CB), slot(u, CB), ACT.Exp).then_inc(at("eb_ready", g)[0], 1)
                    act.wait_ge(*at("rf_ready", g))
                    for e in range(2):
                        last = ac.activation(
                            slot(u, RFM, 2).rearrange("p (d j e i) -> p d j e i", d=FT, j=TT, e=2)[:, :, :, e, :],
                            slot(u, RF).rearrange("p (d j i) -> p d j i", d=FT, j=TT), ACT.Copy,
                            scale=parity[:, e:e + 1])
                    last.then_inc(at("rfm_ready", g)[0], 1)
                for u in range(STREAMS):
                    g = r * 2 + u
                    for k in range(16):
                        b, v = result("blocks", u, k, r)
                        act.wait_ge(full[b], v)
                        ac.activation(slot(u, AB, 8)[:, k * 256:(k + 1) * 256], banks[b][:, 0:256], ACT.Copy)\
                          .then_inc(at("low_copied", g)[0], 1)
                for u in range(STREAMS):
                    g = r * 2 + u
                    b, v = result("y", u, 0, r)
                    act.wait_ge(emptied[b], v)
                    ac.activation(slot(u, SQ), slot(u, YC), ACT.Square).then_inc(at("squared", g)[0], 1)
                for u in range(STREAMS):
                    b, v = result("gatedT", u, 0, r)
                    copy_out(slot(u, ZTs), b, v)
                for u in range(STREAMS):
                    transposed("xT2", u)
                for u in range(STREAMS):
                    g = r * 2 + u
                    for c in range(3):
                        b, v = result("gate_up", u, 2 * c, r)
                        act.wait_ge(full[b], v)
                        ac.activation(slot(u, THF + c), banks[b][:, :], ACT.Tanh, scale=0.5)\
                          .then_inc(at("tanh_gate", g)[0], 1)

        @block.vector
        def _(dve):
            vc = nc.vector
            chain = [0]

            def link(ins):
                chain[0] += 1
                ins.then_inc(dve_chain, 1)
                dve.wait_ge(dve_chain, chain[0])

            dve.wait_ge(act_dt, 2)
            link(vc.tensor_scalar(halfdt[:, :], halfdt[:, :], 0.5, None, ALU.mult))
            hx, hy, sqx, sqy, den, num = work[0], work[1], work[2], work[3], work[4], work[5]
            for tt in range(TT):
                s = slice(tt * NS, (tt + 1) * NS)
                link(vc.tensor_scalar(hx[:, s], hx[:, s], halfdt[:, tt:tt + 1], -1.0, ALU.mult, ALU.mult))
                link(vc.tensor_scalar(hy[:, s], aim_nat[:, s], halfdt[:, tt:tt + 1], None, ALU.mult))
            link(vc.tensor_tensor(sqx, hx, hx, ALU.mult))
            link(vc.tensor_tensor(sqy, hy, hy, ALU.mult))
            link(vc.tensor_scalar(den, hx, -1.0, 1.0, ALU.mult, ALU.add))
            link(vc.tensor_tensor(den, den, den, ALU.mult))
            link(vc.tensor_tensor(den, den, sqy, ALU.add))
            link(vc.reciprocal(den, den))
            link(vc.tensor_tensor(num, sqx, sqy, ALU.add))
            link(vc.tensor_scalar(num, num, -1.0, 1.0, ALU.mult, ALU.add))

            def dup(x):
                return x.rearrange("p (t n) -> p t n", t=TT).unsqueeze(2).to_broadcast([P, TT, 2, NS])
            link(vc.tensor_tensor(pole[:, 0], dup(num), dup(den), ALU.mult))
            link(vc.tensor_scalar(hy, hy, 2.0, None, ALU.mult))
            vc.tensor_tensor(pole[:, 1], dup(hy), dup(den), ALU.mult).then_inc(poles_made, 1)

            dve.wait_ge(c_in, 32)
            BH = B // 2
            v_ = [x.rearrange("p (b t n) -> p b t n", b=BH, t=TT) for x in (tmp1, tmp2)]
            br = b_nat[:, :, :, 0].unsqueeze(1).to_broadcast([P, BH, TT, NS])
            bi = b_nat[:, :, :, 1].unsqueeze(1).to_broadcast([P, BH, TT, NS])
            for part, (x, y, op) in enumerate(((br, bi, ALU.subtract), (bi, br, ALU.add))):
                for b0 in range(0, B, BH):
                    link(vc.tensor_tensor(v_[0], c_nat[:, b0:b0 + BH, :, :, 0], x, ALU.mult))
                    link(vc.tensor_tensor(v_[1], c_nat[:, b0:b0 + BH, :, :, 1], y, ALU.mult))
                    for d in range(2):
                        last = vc.tensor_tensor(cb_nat[:, part, b0:b0 + BH, :, d, :], v_[0], v_[1], op)
                        if b0 == 0 or d == 0:
                            link(last)
                        else:
                            last.then_inc(cb_made, 1)
                            dve.wait_ge(cb_made, part + 1)

            n = PRE_VEC
            dve.wait_ge(emptied[n % NB], n // NB + 1)
            for k in range(7):
                zr, zi = zp[:, k, 0, :], zp[:, k, 1, :]
                link(vc.tensor_tensor(sqt[0], zr, zi, ALU.subtract))
                link(vc.tensor_tensor(sqt[1], zr, zi, ALU.add))
                link(vc.tensor_tensor(zp[:, k + 1, 0, :], sqt[0], sqt[1], ALU.mult))
                last = vc.scalar_tensor_tensor(out=zp[:, k + 1, 1, :], in0=zr, scalar=2.0, in1=zi, op0=ALU.mult,
                                               op1=ALU.mult)
                if k < 6:
                    link(last)
                else:
                    last.then_inc(powers_made, 1)
                    dve.wait_ge(powers_made, 1)
            dve.wait_ge(consts_made, 1)
            link(vc.reduce_sum(parity[:, 0:1], heads4[:, :], AX.X))
            vc.tensor_scalar(parity[:, 1:2], parity[:, 0:1], -1.0, 1.0, ALU.mult, ALU.add).then_inc(parity_made, 1)
            for k, name in enumerate(("gate", "up", "down")):
                dve.wait_ge(weights_in[10 + k], 16)
                vc.tensor_scalar(nat[name], nat[name].bitcast(i32), DEQUANT, None, ALU.mult).then_inc(dequantized, 1)

            dve.wait_ge(q_start, 1)
            for k in range(PRE_CB):
                n = PRE_VEC + PRE_POLE + k
                dve.wait_ge(emptied[n % NB], n // NB + 1)
            vc.memset(tmp1, 0.0).then_inc(p_made, 1)
            vc.memset(tmp2, 0.0).then_inc(p_made, 1)
            dve.wait_ge(p_made, 2)
            gen_base = chain[0]
            GEN_LINKS = 2 * (4 * 4 + 2 + 1)
            with dve.Fori(0, GEN_ROUNDS) as r:
                local = [0]

                def glink(ins):
                    local[0] += 1
                    ins.then_inc(dve_chain, 1)
                    dve.wait_ge(dve_chain, r * GEN_LINKS + (gen_base + local[0]))

                for c in range(2):
                    t0 = (r * 2 + c) * TC
                    for b in (2 * c, 2 * c + 1):
                        dve.wait_ge(full[b], r + USED_A[b])
                    for lv in range(5):
                        m = 1 << lv
                        zr = zp[:, lv, 0, bass.ds(t0, TC)].unsqueeze(2).to_broadcast([P, TC, m])
                        zi = zp[:, lv, 1, bass.ds(t0, TC)].unsqueeze(2).to_broadcast([P, TC, m])
                        ta = tmp1[:, 0:TC * m].rearrange("p (t a) -> p t a", t=TC)
                        tb = tmp2[:, 0:TC * m].rearrange("p (t a) -> p t a", t=TC)
                        vc.tensor_tensor(ta, q1[c][:, :, 0:m], zr, ALU.mult)
                        glink(vc.tensor_tensor(tb, q2[:, :, 0:m], zi, ALU.mult))
                        glink(vc.tensor_tensor(q1[c][:, :, m:2 * m], ta, tb, ALU.subtract))
                        if lv < 4:
                            vc.tensor_tensor(ta, q2[:, :, 0:m], zr, ALU.mult)
                            glink(vc.tensor_tensor(tb, q1[c][:, :, 0:m], zi, ALU.mult))
                            glink(vc.tensor_tensor(q2[:, :, m:2 * m], ta, tb, ALU.add))
                    dve.wait_ge(hi_made, (r * 2 + c) + 1)
                    glink(vc.tensor_tensor(pb[c], cbT[:, 0, :, bass.ds(t0, TC)].rearrange("p b t -> p t b").unsqueeze(3)
                                           .to_broadcast([P, TC, B, HI]),
                                           e1[c].unsqueeze(2).to_broadcast([P, TC, B, HI]), ALU.mult))
                    dve.wait_ge(cross_made, (r * 2 + c) + 1)
                    vc.tensor_tensor(pb[c], pb[c], cross, ALU.add).then_inc(p_made, 1)
                assert local[0] == GEN_LINKS, local[0]

            for n in range(PRE_A + PRE_W):
                dve.wait_ge(emptied[n % NB], n // NB + 1)
            for b in range(NB):
                dve.wait_ge(emptied[b], USED_M[b])
            dve.wait_ge(small_in, 16 * 9)
            with dve.Fori(0, ROUNDS) as r:
                mlocal = [0]

                def mlink(ins):
                    mlocal[0] += 1
                    ins.then_inc(main_dve_chain, 1)
                    dve.wait_ge(main_dve_chain, r * MAIN_DVE_LINKS + mlocal[0])

                def layer_norm(u, n, src, dst):
                    for tt in range(TT):
                        mlink(vc.bn_stats(stats[u][:, tt, :], src[:, tt, :]))
                        apart(dve, "dve")
                        last = vc.bn_aggr(meanvar[u][:, tt, :], stats[u][:, tt, :])
                    last.then_inc(var_ready[u], 1)
                    dve.wait_ge(rstd_ready[u], r * 5 + (n + 1))
                    for tt in range(TT):
                        last = vc.tensor_scalar(dst[:, tt, :], src[:, tt, :], meanvar[u][:, tt, 0:1],
                                                rstd[u][:, tt:tt + 1], ALU.subtract, ALU.mult)
                    last.then_inc(normed[u], 1)

                for u in range(STREAMS):
                    g = r * 2 + u
                    dve.wait_ge(k_loaded[u], r * 32 + 32)
                    layer_norm(u, 0, k_in[u][:, :, :], two(u, XN))
                    dve.wait_ge(normed[u], r * 5 + 1)
                    layer_norm(u, 1, two(u, XN), two(u, N0))
                for u in range(STREAMS):
                    for tt in range(TT):
                        b, v = result("qkv", u, tt, r)
                        dve.wait_ge(full[b], v)
                        vc.tensor_tensor(slot(u, QK + tt), banks[b][:, :], qk_bias[:, :], ALU.add)\
                          .then_inc(emptied[b], 1)
                for u in range(STREAMS):
                    g = r * 2 + u
                    b, v = result("scores", u, 0, r)
                    dve.wait_ge(full[b], v)
                    mlink(vc.reduce_max(smax[u][:, 0:2], bank2(b), AX.X))
                    vc.tensor_scalar(smax[u][:, 2:4], smax[u][:, 0:2], -QK_SCALE, None, ALU.mult)\
                      .then_inc(at("max_ready", g)[0], 1)
                for u in range(STREAMS):
                    b, v = result("scores", u, 0, r)
                    dve.wait_ge(emptied[b], v)
                    mlink(vc.reciprocal(ssum[u][:, 2:4], ssum[u][:, 0:2]))
                    b, v = result("attT", u, 0, r)
                    dve.wait_ge(full[b], v)
                    for qt in range(FT):
                        last = vc.tensor_scalar(two(u, AT_)[:, qt, :], bank2(b)[:, qt, :], ssum[u][:, 2 + qt:3 + qt],
                                                None, ALU.mult)
                    last.then_inc(emptied[b], 1)
                for u in range(STREAMS):
                    g = r * 2 + u
                    b, v = result("attn_out", u, 0, r)
                    dve.wait_ge(full[b], v)
                    dve.wait_ge(*at("base_ready", g))
                    vc.tensor_tensor(slot(u, H), banks[b][:, :], slot(u, BASE), ALU.add).then_inc(emptied[b], 1)
                    dve.wait_ge(emptied[b], v)
                    layer_norm(u, 2, two(u, H), two(u, XN))
                for u in range(STREAMS):
                    g = r * 2 + u
                    dve.wait_ge(*at("diff_ready", g))
                    for name, dst, done in (("mu_k", XK, "xk_ready"), ("mu_r", XR, "xr_ready")):
                        for ft in range(FT):
                            last = vc.scalar_tensor_tensor(out=two(u, dst)[:, ft, :], in0=two(u, DIFF)[:, ft, :],
                                                           scalar=vcol(name, ft), in1=xT[u][:, ft, 0:T],
                                                           op0=ALU.mult, op1=ALU.add)
                        last.then_inc(at(done, g)[0], 1)
                for u in range(STREAMS):
                    g = r * 2 + u
                    bt, vt = result("ffn_kr", u, 1, r)
                    dve.wait_ge(emptied[bt], vt)
                    b, v = result("ffn_v", u, 0, r)
                    dve.wait_ge(full[b], v)
                    vc.scalar_tensor_tensor(out=slot(u, GATED), in0=slot(u, TANH), scalar=1.0, in1=banks[b][:, :],
                                            op0=ALU.add, op1=ALU.mult).then_inc(emptied[b], 1)
                    dve.wait_ge(emptied[b], v)
                    mlink(vc.scalar_tensor_tensor(out=slot(u, H), in0=slot(u, GATED), scalar=0.5, in1=slot(u, H),
                                                  op0=ALU.mult, op1=ALU.add))
                    layer_norm(u, 3, two(u, H), two(u, XN))
                for u in range(STREAMS):
                    g = r * 2 + u
                    b, v = result("xT1", u, 0, r)
                    dve.wait_ge(emptied[b], v)
                    mlink(vc.tensor_tensor(two(u, TMP[0]), xT[u][:, :, 0:T], xT[u][:, :, 2:T + 2], ALU.add))
                    mlink(vc.scalar_tensor_tensor(out=two(u, DX), in0=two(u, TMP[0]), scalar=0.5,
                                                  in1=xT[u][:, :, 1:T + 1], op0=ALU.mult, op1=ALU.subtract))
                    for ft in range(FT):
                        last = vc.scalar_tensor_tensor(out=two(u, XM)[:, ft, :], in0=two(u, DX)[:, ft, :],
                                                       scalar=vcol("maa_x", ft), in1=xT[u][:, ft, 1:T + 1],
                                                       op0=ALU.mult, op1=ALU.add)
                    last.then_inc(at("xm_ready", g)[0], 1)
                for u in range(STREAMS):
                    g = r * 2 + u
                    for f, name in enumerate(("maa_w", "maa_k", "maa_v", "maa_r", "maa_g")):
                        b, v = result("mix", u, f, r)
                        dve.wait_ge(full[b], v)
                        if f >= 2:
                            dve.wait_ge(*at("mixed", g, f - 1))
                        for ft in range(FT):
                            last = vc.scalar_tensor_tensor(out=two(u, TMP[f % 2])[:, ft, :], in0=bank2(b)[:, ft, :],
                                                           scalar=vcol(name, ft), in1=two(u, DX)[:, ft, :],
                                                           op0=ALU.add, op1=ALU.mult)
                        last.then_inc(emptied[b], 1)
                for u in range(STREAMS):
                    g = r * 2 + u
                    b, v = result("low_v_g", u, 2, r)
                    dve.wait_ge(*at("tanh_g", g))
                    vc.scalar_tensor_tensor(out=slot(u, G2), in0=slot(u, THG), scalar=1.0, in1=banks[b][:, :],
                                            op0=ALU.add, op1=ALU.mult).then_inc(emptied[b], 1)
                for u in range(STREAMS):
                    g = r * 2 + u
                    b, v = result("decay", u, 0, r)
                    dve.wait_ge(emptied[b], v)
                    for ft in range(FT):
                        last = vc.tensor_tensor_scan(two(u, CS)[:, ft, :], ones[:, :], two(u, EW)[:, ft, :], 0.0,
                                                     ALU.mult, ALU.subtract)
                    last.then_inc(at("cs_ready", g)[0], 1)
                    dve.wait_ge(*at("cs_ready", g))
                    for src, dst, first, done in ((CS, CF, None, "cf_ready"), (CSB, CB, "csb_ready", "cb_ready")):
                        if first:
                            dve.wait_ge(*at(first, g))
                        for ft in range(FT):
                            last = vc.tensor_scalar(two(u, dst)[:, ft, :], two(u, src)[:, ft, :],
                                                    two(u, src)[:, ft, T // 2:T // 2 + 1], CLIP, ALU.subtract, ALU.min)
                        mlink(last)
                        vc.tensor_scalar(slot(u, dst), slot(u, dst), -CLIP, None, ALU.max).then_inc(at(done, g)[0], 1)
                    br_, vr = result("keys_queries", u, 1, r)
                    bk, vk = result("keys_queries", u, 0, r)
                    dve.wait_ge(full[br_], vr)
                    dve.wait_ge(full[bk], vk)
                    dve.wait_ge(*at("ef_ready", g))
                    vc.tensor_tensor(slot(u, RF), banks[br_][:, :], slot(u, CF), ALU.mult).then_inc(at("rf_ready", g)[0], 1)
                    vc.tensor_tensor(slot(u, KF), banks[bk][:, :], slot(u, EFN), ALU.mult).then_inc(at("kf_ready", g)[0], 1)
                    dve.wait_ge(*at("eb_ready", g))
                    vc.tensor_tensor(slot(u, RB), banks[br_][:, :], slot(u, EBN), ALU.mult).then_inc(emptied[br_], 1)
                    vc.tensor_tensor(slot(u, KB), banks[bk][:, :], slot(u, CB), ALU.mult).then_inc(emptied[bk], 1)
                for u in range(STREAMS):
                    g = r * 2 + u
                    b, v = result("keys", u, 0, r)
                    dve.wait_ge(full[b], v)
                    vc.tensor_copy(slot(u, KTM), banks[b][:, :]).then_inc(emptied[b], 1)
                for u in range(STREAMS):
                    b, v = result("state", u, 0, r)
                    dve.wait_ge(full[b], v)
                    vc.tensor_tensor(slot(u, SBD).rearrange("p (c d) -> p c d", c=4),
                                     banks[b][:, :].rearrange("p (c d) -> p c d", c=4),
                                     blockdiag[:, :].unsqueeze(1).to_broadcast([P, 4, P]), ALU.mult)\
                      .then_inc(emptied[b], 1)
                for u in range(STREAMS):
                    g = r * 2 + u
                    for k in range(16):
                        b, v = result("blocks", u, k, r)
                        dve.wait_ge(*at("low_copied", g, k + 1))
                        apart(dve, "dve")
                        vc.copy_predicated(slot(u, AB, 8)[:, k * 256:(k + 1) * 256],
                                           above[:, :, :].rearrange("p e i -> p (e i)").bitcast(i32),
                                           banks[b][:, 256:512]).then_inc(emptied[b], 1)
                for u in range(STREAMS):
                    g = r * 2 + u
                    b, v = result("y", u, 0, r)

                    def heads(x):
                        return x.rearrange("p (h d) -> p h d", d=HD)

                    def spread(k):
                        return gn[u][:, k, :].unsqueeze(2).to_broadcast([P, TT * NH, HD])
                    dve.wait_ge(full[b], v)
                    mlink(vc.reduce_sum(gn[u][:, 0, :], heads(banks[b][:, :]), AX.X))
                    mlink(vc.tensor_scalar(gn[u][:, 0, :], gn[u][:, 0, :], 1.0 / HD, None, ALU.mult))
                    vc.tensor_tensor(heads(slot(u, YC)), heads(banks[b][:, :]), spread(0), ALU.subtract)\
                      .then_inc(emptied[b], 1)
                    dve.wait_ge(*at("squared", g))
                    vc.reduce_sum(gn[u][:, 1, :], heads(slot(u, SQ)), AX.X).then_inc(at("gvar_ready", g)[0], 1)
                    dve.wait_ge(*at("grstd_ready", g))
                    vc.tensor_tensor(heads(slot(u, ZN)), heads(slot(u, YC)), spread(2), ALU.mult)\
                      .then_inc(at("yn_ready", g)[0], 1)
                    dve.wait_ge(*at("affine_ready", g))
                    vc.scalar_tensor_tensor(out=slot(u, ZG), in0=slot(u, ZN), scalar=0.5, in1=slot(u, G2),
                                            op0=ALU.mult, op1=ALU.mult).then_inc(at("gated_ready", g)[0], 1)
                for u in range(STREAMS):
                    g = r * 2 + u
                    b, v = result("mix_out", u, 0, r)
                    dve.wait_ge(full[b], v)
                    vc.tensor_tensor(slot(u, H), banks[b][:, :], slot(u, H), ALU.add).then_inc(emptied[b], 1)
                    dve.wait_ge(emptied[b], v)
                    layer_norm(u, 4, two(u, H), two(u, XN))
                for u in range(STREAMS):
                    g = r * 2 + u
                    for c in range(3):
                        bg, vg = result("gate_up", u, 2 * c, r)
                        bu, vu = result("gate_up", u, 2 * c + 1, r)
                        dve.wait_ge(*at("tanh_gate", g, c + 1))
                        vc.scalar_tensor_tensor(out=slot(u, SF + c), in0=slot(u, THF + c), scalar=1.0,
                                                in1=banks[bg][:, :], op0=ALU.add, op1=ALU.mult).then_inc(emptied[bg], 1)
                        dve.wait_ge(full[bu], vu)
                        dve.wait_ge(emptied[bg], vg)
                        vc.scalar_tensor_tensor(out=slot(u, HM + c), in0=slot(u, SF + c), scalar=0.5,
                                                in1=banks[bu][:, :], op0=ALU.mult, op1=ALU.mult).then_inc(emptied[bu], 1)
                for u in range(STREAMS):
                    g = r * 2 + u
                    b, v = result("down", u, 0, r)
                    dve.wait_ge(full[b], v)
                    dve.wait_ge(out_free[u], r * 16 + 16)
                    vc.tensor_tensor(out_sb[u][:, :, :], bank2(b), two(u, H), ALU.add).then_inc(emptied[b], 1)
                    dve.wait_ge(emptied[b], v)
                    vc.tensor_copy(smax[u][:, 0:1], ones[:, 0:1]).then_inc(at("out_ready", g)[0], 1)
                assert mlocal[0] == MAIN_DVE_LINKS, mlocal[0]

        @block.tensor
        def _(pe):
            mm = nc.tensor.matmul

            def block_t(b, c, src, cols=P):
                return nc.tensor.transpose(banks[b][0:cols, c * P:c * P + src.shape[0]], src,
                                           ident[0:src.shape[0], 0:src.shape[0]])

            pe.wait_ge(ident_made, 1)
            pe.wait_ge(vec_in, 16 * 12)
            block_t(0, 0, vec_rows[:, :]).then_inc(full[0], 1)
            n = PRE_VEC
            pe.wait_ge(poles_made, 1)
            for part in range(2):
                for tt in range(TT):
                    last = block_t(n % NB, part * TT + tt, pole[:, part, tt].rearrange("p d n -> p (d n)"))
            last.then_inc(full[n % NB], 1)
            blk = 0
            for part in range(2):
                pe.wait_ge(cb_made, part + 1)
                for b in range(B):
                    for tt in range(TT):
                        n = PRE_VEC + PRE_POLE + blk // 4
                        if blk % 4 == 0 and n >= NB:
                            pe.wait_ge(emptied[n % NB], n // NB)
                        last = block_t(n % NB, blk % 4, cb_nat[:, part, b, tt].rearrange("p d n -> p (d n)"))
                        if blk % 4 == 3:
                            last.then_inc(full[n % NB], 1)
                        blk += 1
            blk = 0
            for k, (name, o, i) in enumerate(WEIGHTS):
                pe.wait_ge(weights_in[k], 16)
                if name in ("gate", "up", "down"):
                    pe.wait_ge(dequantized, k - 9)
                src = nat[name].rearrange("p (o i) -> p o i", i=i)
                for kt in range(i // P):
                    for ot in range(o // P):
                        n = PRE_A + blk // 4
                        if blk % 4 == 0:
                            pe.wait_ge(emptied[n % NB], n // NB)
                        last = block_t(n % NB, blk % 4, src[:, ot, kt * P:(kt + 1) * P])
                        if blk % 4 == 3:
                            last.then_inc(full[n % NB], 1)
                        blk += 1
            with pe.Fori(0, GEN_ROUNDS) as r:
                for c in range(2):
                    pe.wait_ge(p_made, (r * 2 + c) + 3)
                    for h in range(2):
                        b = 2 * c + h
                        pe.wait_ge(emptied[b], r + USED_A[b])
                        for t in range(TC // 2):
                            tl = h * (TC // 2) + t
                            last = mm(banks[b][0:B * HI, t * LO:(t + 1) * LO],
                                      pb[c][:, tl].rearrange("p b a -> p (b a)"), q1[c][:, tl, :],
                                      start=True, stop=True)
                        last.then_inc(full[b], 1)
            pe.wait_ge(small_in, 16 * 9)

            with pe.Fori(0, ROUNDS) as r:
                def free_bank(stage, u, k):
                    b, v = result(stage, u, k, r)
                    pe.wait_ge(emptied[b], v - 1)
                    return b

                def wait_emptied(stage, u, k=0):
                    b, v = result(stage, u, k, r)
                    pe.wait_ge(emptied[b], v)

                def transposes(stage, u, src):
                    b = free_bank(stage, u, 0)
                    for tt in range(TT):
                        for ft in range(FT):
                            last = nc.tensor.transpose(bank2(b)[:, ft, tt * P:(tt + 1) * P],
                                                       src[:, tt, ft * P:(ft + 1) * P], ident[:, :])
                    last.then_inc(full[b], 1)

                def feature_major(b, name, x, c0=0, tiles=FT):
                    for ft in range(tiles):
                        for kt in range(FT):
                            last = mm(bank2(b)[:, ft, :], w(name, kt, c0 + ft * P, P), x[:, kt, :],
                                      start=(kt == 0), stop=(kt == FT - 1))
                    last.then_inc(full[b], 1)

                def token_major(b, name, x, kts=FT):
                    for tt in range(TT):
                        for kt in range(kts):
                            last = mm(bank2(b)[:, tt, :], x(kt, tt), w(name, kt, 0, D),
                                      start=(kt == 0), stop=(kt == kts - 1))
                    last.then_inc(full[b], 1)

                def tok(u, s):
                    return lambda kt, tt: two(u, s)[:, kt, tt * P:(tt + 1) * P]

                for u in range(STREAMS):
                    pe.wait_ge(normed[u], r * 5 + 2)
                    transposes("hT", u, two(u, N0))
                for u in range(STREAMS):
                    wait_emptied("hT", u)
                    for tt in range(TT):
                        b = free_bank("qkv", u, tt)
                        for kt in range(FT):
                            last = mm(banks[b][:, :], two(u, HTs)[:, kt, tt * P:(tt + 1) * P],
                                      w("qkv", kt, 0, 2 * D), start=(kt == 0), stop=(kt == FT - 1))
                        last.then_inc(full[b], 1)
                    b = free_bank("qkv", u, 2)
                    feature_major(b, "qkv", two(u, HTs), c0=2 * D)
                for u in range(STREAMS):
                    wait_emptied("qkv", u, 0)
                    wait_emptied("qkv", u, 1)
                    b = free_bank("scores", u, 0)
                    for qt in range(FT):
                        for tt in range(TT):
                            last = mm(bank2(b)[:, qt, :], slot(u, QK + tt)[:, qt * P:(qt + 1) * P],
                                      slot(u, QK + tt)[:, D:2 * D], start=(tt == 0), stop=(tt == TT - 1))
                    last.then_inc(full[b], 1)
                for u in range(STREAMS):
                    wait_emptied("scores", u)
                    transposes("probsT", u, two(u, EX))
                for u in range(STREAMS):
                    wait_emptied("probsT", u)
                    wait_emptied("qkv", u, 2)
                    b = free_bank("attT", u, 0)
                    for qt in range(FT):
                        for kt in range(FT):
                            last = mm(bank2(b)[:, qt, :], two(u, PT)[:, kt, qt * P:(qt + 1) * P],
                                      two(u, VT)[:, kt, :], start=(kt == 0), stop=(kt == FT - 1))
                    last.then_inc(full[b], 1)
                for u in range(STREAMS):
                    wait_emptied("attT", u)
                    token_major(free_bank("attn_out", u, 0), "proj", tok(u, AT_))
                for u in range(STREAMS):
                    pe.wait_ge(normed[u], r * 5 + 3)
                    transposes("xT0", u, two(u, XN))
                for u in range(STREAMS):
                    g = r * 2 + u
                    pe.wait_ge(*at("xk_ready", g))
                    feature_major(free_bank("ffn_kr", u, 0), "ffn_k", two(u, XK))
                    pe.wait_ge(*at("xr_ready", g))
                    token_major(free_bank("ffn_kr", u, 1), "ffn_r", tok(u, XR))
                for u in range(STREAMS):
                    pe.wait_ge(*at("ksq_ready", r * 2 + u))
                    token_major(free_bank("ffn_v", u, 0), "ffn_v", tok(u, KSQ))
                for u in range(STREAMS):
                    pe.wait_ge(normed[u], r * 5 + 4)
                    transposes("xT1", u, two(u, XN))
                for u in range(STREAMS):
                    pe.wait_ge(*at("xm_ready", r * 2 + u))
                    b = free_bank("lowrank", u, 0)
                    for c0, cn in ((0, P), (P, MIX)):
                        for kt in range(FT):
                            last = mm(bank2(b)[0:cn, c0 // P, :], w1[:, kt, c0:c0 + cn], two(u, XM)[:, kt, :],
                                      start=(kt == 0), stop=(kt == FT - 1))
                    last.then_inc(full[b], 1)
                for u in range(STREAMS):
                    wait_emptied("lowrank", u)
                    for f in range(NMIX):
                        b = free_bank("mix", u, f)
                        q = f % 4
                        for ft in range(FT):
                            lhs = (w2a if f < 4 else w2b)[MIX * q:MIX * (q + 1), ft * P:(ft + 1) * P]
                            rhs = slot(u, XXX)[MIX * q:MIX * (q + 1), (f // 4) * T:(f // 4 + 1) * T]
                            last = mm(bank2(b)[:, ft, :], lhs, rhs, start=True, stop=True)
                        last.then_inc(full[b], 1)
                for u in range(STREAMS):
                    g = r * 2 + u
                    pe.wait_ge(*at("mixed", g, 1))
                    b = free_bank("low_v_g", u, 0)
                    for kt in range(FT):
                        last = mm(banks[b][0:DEC, 0:T], dw1[:, kt, :], two(u, XF)[:, kt, :],
                                  start=(kt == 0), stop=(kt == FT - 1))
                    last.then_inc(full[b], 1)
                    pe.wait_ge(*at("mixed", g, 3))
                    token_major(free_bank("low_v_g", u, 1), "v", tok(u, XF + 2))
                    pe.wait_ge(*at("mixed", g, 5))
                    token_major(free_bank("low_v_g", u, 2), "g", tok(u, XF + 4))
                for u in range(STREAMS):
                    wait_emptied("low_v_g", u, 0)
                    b = free_bank("decay", u, 0)
                    for ft in range(FT):
                        last = mm(bank2(b)[:, ft, :], dw2[:, ft * P:(ft + 1) * P], slot(u, ZT)[0:DEC, 0:T],
                                  start=True, stop=True)
                    last.then_inc(full[b], 1)
                for u in range(STREAMS):
                    feature_major(free_bank("keys_queries", u, 0), "k", two(u, XF + 1))
                    feature_major(free_bank("keys_queries", u, 1), "r", two(u, XF + 3))
                for u in range(STREAMS):
                    g = r * 2 + u
                    pe.wait_ge(*at("kf_ready", g))
                    wait_emptied("keys_queries", u, 0)
                    b = free_bank("keys", u, 0)
                    for x, s in enumerate((KF, KB)):
                        for ft in range(FT):
                            last = nc.tensor.transpose(bank2(b)[:, x, ft * P:(ft + 1) * P],
                                                       two(u, s)[:, ft, x * P:(x + 1) * P], ident[:, :])
                    last.then_inc(full[b], 1)
                for u in range(STREAMS):
                    wait_emptied("keys", u)
                    wait_emptied("low_v_g", u, 1)
                    b = free_bank("state", u, 0)
                    for x in range(2):
                        for ft in range(FT):
                            c = (x * FT + ft) * P
                            last = mm(banks[b][:, c:c + P], two(u, KTM)[:, x, ft * P:(ft + 1) * P],
                                      two(u, VV)[:, x, ft * P:(ft + 1) * P], start=True, stop=True)
                    last.then_inc(full[b], 1)
                for u in range(STREAMS):
                    g = r * 2 + u
                    pe.wait_ge(*at("rfm_ready", g))
                    pe.wait_ge(*at("rbm_ready", g))
                    for k0 in range(0, 16, 4):
                        ft, jb = k0 // 8, (k0 // 4) % 2
                        bs = [free_bank("blocks", u, k0 + q) for q in range(4)]
                        for x, (ks_, rs_) in enumerate(((KF, RFM), (KB, RBM))):
                            for q in range(4):
                                rows = slice(32 * q, 32 * q + 32)
                                last = mm(banks[bs[q]][:, x * 256:(x + 1) * 256],
                                          two(u, ks_)[rows, ft, jb * P:(jb + 1) * P],
                                          slot(u, rs_, 2)[rows, (ft * 2 + jb) * 256:(ft * 2 + jb + 1) * 256],
                                          start=True, stop=True)
                                if x == 1:
                                    last.then_inc(full[bs[q]], 1)
                for u in range(STREAMS):
                    wait_emptied("state", u)
                    b = free_bank("y", u, 0)
                    for x, (s, tt) in enumerate(((RF, 1), (RB, 0))):
                        for ft in range(FT):
                            c = (x * FT + ft) * P
                            mm(bank2(b)[:, tt, ft * P:(ft + 1) * P], two(u, s)[:, ft, tt * P:(tt + 1) * P],
                               slot(u, SBD)[:, c:c + P], start=(x == 0 and ft == 0), stop=False, skip_group_check=True)
                    for k in range(16):
                        ft, jb, q = k // 8, (k // 4) % 2, k % 4
                        wait_emptied("blocks", u, k)
                        for e in range(2):
                            h = ft * 8 + q * 2 + e
                            last = mm(bank2(b)[:, jb, h * HD:(h + 1) * HD],
                                      slot(u, AB, 8)[:, k * 256 + e * P:k * 256 + (e + 1) * P],
                                      two(u, VV)[:, jb, h * HD:(h + 1) * HD], start=False,
                                      stop=(k == 15 and e == 1), skip_group_check=True)
                    last.then_inc(full[b], 1)
                for u in range(STREAMS):
                    pe.wait_ge(*at("gated_ready", r * 2 + u))
                    transposes("gatedT", u, two(u, ZG))
                for u in range(STREAMS):
                    wait_emptied("gatedT", u)
                    token_major(free_bank("mix_out", u, 0), "o", tok(u, ZTs))
                for u in range(STREAMS):
                    pe.wait_ge(normed[u], r * 5 + 5)
                    transposes("xT2", u, two(u, XN))
                for u in range(STREAMS):
                    wait_emptied("xT2", u)
                    x = xT[u][:, :, 1:T + 1]
                    for c in range(3):
                        feature_major(free_bank("gate_up", u, 2 * c), "gate", x, c0=2 * c * P)
                        feature_major(free_bank("gate_up", u, 2 * c + 1), "up", x, c0=2 * c * P)
                for u in range(STREAMS):
                    for c in range(3):
                        wait_emptied("gate_up", u, 2 * c + 1)
                    token_major(free_bank("down", u, 0), "down",
                                lambda kt, tt: two(u, HM + kt // 2)[:, kt % 2, tt * P:(tt + 1) * P], kts=HT)


MAIN_DVE_LINKS = STREAMS * (5 * 2 + 1 + 1 + 1 + 2 + 2 + 2)

_INS = ['x', 'L0_tok_log_dt', 'L0_tok_inv_A_real', 'L0_tok_A_imag', 'L0_tok_B_ri', 'L0_attn_norm_w', 'L0_attn_norm_b',
        'L0_attn_qkv_w', 'L0_attn_qkv_b', 'L0_attn_proj_w', 'L0_attn_proj_b', 'L0_ffn_W_r', 'L0_ffn_W_k', 'L0_ffn_W_v',
        'L0_ffn_mu_r', 'L0_ffn_mu_k', 'L1_attn_time_maa_x', 'L1_attn_time_maa_w', 'L1_attn_time_maa_k',
        'L1_attn_time_maa_v', 'L1_attn_time_maa_r', 'L1_attn_time_maa_g', 'L1_attn_time_maa_w1', 'L1_attn_time_maa_w2',
        'L1_attn_time_decay', 'L1_attn_time_decay_w1', 'L1_attn_time_decay_w2', 'L1_attn_W_r', 'L1_attn_W_k',
        'L1_attn_W_v', 'L1_attn_W_g', 'L1_attn_W_o', 'L1_attn_ln_w', 'L1_attn_ln_b', 'L1_ffn_w_gate', 'L1_ffn_w_up',
        'L1_ffn_w_down']


def kernel(**inputs):
    import numpy as _np
    import concourse.bacc as _bacc
    from concourse import mybir as _mybir
    from concourse.bass_utils import run_bass_kernel_spmd as _run

    nc = _bacc.Bacc("TRN2", target_bir_lowering=False, num_devices=1)
    arrays, t_in = {}, {}
    for name in _INS:
        a = _np.ascontiguousarray(inputs[name])
        arrays[f"in_{name}"] = a
        t_in[name] = nc.dram_tensor(f"in_{name}", a.shape, _mybir.dt.from_np(a.dtype), kind="ExternalInput").ap()
    out = nc.dram_tensor("out_0", (B, T, D), f32, kind="ExternalOutput").ap()
    mk_vit_tower(nc, t_in, out)
    r = _run(nc, [arrays], core_ids=[0])
    return r.results[0]["out_0"]
```

```python
import concourse.bass as bass
from concourse import mybir
from contextlib import ExitStack

f32 = mybir.dt.float32
i32 = mybir.dt.int32
ALU = mybir.AluOpType
ACT = mybir.ActivationFunctionType
AX = mybir.AxisListType

B, T, D, NS = 8, 256, 256, 64
P = 128
TT = T // P
FT = D // P
HD = 16
NH = D // HD
MIX, NMIX, DEC = 32, 5, 64
HID = 768
HT = HID // P
LN_EPS = 1e-5
GN_EPS = 1e-5 * 64.0
CLIP = 60.0
QK_SCALE = 1.0 / 16.0
DEQUANT = 1.0 / 127.0

LO, HI = 32, 8
TC = 32
CHUNKS = T // TC
STREAMS = 2

WEIGHTS = [("qkv", 3 * D, D), ("proj", D, D), ("ffn_r", D, D), ("ffn_k", D, D), ("ffn_v", D, D),
           ("r", D, D), ("k", D, D), ("v", D, D), ("g", D, D), ("o", D, D),
           ("gate", HID, D), ("up", HID, D), ("down", D, HID)]
W_AT = {}
_at = 0
for _n, _o, _i in WEIGHTS:
    W_AT[_n] = _at
    _at += (_o // P) * (_i // P)
W_BLOCKS = _at
W_GROUPS = W_BLOCKS // 4

LAYER0 = ["norms", "hT", "qkv", "scores", "probsT", "attT", "attn_out", "xT0", "ffn_kr", "ffn_v"]
HALF = [("mix", "xT1"), ("ff", "y3"), ("mix", "lowrank"), ("ff", "yT"), ("mix", "mix"), ("ff", "head_norm"),
        ("mix", "low"), ("mix", "key"), ("mix", "value"), ("mix", "decay"), ("mix", "query"), ("mix", "gate"),
        ("next", "norms"), ("mix", "factors"), ("ff", "gatedT"), ("ff", "mix_out"), ("mix", "keys"), ("next", "hT"),
        ("mix", "state"), ("next", "qkv"), ("mix", "blocks0"), ("ff", "xT2"), ("next", "scores"),
        ("ff", "gate_up0"), ("next", "probsT"), ("mix", "blocks1"), ("next", "attT"), ("ff", "gate_up1"),
        ("next", "attn_out"), ("ff", "gate_up2"), ("mix", "blocks2"), ("next", "xT0"), ("mix", "blocks3"),
        ("next", "ffn_kr"), ("mix", "y0"), ("mix", "y1"), ("next", "ffn_v"), ("mix", "y2"), ("ff", "down")]
FEED_FORWARD = [step for part, step in HALF if part == "ff"]
RESULTS = {"norms": 0, "head_norm": 0, "hT": 1, "qkv": 3, "scores": 1, "probsT": 1, "attT": 1, "attn_out": 1, "xT0": 1, "ffn_kr": 2, "ffn_v": 1,
           "xT1": 1, "lowrank": 1, "mix": 5, "low": 1, "key": 1, "value": 1, "gate": 1, "decay": 1, "query": 1, "factors": 0, "keys": 1, "state": 1,
           "blocks0": 4, "blocks1": 4, "blocks2": 4, "blocks3": 4, "y0": 0, "y1": 0, "y2": 0, "y3": 0,
           "yT": 0, "gatedT": 1, "mix_out": 1,
           "xT2": 1, "gate_up0": 2, "gate_up1": 2, "gate_up2": 2, "down": 1}


def half(n):
    u = n % 2
    out = []
    for part, step in HALF:
        if part == "mix":
            out.append((step, u, 0))
        elif part == "ff" and n > 0:
            out.append((step, 1 - u, -1))
        elif part == "next" and n < B - 1:
            out.append((step, 1 - u, 1))
    return out


SEGMENTS = {"first": [(s, 0, 0) for s in LAYER0] + half(0),
            "loop": half(1) + half(2),
            "last": half(B - 1) + [(s, 1, 0) for s in FEED_FORWARD]}
ROUNDS = (B - 2) // 2

NB = 8
RING = 7
Y_BANK = 7
FIRST, USES = {}, {}
for _seg, _steps in SEGMENTS.items():
    _n = 0
    for _s, _u, _ in _steps:
        assert (_seg, _s, _u) not in FIRST
        FIRST[_seg, _s, _u] = _n
        _n += RESULTS[_s]
    USES[_seg] = [sum(1 for _k in range(_n) if _k % RING == b) for b in range(NB)]

PRE_VEC = 1
PRE_POLE = 1
PRE_CB = 2 * 2 * B // 4
PRE_A = PRE_VEC + PRE_POLE + PRE_CB
PRE_W = W_GROUPS
CHUNK_BANKS = 4
GEN_ROUNDS = CHUNKS // 2

USED_A = [sum(1 for _k in range(PRE_A + PRE_W) if _k % NB == b) for b in range(NB)]
USED_M = [USED_A[b] + (GEN_ROUNDS if b < CHUNK_BANKS else 0) for b in range(NB)]
BEFORE = {"first": USED_M,
          "loop": [USED_M[b] + USES["first"][b] for b in range(NB)],
          "last": [USED_M[b] + USES["first"][b] + ROUNDS * USES["loop"][b] for b in range(NB)]}


class At:

    def __init__(self, seg, r, u, offset, n):
        self.seg, self.r, self.u = seg, r, u
        self.g = n + offset
        self.j = None

    def result(self, step, k=0):
        n = FIRST[self.seg, step, self.u] + k
        b = n % RING
        done = BEFORE[self.seg][b] + n // RING + 1
        return b, (self.r * USES["loop"][b] + done if self.seg == "loop" else done)


    def y_result(self, k):
        return Y_BANK, self.g * 2 + (USED_M[Y_BANK] + k + 1)


def places(seg, r):
    for i, (step, u, offset) in enumerate(SEGMENTS[seg]):
        if seg == "first":
            n = 0
        elif seg == "loop":
            n = r * 2 + (1 if i < len(half(1)) else 2)
        else:
            n = B - 1
        at_ = At(seg, r, u, offset, n)
        if seg == "loop":
            n0 = 1 if i < len(half(1)) else 2
            at_.g = r * 2 + (n0 + offset)
            at_.j = r + (n0 + offset) // 2
        else:
            at_.j = at_.g // 2
        yield step, at_


def mk_vit_tower(nc, t_in, out):
    kd = nc.dram_tensor("generated_tokens", (B * HI, T, LO), f32, kind="Internal").ap()
    ctx = ExitStack()
    with ctx:
        def sb(name, shape, dt=f32):
            return ctx.enter_context(nc.sbuf_tensor(name, shape, dt))

        def sem(name):
            return ctx.enter_context(nc.semaphore(name))

        wt = sb("weightsT", [P, W_BLOCKS * P])
        ident = sb("ident", [P, P])
        w1 = sb("maa_w1", [P, FT, NMIX * MIX])
        w2a = sb("maa_w2a", [P, D])
        w2b = sb("maa_w2b", [MIX, D])
        dw1 = sb("decay_w1", [P, FT, DEC])
        dw2 = sb("decay_w2", [DEC, D])
        qk_bias = sb("qk_bias", [P, 2 * D])
        pj_bias = sb("proj_bias", [P, D])
        lnw = sb("ln_w", [P, D])
        lnb = sb("ln_b", [P, D])
        vec_rows = sb("vec_rows", [24, P])
        vec = sb("vec", [P, 24])
        blockdiag = sb("blockdiag", [P, P])
        above = sb("above", [P, 2, P])
        heads4 = sb("heads4", [P, 4])
        parity = sb("parity", [P, 2])
        ones = sb("ones", [P, T])
        neg_half = sb("neg_half", [P, 2 * NH])
        head_sel = sb("head_sel", [P, 2, 2, HD])
        VEC = {n: i for i, n in enumerate(["norm_w", "norm_b", "v_bias", "mu_r", "mu_k", "maa_x", "maa_w",
                                           "maa_k", "maa_v", "maa_r", "maa_g", "decay"])}

        def vcol(name, ft):
            c = FT * VEC[name] + ft
            return vec[:, c:c + 1]

        def w(name, kt, c0, cn):
            width = next(o for n, o, _ in WEIGHTS if n == name)
            c = W_AT[name] * P + kt * width + c0
            return wt[:, c:c + cn]

        SLOTS = 32
        arena = [sb(f"arena{u}", [P, SLOTS * 512]) for u in range(STREAMS)]
        xT = [sb(f"xT{u}", [P, FT, T + 2]) for u in range(STREAMS)]
        k_in = [sb(f"tokens_in{u}", [P, TT, D]) for u in range(STREAMS)]
        out_sb = [sb(f"out_sb{u}", [P, TT, D]) for u in range(STREAMS)]
        stats = [sb(f"stats{u}", [P, TT, 6]) for u in range(2 * STREAMS)]
        meanvar = [sb(f"meanvar{u}", [P, TT, 2]) for u in range(2 * STREAMS)]
        rstd = [sb(f"rstd{u}", [P, TT]) for u in range(2 * STREAMS)]
        smax = [sb(f"smax{u}", [P, 4]) for u in range(STREAMS)]
        ssum = [sb(f"ssum{u}", [P, 4]) for u in range(STREAMS)]
        gn = [sb(f"gn{u}", [P, 4, TT * NH]) for u in range(STREAMS)]

        def slot(u, s, n=1):
            return arena[u][:, s * 512:(s + n) * 512]

        def two(u, s):
            return slot(u, s).rearrange("p (a b) -> p a b", a=2)

        H, XN, TN, N0, BASE = 0, 1, 29, 30, 31
        HTs, QK, VT, EX, PT, AT_ = 14, 15, 17, 18, 19, 20
        DIFF, XR, XK, RELU, KSQ, TANH, GATED, MID = 21, 22, 23, 24, 25, 26, 27, 28
        DX, XM, TMP, XF, XXX, ZT = 5, 6, (7, 4), 8, 13, 14
        EW, CS, CSB, CF, CB, EFN, EBN = 15, 16, 17, 18, 19, 20, 21
        RF, RB, KF, KB, RFM, RBM, VV, G2 = 22, 23, 24, 25, 26, 28, 30, 31
        THG, KTM, SBD, AB = 3, 13, 14, 5
        YF, YC, SQ, ZN, ZG, ZTs = 5, 6, 7, 8, 9, 10
        HF = 2
        VE = 3
        GW, GB = 1, 2
        THF, SF, HM = 5, 8, 11

        banks = [ctx.enter_context(nc.psum_tensor(f"bank{b}", [P, 512], f32)) for b in range(NB)]

        def bank2(b):
            return banks[b][:, :].rearrange("p (a b) -> p a b", a=2)

        full = [sem(f"bank{b}_full") for b in range(NB)]
        emptied = [sem(f"bank{b}_emptied") for b in range(NB)]
        inputs_in = sem("inputs_in")
        c_in = sem("c_in")
        vec_in = sem("vec_in")
        small_in = sem("small_in")
        weights_in = [sem(f"weights_in_{n}") for n, _, _ in WEIGHTS]
        ident_made = sem("ident_made")
        consts_made = sem("consts_made")
        parity_made = sem("parity_made")
        dequantized = sem("dequantized")
        act_dt = sem("act_dt")
        poles_made = sem("poles_made")
        cb_made = sem("cb_made")
        powers_made = sem("powers_made")
        q_start = sem("q_start")
        hi_made = sem("high_powers_made")
        cross_made = sem("cross_made")
        p_made = sem("p_made")
        k_stored = [sem(f"k_stored{i}") for i in range(2)]
        k_loaded = [sem(f"k_loaded{u}") for u in range(STREAMS)]
        out_free = [sem(f"out_free{u}") for u in range(STREAMS)]
        dve_chain = sem("dve_chain")
        pool_chain = sem("pool_chain")
        act_chain = sem("act_chain")
        main_dve_chain = sem("main_dve_chain")
        main_pool_chain = sem("main_pool_chain")

        NAMES = {}

        def product(name, per_batch=1):
            NAMES[name] = (sem(name), per_batch)
            return NAMES[name][0]

        def at(name, g, k=None):
            s, n = NAMES[name]
            return s, g * n + (n if k is None else k)

        def norm_at(p, n):
            return (STREAMS + p.u, p.j + 1) if n == 4 else (p.u, p.j * 4 + (n + 1))

        var_ready = [sem(f"var_ready{u}") for u in range(2 * STREAMS)]
        rstd_ready = [sem(f"rstd_ready{u}") for u in range(2 * STREAMS)]
        normed = [sem(f"normed{u}") for u in range(2 * STREAMS)]

        for name, n in [("base_ready", 1), ("max_ready", 1),
                        ("diff_ready", 1), ("xr_ready", 1), ("xk_ready", 1), ("ksq_ready", 1),
                        ("xm_ready", 1), ("mixed", NMIX), ("tanh_low", 1), ("tanh_r", 1),
                        ("tanh_g", 1), ("cs_ready", 1), ("csb_ready", 1), ("cf_ready", 1), ("cb_ready", 1),
                        ("ef_ready", 1), ("eb_ready", 1), ("rf_ready", 1), ("kf_ready", 1),
                        ("rfm_ready", 1), ("rbm_ready", 1), ("low_copied", 16), ("centred", 1), ("squared", 1),
                        ("affine_ready", 1),
                        ("gated_ready", 1), ("ve_ready", 1), ("tanh_gate", 3)]:
            product(name, n)

        waits_apart = {e: sem(f"waits_apart_{e}") for e in ("pool", "dve")}

        class Chain:

            def __init__(self, eng, s, per_loop):
                self.eng, self.sem, self.per_loop = eng, s, per_loop
                self.base, self.local, self.seg = 0, 0, "first"

            def link(self, p, ins):
                if p.seg != self.seg:
                    if self.seg == "loop":
                        assert self.local == self.per_loop, self.local
                        self.base += ROUNDS * self.local
                    else:
                        self.base += self.local
                    self.seg, self.local = p.seg, 0
                self.local += 1
                ins.then_inc(self.sem, 1)
                n = self.base + self.local
                self.eng.wait_ge(self.sem, p.r * self.per_loop + n if p.seg == "loop" else n)

        def run(eng, steps):
            for seg in ("first", "loop", "last"):
                if seg == "loop":
                    with eng.Fori(0, ROUNDS) as r:
                        for step, p in places(seg, r):
                            if step in steps:
                                steps[step](p)
                else:
                    for step, p in places(seg, 0):
                        if step in steps:
                            steps[step](p)

        def apart(eng, name):
            eng.sem_inc(waits_apart[name], 1)

        block = ctx.enter_context(nc.Block())

        flat = {0: 0, 1: 0}

        def carve(a, n):
            c = flat[a]
            flat[a] += n
            assert flat[a] <= SLOTS * 512
            return arena[a][:, c:c + n]

        nat = {}
        for name, o, i in WEIGHTS:
            nat[name] = carve(0, (o // P) * i)
        pole = carve(1, 2 * TT * 2 * NS).rearrange("p (c t d n) -> p c t d n", c=2, t=TT, d=2)
        b_nat = carve(1, TT * NS * 2).rearrange("p (t n c) -> p t n c", t=TT, c=2)
        c_nat = carve(1, B * TT * NS * 2).rearrange("p (b t n c) -> p b t n c", b=B, t=TT, c=2)
        cb_nat = carve(1, 2 * B * TT * 2 * NS).rearrange("p (c b t d n) -> p c b t d n", c=2, b=B, t=TT, d=2)
        cbT = carve(1, 2 * B * T).rearrange("p (c b t) -> p c b t", c=2, b=B)
        zp = carve(1, 8 * 2 * T).rearrange("p (k c t) -> p k c t", k=8, c=2)
        pbuf = cb_nat.rearrange("p c b t d n -> p (c b t d n)")
        pb = [pbuf[:, i * 2048:(i + 1) * 2048].rearrange("p (t b a) -> p t b a", t=TC, b=B) for i in range(2)]
        cross = c_nat.rearrange("p b t n c -> p (b t n c)").rearrange("p (t b a) -> p t b a", t=TC, b=B)
        q1 = [carve(0, TC * LO).rearrange("p (t l) -> p t l", t=TC) for _ in range(2)]
        q2 = carve(1, TC * LO).rearrange("p (t l) -> p t l", t=TC)
        tmp1 = carve(0, TC * LO // 2)
        tmp2 = carve(0, TC * LO // 2)
        e1 = [sb(f"high_re{i}", [P, TC * HI])[:, :].rearrange("p (t a) -> p t a", t=TC) for i in range(2)]
        e2 = [carve(a, TC * HI).rearrange("p (t a) -> p t a", t=TC) for a in range(2)]
        etmp = [carve(0, TC * HI // 2) for _ in range(2)]
        ks = [carve(0, TC * LO) for _ in range(2)]
        work = [k_in[i // 4][:, :, :].rearrange("p t d -> p (t d)")[:, (i % 4) * P:(i % 4 + 1) * P] for i in range(8)]
        inv_nat, aim_nat = work[6], work[7]
        logdt = sb("log_dt", [P, TT])
        halfdt = sb("half_dt", [P, TT])
        sqt = [wt[:, i * 256:(i + 1) * 256] for i in range(4)]

        @block.sync
        def _(sp):
            with nc.allow_non_contiguous_dma(reason="per-token scalars"):
                sp.dma_start(logdt[:, :], t_in["L0_tok_log_dt"].rearrange("(t p) -> p t", p=P)).then_inc(inputs_in, 16)
            sp.dma_start(inv_nat.rearrange("p (t n) -> p t n", t=TT),
                         t_in["L0_tok_inv_A_real"].rearrange("(t p) n -> p t n", p=P)).then_inc(inputs_in, 16)
            sp.dma_start(aim_nat.rearrange("p (t n) -> p t n", t=TT),
                         t_in["L0_tok_A_imag"].rearrange("(t p) n -> p t n", p=P)).then_inc(inputs_in, 16)
            sp.dma_start(b_nat, t_in["L0_tok_B_ri"].rearrange("(t p) n c -> p t n c", p=P)).then_inc(inputs_in, 16)
            for tt in range(TT):
                sp.dma_start(c_nat[:, :, tt].rearrange("p b n c -> p b (n c)"),
                             t_in["x"][:, tt * P:(tt + 1) * P].rearrange("b p n c -> p b (n c)")).then_inc(c_in, 16)
            src = {"qkv": "L0_attn_qkv_w", "proj": "L0_attn_proj_w", "ffn_r": "L0_ffn_W_r", "ffn_k": "L0_ffn_W_k",
                   "ffn_v": "L0_ffn_W_v", "r": "L1_attn_W_r", "k": "L1_attn_W_k", "v": "L1_attn_W_v",
                   "g": "L1_attn_W_g", "o": "L1_attn_W_o", "gate": "L1_ffn_w_gate", "up": "L1_ffn_w_up",
                   "down": "L1_ffn_w_down"}
            for (name, o, i), s in zip(WEIGHTS, weights_in):
                dst = nat[name].bitcast(i32) if name in ("gate", "up", "down") else nat[name]
                sp.dma_start(dst.rearrange("p (o i) -> p o i", i=i),
                             t_in[src[name]].rearrange("(o p) i -> p o i", p=P)).then_inc(s, 16)

            with sp.Fori(0, GEN_ROUNDS) as r:
                for c in range(2):
                    for b in (2 * c, 2 * c + 1):
                        sp.wait_ge(emptied[b], r + (USED_A[b] + 1))
                    sp.dma_start(kd[:, bass.ds((r * 2 + c) * TC, TC), :],
                                 ks[c][0:B * HI, :].rearrange("p (t l) -> p t l", t=TC)).then_inc(k_stored[c], 16)
            for c in range(2):
                sp.wait_ge(k_stored[c], 16 * (GEN_ROUNDS + 1))

            def load(g, u):
                for tt in range(TT):
                    sp.dma_start(k_in[u][:, tt, :].rearrange("p (a l) -> p a l", a=HI),
                                 kd[bass.ds(g * HI, HI), tt * P:(tt + 1) * P, :].rearrange("a p l -> p a l"))\
                      .then_inc(k_loaded[u], 16)

            def load_after(p):
                sp.wait_ge(*at("base_ready", p.g))
                load(p.g + 2, p.u)

            def store(p):
                b, v = p.result("down")
                sp.wait_ge(emptied[b], v)
                sp.dma_start(out[bass.ds(p.g, 1), :, :].rearrange("o (t p) f -> p (o t) f", p=P), out_sb[p.u][:, :, :])\
                  .then_inc(out_free[p.u], 16)

            for u in range(STREAMS):
                load(u, u)
            for step, p in places("first", 0):
                if step == "norms":
                    load_after(p)
            with sp.Fori(0, ROUNDS - 1) as r:
                for step, p in places("loop", r):
                    if step == "norms":
                        load_after(p)
                    if step == "down":
                        store(p)
            for step, p in places("loop", ROUNDS - 1):
                if step == "down":
                    store(p)
            for step, p in places("last", 0):
                if step == "down":
                    store(p)
            for u in range(STREAMS):
                sp.wait_ge(out_free[u], 16 * (B // STREAMS + 1))

        @block.gpsimd
        def _(pool):
            pl = nc.gpsimd
            chain = [0]

            def link(ins):
                chain[0] += 1
                ins.then_inc(pool_chain, 1)
                pool.wait_ge(pool_chain, chain[0])

            link(pl.memset(ident[:, :], 0.0))
            pl.affine_select(out=ident[:, :], in_=ident[:, :], compare_op=ALU.not_equal, fill=1.0, base=0,
                             pattern=[[-1, P]], channel_multiplier=1).then_inc(ident_made, 1)
            link(pl.memset(blockdiag[:, :], 1.0))
            bdv = blockdiag[:, :]
            link(pl.affine_select(out=bdv, in_=bdv, compare_op=ALU.is_ge, fill=0.0, base=0,
                                  pattern=[[-HD, P // HD], [0, HD]], channel_multiplier=1))
            link(pl.affine_select(out=bdv, in_=bdv, compare_op=ALU.is_ge, fill=0.0, base=HD - 1,
                                  pattern=[[HD, P // HD], [0, HD]], channel_multiplier=-1))
            link(pl.memset(above[:, :, :], 1.0))
            link(pl.affine_select(out=above[:, :, :], in_=above[:, :, :], compare_op=ALU.is_gt, fill=0.0, base=0,
                                  pattern=[[0, 2], [-1, P]], channel_multiplier=1))
            link(pl.memset(heads4[:, :], 1.0))
            link(pl.affine_select(out=heads4[:, :], in_=heads4[:, :], compare_op=ALU.is_ge, fill=0.0, base=0,
                                  pattern=[[-2 * HD, 4]], channel_multiplier=1))
            link(pl.affine_select(out=heads4[:, :], in_=heads4[:, :], compare_op=ALU.is_ge, fill=0.0, base=HD - 1,
                                  pattern=[[2 * HD, 4]], channel_multiplier=-1))
            link(pl.memset(ones[:, :], 1.0))
            link(pl.memset(head_sel[:, :, :, :], 0.0))
            link(pl.memset(head_sel[:, 0, 0, :], 1.0))
            link(pl.memset(head_sel[:, 1, 1, :], 1.0))
            for u in range(STREAMS):
                link(pl.memset(xT[u][:, :, :], 0.0))
            pl.memset(neg_half[:, :], -0.5).then_inc(consts_made, 1)
            for q in (q1[0], q1[1], q2):
                link(pl.memset(q[:, :, 0:1], 0.0))
            for q in (e1[0], e1[1], e2[0], e2[1]):
                link(pl.memset(q[:, :, 0:1], 0.0))
            for q in q1:
                link(pl.memset(q[0:NS, :, 0:1], 2.0))
            link(pl.memset(q2[NS:P, :, 0:1], 2.0))
            for q in e1:
                link(pl.memset(q[0:NS, :, 0:1], 1.0))
            for q in e2:
                link(pl.memset(q[NS:P, :, 0:1], 1.0))
            pl.memset(ks[0], 0.0).then_inc(k_stored[0], 16)
            pl.memset(ks[1], 0.0).then_inc(k_stored[1], 16)
            for u in range(STREAMS):
                pl.memset(out_sb[u][:, :, :], 0.0).then_inc(out_free[u], 16)
            link(pl.memset(etmp[0], 0.0))
            pl.memset(etmp[1], 0.0).then_inc(q_start, 1)
            pool.wait_ge(q_start, 1)

            pool.wait_ge(powers_made, 1)
            for c in range(2 * B * TT // 4):
                n = PRE_VEC + PRE_POLE + c
                pool.wait_ge(emptied[n % NB], n // NB + 1)
            gen_base = chain[0]
            GEN_LINKS = 2 * (4 + 4 + 3)
            with pool.Fori(0, GEN_ROUNDS) as r:
                local = [0]

                def glink(ins):
                    local[0] += 1
                    ins.then_inc(pool_chain, 1)
                    pool.wait_ge(pool_chain, r * GEN_LINKS + (gen_base + local[0]))
                    apart(pool, "pool")

                for c in range(2):
                    t0 = (r * 2 + c) * TC
                    pool.wait_ge(p_made, (r * 2 + c) + 1)
                    apart(pool, "pool")
                    for lv, m in enumerate((1, 2, 4)):
                        zr = zp[:, 5 + lv, 0, bass.ds(t0, TC)].unsqueeze(2).to_broadcast([P, TC, m])
                        zi = zp[:, 5 + lv, 1, bass.ds(t0, TC)].unsqueeze(2).to_broadcast([P, TC, m])
                        ta = etmp[0][:, 0:TC * m].rearrange("p (t a) -> p t a", t=TC)
                        tb = etmp[1][:, 0:TC * m].rearrange("p (t a) -> p t a", t=TC)
                        pl.tensor_tensor(ta, e1[c][:, :, 0:m], zr, ALU.mult)
                        glink(pl.tensor_tensor(tb, e2[c][:, :, 0:m], zi, ALU.mult))
                        glink(pl.tensor_tensor(e1[c][:, :, m:2 * m], ta, tb, ALU.add))
                        pl.tensor_tensor(ta, e2[c][:, :, 0:m], zr, ALU.mult)
                        glink(pl.tensor_tensor(tb, e1[c][:, :, 0:m], zi, ALU.mult))
                        last = pl.tensor_tensor(e2[c][:, :, m:2 * m], ta, tb, ALU.subtract)
                        if lv < 2:
                            glink(last)
                        else:
                            last.then_inc(hi_made, 1)
                            pool.wait_ge(hi_made, (r * 2 + c) + 1)
                    pool.wait_ge(p_made, (r * 2 + c) + 2)
                    apart(pool, "pool")
                    pl.tensor_tensor(cross, cbT[:, 1, :, bass.ds(t0, TC)].rearrange("p b t -> p t b").unsqueeze(3)
                                     .to_broadcast([P, TC, B, HI]),
                                     e2[c].unsqueeze(2).to_broadcast([P, TC, B, HI]), ALU.mult).then_inc(cross_made, 1)
                assert local[0] == GEN_LINKS, local[0]
            pool.wait_ge(weights_in[0], 16)

            for n in range(PRE_A + PRE_W):
                pool.wait_ge(emptied[n % NB], n // NB + 1)
            chain_ = Chain(pool, main_pool_chain, 2 * (5 + 1))

            def rstd_of(p, n):
                u, v = norm_at(p, n)
                pool.wait_ge(var_ready[u], v)
                apart(pool, "pool")
                chain_.link(p, pl.tensor_scalar(rstd[u][:, :], meanvar[u][:, :, 1], LN_EPS, 1.0, ALU.add, ALU.mult))
                pl.tensor_tensor(rstd[u][:, :], rstd[u][:, :], neg_half[:, 0:TT], ALU.pow).then_inc(rstd_ready[u], 1)

            def norms(p):
                u = p.u
                rstd_of(p, 0)
                rstd_of(p, 1)
                pool.wait_ge(normed[norm_at(p, 0)[0]], norm_at(p, 0)[1])
                chain_.link(p, pl.tensor_tensor(two(u, BASE), k_in[u][:, :, :], two(u, TN), ALU.add))
                pl.tensor_tensor(two(u, BASE), two(u, BASE), pj_bias[:, :].unsqueeze(1).to_broadcast([P, TT, D]),
                                 ALU.add).then_inc(at("base_ready", p.g)[0], 1)

            def attn_out(p):
                rstd_of(p, 2)

            def xT0(p):
                b, v = p.result("xT0")
                pool.wait_ge(emptied[b], v)
                pl.tensor_tensor(two(p.u, DIFF), xT[p.u][:, :, 1:T + 1], xT[p.u][:, :, 0:T], ALU.subtract)\
                  .then_inc(at("diff_ready", p.g)[0], 1)

            def ffn_v(p):
                rstd_of(p, 3)

            def mix(p):
                u = p.u
                for f in range(NMIX):
                    b, v = p.result("mix", f)
                    pool.wait_ge(emptied[b], v)
                    pl.tensor_tensor(two(u, XF + f), two(u, TMP[f % 2]), xT[u][:, :, 1:T + 1], ALU.add)\
                      .then_inc(at("mixed", p.g)[0], 1)

            def decay(p):
                pool.wait_ge(*at("cs_ready", p.g))
                pl.tensor_tensor(two(p.u, CSB), two(p.u, CS), two(p.u, EW), ALU.add)\
                  .then_inc(at("csb_ready", p.g)[0], 1)

            def factors(p):
                u = p.u
                b, v = p.result("query")
                pool.wait_ge(emptied[b], v)
                apart(pool, "pool")
                for e in range(2):
                    last = pl.tensor_scalar(
                        slot(u, RBM, 2).rearrange("p (d j e i) -> p d j e i", d=FT, j=TT, e=2)[:, :, :, e, :],
                        slot(u, RB).rearrange("p (d j i) -> p d j i", d=FT, j=TT),
                        parity[:, e:e + 1], 1.0, ALU.mult, ALU.mult)
                last.then_inc(at("rbm_ready", p.g)[0], 1)

            def gate(p):
                u = p.u
                b, v = p.result("gate")
                pool.wait_ge(emptied[b], v)
                for dst, row in ((GW, lnw), (GB, lnb)):
                    last = pl.tensor_tensor(two(u, dst), two(u, G2), row[:, :].unsqueeze(1).to_broadcast([P, TT, D]),
                                            ALU.mult)
                last.then_inc(at("affine_ready", p.g)[0], 1)
                b, v = p.result("value")
                pool.wait_ge(emptied[b], v)
                pl.tensor_tensor(slot(u, VE, 2).rearrange("p (h e d) -> p h e d", h=TT * NH // 2, e=2),
                                 slot(u, VV).rearrange("p (h d) -> p h d", h=TT * NH // 2).unsqueeze(2)
                                 .to_broadcast([P, TT * NH // 2, 2, 2 * HD]),
                                 head_sel[:, :, :, :].rearrange("p e f d -> p e (f d)").unsqueeze(1)
                                 .to_broadcast([P, TT * NH // 2, 2, 2 * HD]), ALU.mult)\
                  .then_inc(at("ve_ready", p.g)[0], 1)

            def mix_out(p):
                rstd_of(p, 4)

            run(pool, {"norms": norms, "attn_out": attn_out, "xT0": xT0, "ffn_v": ffn_v, "mix": mix, "decay": decay,
                       "gate": gate, "factors": factors, "mix_out": mix_out})

        @block.scalar
        def _(act):
            ac = nc.scalar
            rows = ["L0_attn_norm_w", "L0_attn_norm_b", None, "L0_ffn_mu_r", "L0_ffn_mu_k", "L1_attn_time_maa_x",
                    "L1_attn_time_maa_w", "L1_attn_time_maa_k", "L1_attn_time_maa_v", "L1_attn_time_maa_r",
                    "L1_attn_time_maa_g", "L1_attn_time_decay"]
            for i, name in enumerate(rows):
                if name is None:
                    src = t_in["L0_attn_qkv_b"][2 * D:3 * D]
                elif name.startswith("L1"):
                    src = t_in[name][0, 0, :]
                else:
                    src = t_in[name]
                act.dma_start(vec_rows[FT * i:FT * (i + 1), :], src.rearrange("(t p) -> t p", p=P)).then_inc(vec_in, 16)
            act.dma_start(w1[:, :, :], t_in["L1_attn_time_maa_w1"].rearrange("(t p) m -> p t m", p=P)).then_inc(small_in, 16)
            w2 = t_in["L1_attn_time_maa_w2"].rearrange("f m d -> (f m) d")
            act.dma_start(w2a[:, :], w2[0:P, :]).then_inc(small_in, 16)
            act.dma_start(w2b[:, :], w2[P:P + MIX, :]).then_inc(small_in, 16)
            act.dma_start(dw1[:, :, :], t_in["L1_attn_time_decay_w1"].rearrange("(t p) m -> p t m", p=P)).then_inc(small_in, 16)
            act.dma_start(dw2[:, :], t_in["L1_attn_time_decay_w2"]).then_inc(small_in, 16)
            for dst, src in ((qk_bias, t_in["L0_attn_qkv_b"][0:2 * D]), (pj_bias, t_in["L0_attn_proj_b"]),
                             (lnw, t_in["L1_attn_ln_w"]), (lnb, t_in["L1_attn_ln_b"])):
                act.dma_start(dst[:, :], src.partition_broadcast(P)).then_inc(small_in, 16)

            act.wait_ge(inputs_in, 64)
            ac.activation(halfdt[:, :], logdt[:, :], ACT.Exp).then_inc(act_dt, 1)
            ac.activation(work[0], inv_nat, ACT.Exp).then_inc(act_dt, 1)

            def copy_out(dst, b, v, src=None):
                act.wait_ge(full[b], v)
                ac.activation(dst, banks[b][:, :] if src is None else src, ACT.Copy).then_inc(emptied[b], 1)

            act.wait_ge(full[0], 1)
            ac.activation(vec[:, :], banks[0][:, 0:24], ACT.Copy).then_inc(emptied[0], 1)
            n = PRE_VEC
            copy_out(zp[:, 0].rearrange("p c t -> p (c t)"), n % NB, n // NB + 1)
            for k in range(PRE_CB):
                n = PRE_VEC + PRE_POLE + k
                copy_out(cbT.rearrange("p c b t -> p (c b t)")[:, k * 512:(k + 1) * 512], n % NB, n // NB + 1)
            act.wait_ge(powers_made, 1)
            for k in range(W_GROUPS):
                n = PRE_A + k
                copy_out(wt[:, k * 512:(k + 1) * 512], n % NB, n // NB + 1)
            with act.Fori(0, GEN_ROUNDS) as r:
                for c in range(2):
                    act.wait_ge(k_stored[c], r * 16 + 16)
                    for h in range(2):
                        b = 2 * c + h
                        act.wait_ge(full[b], r + (USED_A[b] + 1))
                        ac.activation(ks[c][0:B * HI, h * 512:(h + 1) * 512], banks[b][0:B * HI, :], ACT.Copy)\
                          .then_inc(emptied[b], 1)

            def transposed(step):
                def f(p):
                    b, v = p.result(step)
                    act.wait_ge(full[b], v)
                    ac.activation(xT[p.u][:, :, 1:T + 1], bank2(b), ACT.Copy).then_inc(emptied[b], 1)
                return f

            def copied(step, dst, k=0):
                def f(p):
                    b, v = p.result(step, k)
                    copy_out(slot(p.u, dst), b, v)
                return f

            def affine(p, dst, step, k, func, bias, scale=None):
                b, v = p.result(step, k)
                act.wait_ge(full[b], v)
                for ft in range(FT):
                    last = ac.activation(two(p.u, dst)[:, ft, :], bank2(b)[:, ft, :], func, bias=vcol(bias, ft),
                                         scale=1.0 if scale is None else vcol(scale, ft))
                last.then_inc(emptied[b], 1)

            def scores(p):
                u = p.u
                b, v = p.result("scores")
                act.wait_ge(*at("max_ready", p.g))
                for qt in range(FT):
                    last = ac.activation(two(u, EX)[:, qt, :], bank2(b)[:, qt, :], ACT.Exp,
                                         bias=smax[u][:, 2 + qt:3 + qt], scale=QK_SCALE,
                                         accum_out=ssum[u][:, qt:qt + 1])
                last.then_inc(emptied[b], 1)

            def ffn_kr(p):
                u = p.u
                b, v = p.result("ffn_kr", 0)
                act.wait_ge(full[b], v)
                ac.activation(slot(u, RELU), banks[b][:, :], ACT.Relu).then_inc(emptied[b], 1)
                act.wait_ge(emptied[b], v)
                ac.activation(slot(u, KSQ), slot(u, RELU), ACT.Square).then_inc(at("ksq_ready", p.g)[0], 1)
                b, v = p.result("ffn_kr", 1)
                act.wait_ge(full[b], v)
                ac.activation(slot(u, TANH), banks[b][:, :], ACT.Tanh, scale=0.5).then_inc(emptied[b], 1)

            def lowrank(p):
                b, v = p.result("lowrank")
                act.wait_ge(full[b], v)
                ac.activation(slot(p.u, XXX)[:, 0:T], banks[b][:, 0:T], ACT.Tanh)
                ac.activation(slot(p.u, XXX)[0:MIX, T:2 * T], banks[b][0:MIX, T:2 * T], ACT.Tanh)\
                  .then_inc(emptied[b], 1)

            def low(p):
                b, v = p.result("low")
                act.wait_ge(full[b], v)
                ac.activation(slot(p.u, ZT)[0:DEC, 0:T], banks[b][0:DEC, 0:T], ACT.Tanh).then_inc(emptied[b], 1)

            def gate(p):
                b, v = p.result("gate")
                act.wait_ge(full[b], v)
                ac.activation(slot(p.u, THG), banks[b][:, :], ACT.Tanh, scale=0.5).then_inc(at("tanh_g", p.g)[0], 1)

            def factors(p):
                u, g = p.u, p.g
                act.wait_ge(*at("cf_ready", g))
                ac.activation(slot(u, EFN), slot(u, CF), ACT.Exp, scale=-1.0)
                ac.activation(slot(u, CF), slot(u, CF), ACT.Exp).then_inc(at("ef_ready", g)[0], 1)
                act.wait_ge(*at("cb_ready", g))
                ac.activation(slot(u, EBN), slot(u, CB), ACT.Exp, scale=-1.0)
                ac.activation(slot(u, CB), slot(u, CB), ACT.Exp).then_inc(at("eb_ready", g)[0], 1)
                act.wait_ge(*at("rf_ready", g))
                for e in range(2):
                    last = ac.activation(
                        slot(u, RFM, 2).rearrange("p (d j e i) -> p d j e i", d=FT, j=TT, e=2)[:, :, :, e, :],
                        slot(u, RF).rearrange("p (d j i) -> p d j i", d=FT, j=TT), ACT.Copy,
                        scale=parity[:, e:e + 1])
                last.then_inc(at("rfm_ready", g)[0], 1)

            def blocks(c):
                def f(p):
                    for q in range(4):
                        k = 4 * c + q
                        b, v = p.result(f"blocks{c}", q)
                        act.wait_ge(full[b], v)
                        ac.activation(slot(p.u, AB, 8)[:, k * 256:(k + 1) * 256], banks[b][:, 0:256], ACT.Copy)\
                          .then_inc(at("low_copied", p.g)[0], 1)
                return f

            def y_out(p):
                b, v = p.y_result(0)
                copy_out(slot(p.u, YF), b, v)

            def y_tokens(p):
                b, v = p.y_result(1)
                act.wait_ge(emptied[b], v)
                ac.activation(slot(p.u, SQ), slot(p.u, YC), ACT.Square).then_inc(at("squared", p.g)[0], 1)

            def gate_up(c):
                def f(p):
                    b, v = p.result(f"gate_up{c}", 0)
                    act.wait_ge(full[b], v)
                    ac.activation(slot(p.u, THF + c), banks[b][:, :], ACT.Tanh, scale=0.5)\
                      .then_inc(at("tanh_gate", p.g)[0], 1)
                return f

            run(act, {"hT": lambda p: affine(p, HTs, "hT", 0, ACT.Identity, "norm_b", "norm_w"),
                      "qkv": lambda p: affine(p, VT, "qkv", 2, ACT.Identity, "v_bias"),
                      "scores": scores, "probsT": copied("probsT", PT), "xT0": transposed("xT0"), "ffn_kr": ffn_kr,
                      "xT1": transposed("xT1"), "lowrank": lowrank, "low": low, "value": copied("value", VV), "gate": gate,
                      "decay": lambda p: affine(p, EW, "decay", 0, ACT.Exp, "decay"), "factors": factors,
                      "blocks0": blocks(0), "blocks1": blocks(1), "blocks2": blocks(2), "blocks3": blocks(3), "y3": y_out,
                      "yT": y_tokens, "gatedT": copied("gatedT", ZTs), "xT2": transposed("xT2"),
                      "gate_up0": gate_up(0), "gate_up1": gate_up(1), "gate_up2": gate_up(2)})

        @block.vector
        def _(dve):
            vc = nc.vector
            chain = [0]

            def link(ins):
                chain[0] += 1
                ins.then_inc(dve_chain, 1)
                dve.wait_ge(dve_chain, chain[0])

            dve.wait_ge(act_dt, 2)
            link(vc.tensor_scalar(halfdt[:, :], halfdt[:, :], 0.5, None, ALU.mult))
            hx, hy, sqx, sqy, den, num = work[0], work[1], work[2], work[3], work[4], work[5]
            for tt in range(TT):
                s = slice(tt * NS, (tt + 1) * NS)
                link(vc.tensor_scalar(hx[:, s], hx[:, s], halfdt[:, tt:tt + 1], -1.0, ALU.mult, ALU.mult))
                link(vc.tensor_scalar(hy[:, s], aim_nat[:, s], halfdt[:, tt:tt + 1], None, ALU.mult))
            link(vc.tensor_tensor(sqx, hx, hx, ALU.mult))
            link(vc.tensor_tensor(sqy, hy, hy, ALU.mult))
            link(vc.tensor_scalar(den, hx, -1.0, 1.0, ALU.mult, ALU.add))
            link(vc.tensor_tensor(den, den, den, ALU.mult))
            link(vc.tensor_tensor(den, den, sqy, ALU.add))
            link(vc.reciprocal(den, den))
            link(vc.tensor_tensor(num, sqx, sqy, ALU.add))
            link(vc.tensor_scalar(num, num, -1.0, 1.0, ALU.mult, ALU.add))

            def dup(x):
                return x.rearrange("p (t n) -> p t n", t=TT).unsqueeze(2).to_broadcast([P, TT, 2, NS])
            link(vc.tensor_tensor(pole[:, 0], dup(num), dup(den), ALU.mult))
            link(vc.tensor_scalar(hy, hy, 2.0, None, ALU.mult))
            vc.tensor_tensor(pole[:, 1], dup(hy), dup(den), ALU.mult).then_inc(poles_made, 1)

            dve.wait_ge(c_in, 32)
            BH = B // 2
            v_ = [x.rearrange("p (b t n) -> p b t n", b=BH, t=TT) for x in (tmp1, tmp2)]
            br = b_nat[:, :, :, 0].unsqueeze(1).to_broadcast([P, BH, TT, NS])
            bi = b_nat[:, :, :, 1].unsqueeze(1).to_broadcast([P, BH, TT, NS])
            for part, (x, y, op) in enumerate(((br, bi, ALU.subtract), (bi, br, ALU.add))):
                for b0 in range(0, B, BH):
                    link(vc.tensor_tensor(v_[0], c_nat[:, b0:b0 + BH, :, :, 0], x, ALU.mult))
                    link(vc.tensor_tensor(v_[1], c_nat[:, b0:b0 + BH, :, :, 1], y, ALU.mult))
                    for d in range(2):
                        last = vc.tensor_tensor(cb_nat[:, part, b0:b0 + BH, :, d, :], v_[0], v_[1], op)
                        if b0 == 0 or d == 0:
                            link(last)
                        else:
                            last.then_inc(cb_made, 1)
                            dve.wait_ge(cb_made, part + 1)

            n = PRE_VEC
            dve.wait_ge(emptied[n % NB], n // NB + 1)
            for k in range(7):
                zr, zi = zp[:, k, 0, :], zp[:, k, 1, :]
                link(vc.tensor_tensor(sqt[0], zr, zi, ALU.subtract))
                link(vc.tensor_tensor(sqt[1], zr, zi, ALU.add))
                link(vc.tensor_tensor(zp[:, k + 1, 0, :], sqt[0], sqt[1], ALU.mult))
                last = vc.scalar_tensor_tensor(out=zp[:, k + 1, 1, :], in0=zr, scalar=2.0, in1=zi, op0=ALU.mult,
                                               op1=ALU.mult)
                if k < 6:
                    link(last)
                else:
                    last.then_inc(powers_made, 1)
                    dve.wait_ge(powers_made, 1)
            dve.wait_ge(consts_made, 1)
            link(vc.reduce_sum(parity[:, 0:1], heads4[:, :], AX.X))
            vc.tensor_scalar(parity[:, 1:2], parity[:, 0:1], -1.0, 1.0, ALU.mult, ALU.add).then_inc(parity_made, 1)
            for k, name in enumerate(("gate", "up", "down")):
                dve.wait_ge(weights_in[10 + k], 16)
                vc.tensor_scalar(nat[name], nat[name].bitcast(i32), DEQUANT, None, ALU.mult).then_inc(dequantized, 1)

            dve.wait_ge(q_start, 1)
            for k in range(PRE_CB):
                n = PRE_VEC + PRE_POLE + k
                dve.wait_ge(emptied[n % NB], n // NB + 1)
            vc.memset(tmp1, 0.0).then_inc(p_made, 1)
            vc.memset(tmp2, 0.0).then_inc(p_made, 1)
            dve.wait_ge(p_made, 2)
            gen_base = chain[0]
            GEN_LINKS = 2 * (4 * 4 + 2 + 1)
            with dve.Fori(0, GEN_ROUNDS) as r:
                local = [0]

                def glink(ins):
                    local[0] += 1
                    ins.then_inc(dve_chain, 1)
                    dve.wait_ge(dve_chain, r * GEN_LINKS + (gen_base + local[0]))

                for c in range(2):
                    t0 = (r * 2 + c) * TC
                    for b in (2 * c, 2 * c + 1):
                        dve.wait_ge(full[b], r + USED_A[b])
                    for lv in range(5):
                        m = 1 << lv
                        zr = zp[:, lv, 0, bass.ds(t0, TC)].unsqueeze(2).to_broadcast([P, TC, m])
                        zi = zp[:, lv, 1, bass.ds(t0, TC)].unsqueeze(2).to_broadcast([P, TC, m])
                        ta = tmp1[:, 0:TC * m].rearrange("p (t a) -> p t a", t=TC)
                        tb = tmp2[:, 0:TC * m].rearrange("p (t a) -> p t a", t=TC)
                        vc.tensor_tensor(ta, q1[c][:, :, 0:m], zr, ALU.mult)
                        glink(vc.tensor_tensor(tb, q2[:, :, 0:m], zi, ALU.mult))
                        glink(vc.tensor_tensor(q1[c][:, :, m:2 * m], ta, tb, ALU.subtract))
                        if lv < 4:
                            vc.tensor_tensor(ta, q2[:, :, 0:m], zr, ALU.mult)
                            glink(vc.tensor_tensor(tb, q1[c][:, :, 0:m], zi, ALU.mult))
                            glink(vc.tensor_tensor(q2[:, :, m:2 * m], ta, tb, ALU.add))
                    dve.wait_ge(hi_made, (r * 2 + c) + 1)
                    glink(vc.tensor_tensor(pb[c], cbT[:, 0, :, bass.ds(t0, TC)].rearrange("p b t -> p t b").unsqueeze(3)
                                           .to_broadcast([P, TC, B, HI]),
                                           e1[c].unsqueeze(2).to_broadcast([P, TC, B, HI]), ALU.mult))
                    dve.wait_ge(cross_made, (r * 2 + c) + 1)
                    vc.tensor_tensor(pb[c], pb[c], cross, ALU.add).then_inc(p_made, 1)
                assert local[0] == GEN_LINKS, local[0]

            for n in range(PRE_A + PRE_W):
                dve.wait_ge(emptied[n % NB], n // NB + 1)
            for b in range(NB):
                dve.wait_ge(emptied[b], USED_M[b])
            dve.wait_ge(small_in, 16 * 9)
            chain_ = Chain(dve, main_dve_chain, 2 * 35)

            def layer_norm(p, n, src, dst):
                u, v = norm_at(p, n)
                for tt in range(TT):
                    chain_.link(p, vc.bn_stats(stats[u][:, tt, :], src[:, tt, :]))
                    apart(dve, "dve")
                    last = vc.bn_aggr(meanvar[u][:, tt, :], stats[u][:, tt, :])
                last.then_inc(var_ready[u], 1)
                dve.wait_ge(rstd_ready[u], v)
                for tt in range(TT):
                    last = vc.tensor_scalar(dst[:, tt, :], src[:, tt, :], meanvar[u][:, tt, 0:1],
                                            rstd[u][:, tt:tt + 1], ALU.subtract, ALU.mult)
                last.then_inc(normed[u], 1)

            def norms(p):
                dve.wait_ge(k_loaded[p.u], p.j * 32 + 32)
                layer_norm(p, 0, k_in[p.u][:, :, :], two(p.u, TN))
                dve.wait_ge(normed[norm_at(p, 0)[0]], norm_at(p, 0)[1])
                layer_norm(p, 1, two(p.u, TN), two(p.u, N0))

            def qkv(p):
                for tt in range(TT):
                    b, v = p.result("qkv", tt)
                    dve.wait_ge(full[b], v)
                    vc.tensor_tensor(slot(p.u, QK + tt), banks[b][:, :], qk_bias[:, :], ALU.add).then_inc(emptied[b], 1)

            def scores(p):
                u = p.u
                b, v = p.result("scores")
                dve.wait_ge(full[b], v)
                chain_.link(p, vc.reduce_max(smax[u][:, 0:2], bank2(b), AX.X))
                vc.tensor_scalar(smax[u][:, 2:4], smax[u][:, 0:2], -QK_SCALE, None, ALU.mult)\
                  .then_inc(at("max_ready", p.g)[0], 1)

            def attT(p):
                u = p.u
                b, v = p.result("scores")
                dve.wait_ge(emptied[b], v)
                chain_.link(p, vc.reciprocal(ssum[u][:, 2:4], ssum[u][:, 0:2]))
                b, v = p.result("attT")
                dve.wait_ge(full[b], v)
                for qt in range(FT):
                    last = vc.tensor_scalar(two(u, AT_)[:, qt, :], bank2(b)[:, qt, :], ssum[u][:, 2 + qt:3 + qt],
                                            None, ALU.mult)
                last.then_inc(emptied[b], 1)

            def attn_out(p):
                u = p.u
                b, v = p.result("attn_out")
                dve.wait_ge(full[b], v)
                dve.wait_ge(*at("base_ready", p.g))
                vc.tensor_tensor(slot(u, MID), banks[b][:, :], slot(u, BASE), ALU.add).then_inc(emptied[b], 1)
                dve.wait_ge(emptied[b], v)
                layer_norm(p, 2, two(u, MID), two(u, TN))

            def xT0(p):
                u = p.u
                dve.wait_ge(*at("diff_ready", p.g))
                for name, dst, done in (("mu_k", XK, "xk_ready"), ("mu_r", XR, "xr_ready")):
                    for ft in range(FT):
                        last = vc.scalar_tensor_tensor(out=two(u, dst)[:, ft, :], in0=two(u, DIFF)[:, ft, :],
                                                       scalar=vcol(name, ft), in1=xT[u][:, ft, 0:T],
                                                       op0=ALU.mult, op1=ALU.add)
                    last.then_inc(at(done, p.g)[0], 1)

            def ffn_v(p):
                u = p.u
                bt, vt = p.result("ffn_kr", 1)
                dve.wait_ge(emptied[bt], vt)
                b, v = p.result("ffn_v")
                dve.wait_ge(full[b], v)
                vc.scalar_tensor_tensor(out=slot(u, GATED), in0=slot(u, TANH), scalar=1.0, in1=banks[b][:, :],
                                        op0=ALU.add, op1=ALU.mult).then_inc(emptied[b], 1)
                dve.wait_ge(emptied[b], v)
                chain_.link(p, vc.scalar_tensor_tensor(out=slot(u, H), in0=slot(u, GATED), scalar=0.5, in1=slot(u, MID),
                                                       op0=ALU.mult, op1=ALU.add))
                layer_norm(p, 3, two(u, H), two(u, XN))

            def xT1(p):
                u = p.u
                b, v = p.result("xT1")
                dve.wait_ge(emptied[b], v)
                chain_.link(p, vc.tensor_tensor(two(u, TMP[0]), xT[u][:, :, 0:T], xT[u][:, :, 2:T + 2], ALU.add))
                chain_.link(p, vc.scalar_tensor_tensor(out=two(u, DX), in0=two(u, TMP[0]), scalar=0.5,
                                                       in1=xT[u][:, :, 1:T + 1], op0=ALU.mult, op1=ALU.subtract))
                for ft in range(FT):
                    last = vc.scalar_tensor_tensor(out=two(u, XM)[:, ft, :], in0=two(u, DX)[:, ft, :],
                                                   scalar=vcol("maa_x", ft), in1=xT[u][:, ft, 1:T + 1],
                                                   op0=ALU.mult, op1=ALU.add)
                last.then_inc(at("xm_ready", p.g)[0], 1)

            def mix(p):
                u = p.u
                for f, name in enumerate(("maa_w", "maa_k", "maa_v", "maa_r", "maa_g")):
                    b, v = p.result("mix", f)
                    dve.wait_ge(full[b], v)
                    if f >= 2:
                        dve.wait_ge(*at("mixed", p.g, f - 1))
                    for ft in range(FT):
                        last = vc.scalar_tensor_tensor(out=two(u, TMP[f % 2])[:, ft, :], in0=bank2(b)[:, ft, :],
                                                       scalar=vcol(name, ft), in1=two(u, DX)[:, ft, :],
                                                       op0=ALU.add, op1=ALU.mult)
                    last.then_inc(emptied[b], 1)

            def gate(p):
                b, v = p.result("gate")
                dve.wait_ge(*at("tanh_g", p.g))
                vc.scalar_tensor_tensor(out=slot(p.u, G2), in0=slot(p.u, THG), scalar=1.0, in1=banks[b][:, :],
                                        op0=ALU.add, op1=ALU.mult).then_inc(emptied[b], 1)

            def decay(p):
                u, g = p.u, p.g
                b, v = p.result("decay")
                dve.wait_ge(emptied[b], v)
                for ft in range(FT):
                    last = vc.tensor_tensor_scan(two(u, CS)[:, ft, :], ones[:, :], two(u, EW)[:, ft, :], 0.0,
                                                 ALU.mult, ALU.subtract)
                last.then_inc(at("cs_ready", g)[0], 1)
                dve.wait_ge(*at("cs_ready", g))
                for src, dst, first, done in ((CS, CF, None, "cf_ready"), (CSB, CB, "csb_ready", "cb_ready")):
                    if first:
                        dve.wait_ge(*at(first, g))
                    for ft in range(FT):
                        last = vc.tensor_scalar(two(u, dst)[:, ft, :], two(u, src)[:, ft, :],
                                                two(u, src)[:, ft, T // 2:T // 2 + 1], CLIP, ALU.subtract, ALU.min)
                    chain_.link(p, last)
                    vc.tensor_scalar(slot(u, dst), slot(u, dst), -CLIP, None, ALU.max).then_inc(at(done, g)[0], 1)

            def factors(p):
                u, g = p.u, p.g
                br_, vr = p.result("query")
                bk, vk = p.result("key")
                dve.wait_ge(full[bk], vk)
                dve.wait_ge(full[br_], vr)
                dve.wait_ge(*at("ef_ready", g))
                vc.tensor_tensor(slot(u, RF), banks[br_][:, :], slot(u, CF), ALU.mult).then_inc(at("rf_ready", g)[0], 1)
                vc.tensor_tensor(slot(u, KF), banks[bk][:, :], slot(u, EFN), ALU.mult).then_inc(at("kf_ready", g)[0], 1)
                dve.wait_ge(*at("eb_ready", g))
                vc.tensor_tensor(slot(u, RB), banks[br_][:, :], slot(u, EBN), ALU.mult).then_inc(emptied[br_], 1)
                vc.tensor_tensor(slot(u, KB), banks[bk][:, :], slot(u, CB), ALU.mult).then_inc(emptied[bk], 1)

            def keys(p):
                b, v = p.result("keys")
                dve.wait_ge(full[b], v)
                vc.tensor_copy(slot(p.u, KTM), banks[b][:, :]).then_inc(emptied[b], 1)

            def state(p):
                b, v = p.result("state")
                dve.wait_ge(full[b], v)
                vc.tensor_tensor(slot(p.u, SBD).rearrange("p (c d) -> p c d", c=4),
                                 banks[b][:, :].rearrange("p (c d) -> p c d", c=4),
                                 blockdiag[:, :].unsqueeze(1).to_broadcast([P, 4, P]), ALU.mult)\
                  .then_inc(emptied[b], 1)

            def blocks(c):
                def f(p):
                    for q in range(4):
                        k = 4 * c + q
                        b, v = p.result(f"blocks{c}", q)
                        dve.wait_ge(*at("low_copied", p.g, k + 1))
                        apart(dve, "dve")
                        vc.copy_predicated(slot(p.u, AB, 8)[:, k * 256:(k + 1) * 256],
                                           above[:, :, :].rearrange("p e i -> p (e i)").bitcast(i32),
                                           banks[b][:, 256:512]).then_inc(emptied[b], 1)
                return f

            def heads(x):
                return x.rearrange("p (h d) -> p h d", d=HD)

            def y(p):
                u = p.u
                b, v = p.y_result(1)
                dve.wait_ge(full[b], v)
                chain_.link(p, vc.reduce_sum(gn[u][:, 0, :], heads(banks[b][:, :]), AX.X))
                chain_.link(p, vc.tensor_scalar(gn[u][:, 0, :], gn[u][:, 0, :], 1.0 / HD, None, ALU.mult))
                vc.tensor_tensor(heads(slot(u, YC)), heads(banks[b][:, :]),
                                 gn[u][:, 0, :].unsqueeze(2).to_broadcast([P, TT * NH, HD]), ALU.subtract)\
                  .then_inc(emptied[b], 1)

            def head_norm(p):
                u = p.u
                var, root, sq, bits = (gn[u][:, i, :] for i in (1, 2, 3, 0))
                dve.wait_ge(*at("squared", p.g))
                chain_.link(p, vc.reduce_sum(var, heads(slot(u, SQ)), AX.X))
                chain_.link(p, vc.tensor_scalar(var, var, 1.0 / HD, GN_EPS, ALU.mult, ALU.add))
                chain_.link(p, vc.tensor_scalar(bits.bitcast(i32), var.bitcast(i32), 1, None, ALU.logical_shift_right))
                chain_.link(p, vc.tensor_scalar(root.bitcast(i32), bits.bitcast(i32), -1.0, float(0x5f3759df),
                                                ALU.mult, ALU.add))
                for _ in range(3):
                    chain_.link(p, vc.tensor_tensor(sq, root, root, ALU.mult))
                    chain_.link(p, vc.scalar_tensor_tensor(out=sq, in0=sq, scalar=-0.5, in1=var, op0=ALU.mult,
                                                           op1=ALU.mult))
                    chain_.link(p, vc.scalar_tensor_tensor(out=root, in0=sq, scalar=1.5, in1=root, op0=ALU.add,
                                                           op1=ALU.mult))
                chain_.link(p, vc.tensor_tensor(heads(slot(u, ZN)), heads(slot(u, YC)),
                                                root.unsqueeze(2).to_broadcast([P, TT * NH, HD]), ALU.mult))
                dve.wait_ge(*at("affine_ready", p.g))
                chain_.link(p, vc.tensor_tensor(slot(u, ZN), slot(u, ZN), slot(u, GW), ALU.mult))
                chain_.link(p, vc.tensor_tensor(slot(u, ZN), slot(u, ZN), slot(u, GB), ALU.add))
                vc.tensor_scalar(slot(u, ZG), slot(u, ZN), 0.5, None, ALU.mult).then_inc(at("gated_ready", p.g)[0], 1)

            def mix_out(p):
                u = p.u
                b, v = p.result("mix_out")
                dve.wait_ge(full[b], v)
                vc.tensor_tensor(slot(u, HF), banks[b][:, :], slot(u, H), ALU.add).then_inc(emptied[b], 1)
                dve.wait_ge(emptied[b], v)
                layer_norm(p, 4, two(u, HF), two(u, XN))

            def gate_up(c):
                def f(p):
                    u = p.u
                    bg, vg = p.result(f"gate_up{c}", 0)
                    bu, vu = p.result(f"gate_up{c}", 1)
                    dve.wait_ge(*at("tanh_gate", p.g, c + 1))
                    vc.scalar_tensor_tensor(out=slot(u, SF + c), in0=slot(u, THF + c), scalar=1.0,
                                            in1=banks[bg][:, :], op0=ALU.add, op1=ALU.mult).then_inc(emptied[bg], 1)
                    dve.wait_ge(full[bu], vu)
                    dve.wait_ge(emptied[bg], vg)
                    vc.scalar_tensor_tensor(out=slot(u, HM + c), in0=slot(u, SF + c), scalar=0.5,
                                            in1=banks[bu][:, :], op0=ALU.mult, op1=ALU.mult).then_inc(emptied[bu], 1)
                return f

            def down(p):
                b, v = p.result("down")
                dve.wait_ge(full[b], v)
                dve.wait_ge(out_free[p.u], p.j * 16 + 16)
                vc.tensor_tensor(out_sb[p.u][:, :, :], bank2(b), two(p.u, HF), ALU.add).then_inc(emptied[b], 1)

            run(dve, {"norms": norms, "qkv": qkv, "scores": scores, "attT": attT, "attn_out": attn_out, "xT0": xT0,
                      "ffn_v": ffn_v, "xT1": xT1, "mix": mix, "gate": gate, "decay": decay,
                      "factors": factors, "keys": keys, "state": state, "blocks0": blocks(0),
                      "blocks1": blocks(1), "blocks2": blocks(2), "blocks3": blocks(3), "yT": y,
                      "head_norm": head_norm, "mix_out": mix_out, "gate_up0": gate_up(0), "gate_up1": gate_up(1),
                      "gate_up2": gate_up(2), "down": down})

        @block.tensor
        def _(pe):
            mm = nc.tensor.matmul

            def block_t(b, c, src, cols=P):
                return nc.tensor.transpose(banks[b][0:cols, c * P:c * P + src.shape[0]], src,
                                           ident[0:src.shape[0], 0:src.shape[0]])

            pe.wait_ge(ident_made, 1)
            pe.wait_ge(vec_in, 16 * 12)
            block_t(0, 0, vec_rows[:, :]).then_inc(full[0], 1)
            n = PRE_VEC
            pe.wait_ge(poles_made, 1)
            for part in range(2):
                for tt in range(TT):
                    last = block_t(n % NB, part * TT + tt, pole[:, part, tt].rearrange("p d n -> p (d n)"))
            last.then_inc(full[n % NB], 1)
            blk = 0
            for part in range(2):
                pe.wait_ge(cb_made, part + 1)
                for b in range(B):
                    for tt in range(TT):
                        n = PRE_VEC + PRE_POLE + blk // 4
                        if blk % 4 == 0 and n >= NB:
                            pe.wait_ge(emptied[n % NB], n // NB)
                        last = block_t(n % NB, blk % 4, cb_nat[:, part, b, tt].rearrange("p d n -> p (d n)"))
                        if blk % 4 == 3:
                            last.then_inc(full[n % NB], 1)
                        blk += 1
            blk = 0
            for k, (name, o, i) in enumerate(WEIGHTS):
                pe.wait_ge(weights_in[k], 16)
                if name in ("gate", "up", "down"):
                    pe.wait_ge(dequantized, k - 9)
                src = nat[name].rearrange("p (o i) -> p o i", i=i)
                for kt in range(i // P):
                    for ot in range(o // P):
                        n = PRE_A + blk // 4
                        if blk % 4 == 0:
                            pe.wait_ge(emptied[n % NB], n // NB)
                        last = block_t(n % NB, blk % 4, src[:, ot, kt * P:(kt + 1) * P])
                        if blk % 4 == 3:
                            last.then_inc(full[n % NB], 1)
                        blk += 1
            with pe.Fori(0, GEN_ROUNDS) as r:
                for c in range(2):
                    pe.wait_ge(p_made, (r * 2 + c) + 3)
                    for h in range(2):
                        b = 2 * c + h
                        pe.wait_ge(emptied[b], r + USED_A[b])
                        for t in range(TC // 2):
                            tl = h * (TC // 2) + t
                            last = mm(banks[b][0:B * HI, t * LO:(t + 1) * LO],
                                      pb[c][:, tl].rearrange("p b a -> p (b a)"), q1[c][:, tl, :],
                                      start=True, stop=True)
                        last.then_inc(full[b], 1)
            pe.wait_ge(small_in, 16 * 9)

            def free_bank(p, step, k=0):
                b, v = p.result(step, k)
                pe.wait_ge(emptied[b], v - 1)
                return b

            def wait_emptied(p, step, k=0):
                b, v = p.result(step, k)
                pe.wait_ge(emptied[b], v)

            def transposes(p, step, s):
                transposed_to(free_bank(p, step), p, s)

            def transposed_to(b, p, s):
                for tt in range(TT):
                    for ft in range(FT):
                        last = nc.tensor.transpose(bank2(b)[:, ft, tt * P:(tt + 1) * P],
                                                   two(p.u, s)[:, tt, ft * P:(ft + 1) * P], ident[:, :])
                last.then_inc(full[b], 1)

            def feature_major(b, name, x, c0=0):
                for ft in range(FT):
                    for kt in range(FT):
                        last = mm(bank2(b)[:, ft, :], w(name, kt, c0 + ft * P, P), x[:, kt, :],
                                  start=(kt == 0), stop=(kt == FT - 1))
                last.then_inc(full[b], 1)

            def token_major(b, name, x, kts=FT):
                for tt in range(TT):
                    for kt in range(kts):
                        last = mm(bank2(b)[:, tt, :], x(kt, tt), w(name, kt, 0, D),
                                  start=(kt == 0), stop=(kt == kts - 1))
                last.then_inc(full[b], 1)

            def tok(u, s):
                return lambda kt, tt: two(u, s)[:, kt, tt * P:(tt + 1) * P]

            def after_norm(step, n, s):
                def f(p):
                    pe.wait_ge(normed[norm_at(p, n)[0]], norm_at(p, n)[1])
                    transposes(p, step, s)
                return f

            def qkv(p):
                u = p.u
                wait_emptied(p, "hT")
                for tt in range(TT):
                    b = free_bank(p, "qkv", tt)
                    for kt in range(FT):
                        last = mm(banks[b][:, :], two(u, HTs)[:, kt, tt * P:(tt + 1) * P],
                                  w("qkv", kt, 0, 2 * D), start=(kt == 0), stop=(kt == FT - 1))
                    last.then_inc(full[b], 1)
                feature_major(free_bank(p, "qkv", 2), "qkv", two(u, HTs), c0=2 * D)

            def scores(p):
                u = p.u
                wait_emptied(p, "qkv", 0)
                wait_emptied(p, "qkv", 1)
                b = free_bank(p, "scores")
                for qt in range(FT):
                    for tt in range(TT):
                        last = mm(bank2(b)[:, qt, :], slot(u, QK + tt)[:, qt * P:(qt + 1) * P],
                                  slot(u, QK + tt)[:, D:2 * D], start=(tt == 0), stop=(tt == TT - 1))
                last.then_inc(full[b], 1)

            def probsT(p):
                wait_emptied(p, "qkv", 2)
                wait_emptied(p, "scores")
                transposes(p, "probsT", EX)

            def attT(p):
                u = p.u
                wait_emptied(p, "probsT")
                b = free_bank(p, "attT")
                for qt in range(FT):
                    for kt in range(FT):
                        last = mm(bank2(b)[:, qt, :], two(u, PT)[:, kt, qt * P:(qt + 1) * P],
                                  two(u, VT)[:, kt, :], start=(kt == 0), stop=(kt == FT - 1))
                last.then_inc(full[b], 1)

            def attn_out(p):
                wait_emptied(p, "attT")
                token_major(free_bank(p, "attn_out"), "proj", tok(p.u, AT_))

            def ffn_kr(p):
                pe.wait_ge(*at("xk_ready", p.g))
                feature_major(free_bank(p, "ffn_kr", 0), "ffn_k", two(p.u, XK))
                pe.wait_ge(*at("xr_ready", p.g))
                token_major(free_bank(p, "ffn_kr", 1), "ffn_r", tok(p.u, XR))

            def ffn_v(p):
                pe.wait_ge(*at("ksq_ready", p.g))
                token_major(free_bank(p, "ffn_v"), "ffn_v", tok(p.u, KSQ))

            def lowrank(p):
                pe.wait_ge(*at("xm_ready", p.g))
                b = free_bank(p, "lowrank")
                for c0, cn in ((0, P), (P, MIX)):
                    for kt in range(FT):
                        last = mm(bank2(b)[0:cn, c0 // P, :], w1[:, kt, c0:c0 + cn], two(p.u, XM)[:, kt, :],
                                  start=(kt == 0), stop=(kt == FT - 1))
                last.then_inc(full[b], 1)

            def mix(p):
                wait_emptied(p, "lowrank")
                for f in range(NMIX):
                    b = free_bank(p, "mix", f)
                    q = f % 4
                    for ft in range(FT):
                        lhs = (w2a if f < 4 else w2b)[MIX * q:MIX * (q + 1), ft * P:(ft + 1) * P]
                        rhs = slot(p.u, XXX)[MIX * q:MIX * (q + 1), (f // 4) * T:(f // 4 + 1) * T]
                        last = mm(bank2(b)[:, ft, :], lhs, rhs, start=True, stop=True)
                    last.then_inc(full[b], 1)

            def low(p):
                pe.wait_ge(*at("mixed", p.g, 1))
                b = free_bank(p, "low")
                for kt in range(FT):
                    last = mm(banks[b][0:DEC, 0:T], dw1[:, kt, :], two(p.u, XF)[:, kt, :],
                              start=(kt == 0), stop=(kt == FT - 1))
                last.then_inc(full[b], 1)

            def key(p):
                pe.wait_ge(*at("mixed", p.g, 2))
                feature_major(free_bank(p, "key"), "k", two(p.u, XF + 1))

            def value(p):
                pe.wait_ge(*at("mixed", p.g, 3))
                token_major(free_bank(p, "value"), "v", tok(p.u, XF + 2))

            def query(p):
                pe.wait_ge(*at("mixed", p.g, 4))
                feature_major(free_bank(p, "query"), "r", two(p.u, XF + 3))

            def gate(p):
                pe.wait_ge(*at("mixed", p.g, 5))
                token_major(free_bank(p, "gate"), "g", tok(p.u, XF + 4))

            def decay(p):
                wait_emptied(p, "low")
                b = free_bank(p, "decay")
                for ft in range(FT):
                    last = mm(bank2(b)[:, ft, :], dw2[:, ft * P:(ft + 1) * P], slot(p.u, ZT)[0:DEC, 0:T],
                              start=True, stop=True)
                last.then_inc(full[b], 1)


            def keys(p):
                pe.wait_ge(*at("kf_ready", p.g))
                wait_emptied(p, "key")
                b = free_bank(p, "keys")
                for x, s in enumerate((KF, KB)):
                    for ft in range(FT):
                        last = nc.tensor.transpose(bank2(b)[:, x, ft * P:(ft + 1) * P],
                                                   two(p.u, s)[:, ft, x * P:(x + 1) * P], ident[:, :])
                last.then_inc(full[b], 1)

            def state(p):
                u = p.u
                wait_emptied(p, "keys")
                wait_emptied(p, "value")
                b = free_bank(p, "state")
                for x in range(2):
                    for ft in range(FT):
                        c = (x * FT + ft) * P
                        last = mm(banks[b][:, c:c + P], two(u, KTM)[:, x, ft * P:(ft + 1) * P],
                                  two(u, VV)[:, x, ft * P:(ft + 1) * P], start=True, stop=True)
                last.then_inc(full[b], 1)

            def blocks(c):
                def f(p):
                    u = p.u
                    if c == 0:
                        pe.wait_ge(*at("rfm_ready", p.g))
                        pe.wait_ge(*at("rbm_ready", p.g))
                    ft, jb = c // 2, c % 2
                    bs = [free_bank(p, f"blocks{c}", q) for q in range(4)]
                    for x, (ks_, rs_) in enumerate(((KF, RFM), (KB, RBM))):
                        for q in range(4):
                            rows = slice(32 * q, 32 * q + 32)
                            last = mm(banks[bs[q]][:, x * 256:(x + 1) * 256],
                                      two(u, ks_)[rows, ft, jb * P:(jb + 1) * P],
                                      slot(u, rs_, 2)[rows, (ft * 2 + jb) * 256:(ft * 2 + jb + 1) * 256],
                                      start=True, stop=True)
                            if x == 1:
                                last.then_inc(full[bs[q]], 1)
                return f

            def y(part):
                def f(p):
                    u = p.u
                    if part == 0:
                        wait_emptied(p, "state")
                        pe.wait_ge(*at("ve_ready", p.g))
                        b, v = p.y_result(0)
                        pe.wait_ge(emptied[b], v - 1)
                        for x, (s, tt) in enumerate(((RF, 1), (RB, 0))):
                            for ft in range(FT):
                                c = (x * FT + ft) * P
                                mm(bank2(b)[:, ft, tt * P:(tt + 1) * P], slot(u, SBD)[:, c:c + P],
                                   two(u, s)[:, ft, tt * P:(tt + 1) * P], start=(x == 0 and ft == 0), stop=False,
                                   skip_group_check=True)
                    else:
                        b, _ = p.y_result(0)
                    ft, jb = part // 2, part % 2
                    for q in range(4):
                        if part < 3:
                            wait_emptied(p, f"blocks{part}", q)
                        if part == 2:
                            wait_emptied(p, f"blocks3", q)
                        for e in range(2):
                            c = (((jb * NH // 2) + ft * 4 + q) * 2 + e) * 2 * HD
                            last = mm(bank2(b)[2 * HD * q:2 * HD * (q + 1), ft, jb * P:(jb + 1) * P],
                                      slot(u, VE, 2)[:, c:c + 2 * HD],
                                      slot(u, AB, 8)[:, (4 * part + q) * 256 + e * P:(4 * part + q) * 256 + (e + 1) * P],
                                      start=False, stop=(part == 3 and q == 3 and e == 1), skip_group_check=True)
                    if part == 3:
                        last.then_inc(full[b], 1)
                return f

            def yT(p):
                b, v = p.y_result(1)
                pe.wait_ge(emptied[b], v - 1)
                transposed_to(b, p, YF)

            def gatedT(p):
                pe.wait_ge(*at("gated_ready", p.g))
                transposes(p, "gatedT", ZG)

            def mix_out(p):
                wait_emptied(p, "gatedT")
                token_major(free_bank(p, "mix_out"), "o", tok(p.u, ZTs))

            def gate_up(c):
                def f(p):
                    if c == 0:
                        wait_emptied(p, "xT2")
                    x = xT[p.u][:, :, 1:T + 1]
                    feature_major(free_bank(p, f"gate_up{c}", 0), "gate", x, c0=2 * c * P)
                    feature_major(free_bank(p, f"gate_up{c}", 1), "up", x, c0=2 * c * P)
                return f

            def down(p):
                for c in range(3):
                    wait_emptied(p, f"gate_up{c}", 1)
                token_major(free_bank(p, "down"), "down",
                            lambda kt, tt: two(p.u, HM + kt // 2)[:, kt % 2, tt * P:(tt + 1) * P], kts=HT)

            run(pe, {"hT": after_norm("hT", 1, N0), "qkv": qkv, "scores": scores, "probsT": probsT, "attT": attT,
                     "attn_out": attn_out, "xT0": after_norm("xT0", 2, TN), "ffn_kr": ffn_kr, "ffn_v": ffn_v,
                     "xT1": after_norm("xT1", 3, XN), "lowrank": lowrank, "mix": mix, "low": low, "key": key,
                     "value": value, "query": query, "gate": gate, "decay": decay, "keys": keys, "state": state,
                     "blocks0": blocks(0), "blocks1": blocks(1), "blocks2": blocks(2), "blocks3": blocks(3), "y0": y(0),
                     "y1": y(1), "y2": y(2), "y3": y(3), "yT": yT, "gatedT": gatedT, "mix_out": mix_out, "xT2": after_norm("xT2", 4, XN),
                     "gate_up0": gate_up(0), "gate_up1": gate_up(1), "gate_up2": gate_up(2), "down": down})



_INS = ['x', 'L0_tok_log_dt', 'L0_tok_inv_A_real', 'L0_tok_A_imag', 'L0_tok_B_ri', 'L0_attn_norm_w', 'L0_attn_norm_b',
        'L0_attn_qkv_w', 'L0_attn_qkv_b', 'L0_attn_proj_w', 'L0_attn_proj_b', 'L0_ffn_W_r', 'L0_ffn_W_k', 'L0_ffn_W_v',
        'L0_ffn_mu_r', 'L0_ffn_mu_k', 'L1_attn_time_maa_x', 'L1_attn_time_maa_w', 'L1_attn_time_maa_k',
        'L1_attn_time_maa_v', 'L1_attn_time_maa_r', 'L1_attn_time_maa_g', 'L1_attn_time_maa_w1', 'L1_attn_time_maa_w2',
        'L1_attn_time_decay', 'L1_attn_time_decay_w1', 'L1_attn_time_decay_w2', 'L1_attn_W_r', 'L1_attn_W_k',
        'L1_attn_W_v', 'L1_attn_W_g', 'L1_attn_W_o', 'L1_attn_ln_w', 'L1_attn_ln_b', 'L1_ffn_w_gate', 'L1_ffn_w_up',
        'L1_ffn_w_down']


def kernel(**inputs):
    import numpy as _np
    import concourse.bacc as _bacc
    from concourse import mybir as _mybir
    from concourse.bass_utils import run_bass_kernel_spmd as _run

    nc = _bacc.Bacc("TRN2", target_bir_lowering=False, num_devices=1)
    arrays, t_in = {}, {}
    for name in _INS:
        a = _np.ascontiguousarray(inputs[name])
        arrays[f"in_{name}"] = a
        t_in[name] = nc.dram_tensor(f"in_{name}", a.shape, _mybir.dt.from_np(a.dtype), kind="ExternalInput").ap()
    out = nc.dram_tensor("out_0", (B, T, D), f32, kind="ExternalOutput").ap()
    mk_vit_tower(nc, t_in, out)
    r = _run(nc, [arrays], core_ids=[0])
    return r.results[0]["out_0"]
```

```python
import concourse.bass as bass
from concourse import mybir
from contextlib import ExitStack

f32 = mybir.dt.float32
i32 = mybir.dt.int32
ALU = mybir.AluOpType
ACT = mybir.ActivationFunctionType
AX = mybir.AxisListType

B, T, D, NS = 8, 256, 256, 64
P = 128
TT = T // P
FT = D // P
HD = 16
NH = D // HD
MIX, NMIX, DEC = 32, 5, 64
HID = 768
HT = HID // P
LN_EPS = 1e-5
GN_EPS = 1e-5 * 64.0
CLIP = 60.0
QK_SCALE = 1.0 / 16.0
DEQUANT = 1.0 / 127.0

LO, HI = 32, 8
TC = 32
CHUNKS = T // TC
STREAMS = 2

WEIGHTS = [("qkv", 3 * D, D), ("proj", D, D), ("ffn_r", D, D), ("ffn_k", D, D), ("ffn_v", D, D),
           ("r", D, D), ("k", D, D), ("v", D, D), ("g", D, D), ("o", D, D),
           ("gate", HID, D), ("up", HID, D), ("down", D, HID)]
W_AT = {}
_at = 0
for _n, _o, _i in WEIGHTS:
    W_AT[_n] = _at
    _at += (_o // P) * (_i // P)
W_BLOCKS = _at
W_GROUPS = W_BLOCKS // 4

LAYER0 = ["norm0", "apply0", "norm1", "apply1", "base", "hT", "qkv", "scores", "probsT", "attT", "attn_out",
          "apply2", "xT0", "ffn_kr", "ffn_v", "apply3", "xT1", "lowrank"]
HALF = [("next", "norm0"), ("mix", "mixA"), ("ff", "yT"), ("next", "apply0"), ("mix", "low"), ("mix", "mixB"),
        ("next", "norm1"), ("ff", "head_var"), ("mix", "decay"), ("ff", "head_root"), ("mix", "value"),
        ("mix", "key"), ("next", "apply1"), ("next", "hT"), ("ff", "head_norm"), ("mix", "gate"),
        ("mix", "query"), ("mix", "factors"), ("ff", "gatedT"), ("next", "qkv"), ("ff", "mix_out"),
        ("mix", "keys"), ("ff", "apply4"), ("mix", "state"), ("next", "base"), ("next", "scores"),
        ("mix", "blocks0"), ("ff", "xT2"), ("mix", "values"), ("next", "probsT"), ("mix", "blocks1"),
        ("ff", "gate_up0"), ("next", "attT"), ("mix", "blocks2"), ("ff", "gate_up1"), ("mix", "blocks3"),
        ("next", "attn_out"), ("next", "apply2"), ("mix", "blocks4"), ("ff", "gate_up2"), ("next", "xT0"),
        ("mix", "blocks5"), ("mix", "blocks6"), ("next", "ffn_kr"), ("next", "ffn_v"), ("next", "apply3"),
        ("ff", "down"), ("next", "xT1"), ("mix", "blocks7"), ("mix", "y0"), ("mix", "y1"), ("next", "lowrank"),
        ("mix", "y2"), ("mix", "y3")]
MIXES = {"mixA": (0, 1, 2), "mixB": (3, 4)}
FEED_FORWARD = [step for part, step in HALF if part == "ff"]
RESULTS = {"norm0": 0, "norm1": 0, "base": 0, "values": 0, "head_var": 0, "head_root": 0, "head_norm": 0,
           "apply0": 0, "apply1": 0, "apply2": 0, "apply3": 0, "apply4": 0, "hT": 1, "qkv": 3, "scores": 1,
           "probsT": 1, "attT": 1, "attn_out": 1, "xT0": 1, "ffn_kr": 2, "ffn_v": 1, "xT1": 1, "lowrank": 1,
           "mixA": 3, "mixB": 2, "low": 1, "key": 1, "value": 1, "gate": 1, "decay": 1, "query": 1, "factors": 0,
           "keys": 1, "state": 1, "blocks0": 2, "blocks1": 2, "blocks2": 2, "blocks3": 2, "blocks4": 2, "blocks5": 2,
           "blocks6": 2, "blocks7": 2, "y0": 0, "y1": 0, "y2": 0, "y3": 0, "yT": 0, "gatedT": 1, "mix_out": 1,
           "xT2": 1, "gate_up0": 2, "gate_up1": 2, "gate_up2": 2, "down": 1}


def half(n):
    u = n % 2
    out = []
    for part, step in HALF:
        if part == "mix":
            out.append((step, u, 0))
        elif part == "ff" and n > 0:
            out.append((step, 1 - u, -1))
        elif part == "next" and 0 < n < B - 1:
            out.append((step, 1 - u, 1))
    return out


SEGMENTS = {"first": [(s, b, b) for s in LAYER0 for b in range(STREAMS)] + half(0),
            "loop": half(1) + half(2),
            "last": half(B - 1) + [(s, 1, 0) for s in FEED_FORWARD]}
ROUNDS = (B - 2) // 2

NB = 8
RING = 7
Y_BANK = 7
FIRST, USES = {}, {}
for _seg, _steps in SEGMENTS.items():
    _n = 0
    for _s, _u, _ in _steps:
        assert (_seg, _s, _u) not in FIRST
        FIRST[_seg, _s, _u] = _n
        _n += RESULTS[_s]
    USES[_seg] = [sum(1 for _k in range(_n) if _k % RING == b) for b in range(NB)]

PRE_POLE = 1
PRE_CB = 2 * 2 * B // 4
PRE_A = PRE_POLE + PRE_CB
PRE_W = W_GROUPS
PRE_ALL = PRE_A + PRE_W + 1
CHUNK_BANKS = 4
GEN_ROUNDS = CHUNKS // 2

USED_A = [sum(1 for _k in range(PRE_ALL) if _k % NB == b) for b in range(NB)]
USED_M = [USED_A[b] + (GEN_ROUNDS if b < CHUNK_BANKS else 0) for b in range(NB)]
BEFORE = {"first": USED_M,
          "loop": [USED_M[b] + USES["first"][b] for b in range(NB)],
          "last": [USED_M[b] + USES["first"][b] + ROUNDS * USES["loop"][b] for b in range(NB)]}


class At:

    def __init__(self, seg, r, u, offset, n):
        self.seg, self.r, self.u = seg, r, u
        self.g = n + offset
        self.j = None

    def result(self, step, k=0):
        n = FIRST[self.seg, step, self.u] + k
        b = n % RING
        done = BEFORE[self.seg][b] + n // RING + 1
        return b, (self.r * USES["loop"][b] + done if self.seg == "loop" else done)

    def y_result(self, k):
        return Y_BANK, self.g * 2 + (USED_M[Y_BANK] + k + 1)


def places(seg, r):
    for i, (step, u, offset) in enumerate(SEGMENTS[seg]):
        if seg == "first":
            n = 0
        elif seg == "loop":
            n = r * 2 + (1 if i < len(half(1)) else 2)
        else:
            n = B - 1
        at_ = At(seg, r, u, offset, n)
        if seg == "loop":
            n0 = 1 if i < len(half(1)) else 2
            at_.g = r * 2 + (n0 + offset)
            at_.j = r + (n0 + offset) // 2
        else:
            at_.j = at_.g // 2
        yield step, at_


def mk_vit_tower(nc, t_in, out):
    kd = nc.dram_tensor("generated_tokens", (B * HI, T, LO), f32, kind="Internal").ap()
    ctx = ExitStack()
    with ctx:
        def sb(name, shape, dt=f32):
            return ctx.enter_context(nc.sbuf_tensor(name, shape, dt))

        def sem(name):
            return ctx.enter_context(nc.semaphore(name))

        wt = sb("weightsT", [P, W_BLOCKS * P])
        ident = sb("ident", [P, P])
        w1 = sb("maa_w1", [P, FT, NMIX * MIX])
        w2a = sb("maa_w2a", [P, D])
        w2b = sb("maa_w2b", [MIX, D])
        dw1 = sb("decay_w1", [P, FT, DEC])
        dw2 = sb("decay_w2", [DEC, D])
        qk_bias = sb("qk_bias", [P, 2 * D])
        pj_bias = sb("proj_bias", [P, D])
        lnw = sb("ln_w", [P, D])
        lnb = sb("ln_b", [P, D])
        vec_rows = sb("vec_rows", [24, P])
        vec = sb("vec", [P, 24])
        blockdiag = sb("blockdiag", [P, P])
        above = sb("above", [P, 2, P])
        heads4 = sb("heads4", [P, 4])
        parity = sb("parity", [P, 2])
        ones = sb("ones", [P, T])
        shift = [sb(f"shift{u}", [P, TT]) for u in range(2 * STREAMS)]
        neg_half = sb("neg_half", [P, 2 * NH])
        head_sel = sb("head_sel", [P, 2, 2, HD])
        VEC = {n: i for i, n in enumerate(["norm_w", "norm_b", "v_bias", "mu_r", "mu_k", "maa_x", "maa_w",
                                           "maa_k", "maa_v", "maa_r", "maa_g", "decay"])}

        def vcol(name, ft):
            c = FT * VEC[name] + ft
            return vec[:, c:c + 1]

        def w(name, kt, c0, cn):
            width = next(o for n, o, _ in WEIGHTS if n == name)
            c = W_AT[name] * P + kt * width + c0
            return wt[:, c:c + cn]

        SLOTS = 32
        arena = [sb(f"arena{u}", [P, SLOTS * 512]) for u in range(STREAMS)]
        xT = [sb(f"xT{u}", [P, FT, T + 2]) for u in range(STREAMS)]
        k_in = [sb(f"tokens_in{u}", [P, TT, D]) for u in range(STREAMS)]
        out_sb = [sb(f"out_sb{u}", [P, TT, D]) for u in range(STREAMS)]
        stats = [sb(f"stats{u}", [P, TT, 6]) for u in range(2 * STREAMS)]
        meanvar = [sb(f"meanvar{u}", [P, TT, 2]) for u in range(2 * STREAMS)]
        rstd = [sb(f"rstd{u}", [P, TT]) for u in range(2 * STREAMS)]
        smax = [sb(f"smax{u}", [P, 4]) for u in range(STREAMS)]
        ssum = [sb(f"ssum{u}", [P, 4]) for u in range(STREAMS)]
        gn = [sb(f"gn{u}", [P, 4, TT * NH]) for u in range(STREAMS)]

        def slot(u, s, n=1):
            return arena[u][:, s * 512:(s + n) * 512]

        def two(u, s):
            return slot(u, s).rearrange("p (a b) -> p a b", a=2)

        H, XN, TN, N0, BASE = 0, 1, 29, 30, 31
        HTs, QK, VT, EX, PT, AT_ = 14, 15, 17, 18, 19, 20
        DIFF, XR, XK, RELU, KSQ, TANH, GATED, MID = 21, 22, 23, 24, 25, 26, 27, 28
        DX, XM, TMP, XF, XXX, ZT = 5, 6, (7, 4), 8, 13, 14
        EW, CS, CSB, CF, CB, EFN, EBN = 15, 16, 17, 18, 19, 20, 21
        RF, RB, KF, KB, RFM, RBM, VV, G2 = 22, 23, 24, 25, 26, 28, 30, 31
        THG, KTM, SBD, AB = 3, 13, 14, 5
        YF, YC, SQ, ZN, ZG, ZTs = 5, 6, 7, 8, 9, 10
        HF = 2
        VE = 3
        GW, GB = 1, 2
        THF, SF, HM = 5, 8, 11

        banks = [ctx.enter_context(nc.psum_tensor(f"bank{b}", [P, 512], f32)) for b in range(NB)]

        def bank2(b):
            return banks[b][:, :].rearrange("p (a b) -> p a b", a=2)

        full = [sem(f"bank{b}_full") for b in range(NB)]
        emptied = [sem(f"bank{b}_emptied") for b in range(NB)]
        inputs_in = sem("inputs_in")
        c_in = sem("c_in")
        vec_in = sem("vec_in")
        small_in = sem("small_in")
        weights_in = [sem(f"weights_in_{n}") for n, _, _ in WEIGHTS]
        ident_made = sem("ident_made")
        consts_made = sem("consts_made")
        parity_made = sem("parity_made")
        dequantized = sem("dequantized")
        act_dt = sem("act_dt")
        poles_made = sem("poles_made")
        cb_made = [sem(f"cb_{x}_made") for x in ("re", "im")]
        powers_made = sem("powers_made")
        q_start = sem("q_start")
        hi_made = sem("high_powers_made")
        cross_made = sem("cross_made")
        p_made = sem("p_made")
        k_stored = [sem(f"k_stored{i}") for i in range(2)]
        k_loaded = [sem(f"k_loaded{u}") for u in range(STREAMS)]
        out_free = [sem(f"out_free{u}") for u in range(STREAMS)]
        dve_chain = sem("dve_chain")
        pool_chain = sem("pool_chain")
        main_dve_chain = sem("main_dve_chain")
        main_pool_chain = sem("main_pool_chain")

        NAMES = {}

        def product(name, per_batch=1):
            NAMES[name] = (sem(name), per_batch)
            return NAMES[name][0]

        def at(name, g, k=None):
            s, n = NAMES[name]
            return s, g * n + (n if k is None else k)

        def norm_at(p, n):
            return (STREAMS + p.u, p.j + 1) if n == 4 else (p.u, p.j * 4 + (n + 1))

        var_ready = [sem(f"var_ready{u}") for u in range(2 * STREAMS)]
        rstd_ready = [sem(f"rstd_ready{u}") for u in range(2 * STREAMS)]
        normed = [sem(f"normed{u}") for u in range(2 * STREAMS)]

        for name, n in [("base_ready", 1), ("max_ready", 1),
                        ("diff_ready", 1), ("xr_ready", 1), ("xk_ready", 1), ("ksq_ready", 1),
                        ("xm_ready", 1), ("mixed", NMIX),
                        ("tanh_g", 1), ("cs_ready", 1), ("csb_ready", 1), ("cf_ready", 1), ("cb_ready", 1),
                        ("ef_ready", 1), ("eb_ready", 1), ("rf_ready", 1), ("kf_ready", 1),
                        ("rfm_ready", 1), ("rbm_ready", 1), ("low_copied", 16), ("squared", 1),
                        ("affine_ready", 1),
                        ("gated_ready", 1), ("ve_ready", 1), ("xxx_ready", 1), ("tanh_gate", 3)]:
            product(name, n)

        waits_apart = {e: sem(f"waits_apart_{e}") for e in ("pool", "dve")}

        class Chain:

            def __init__(self, eng, s, per_loop):
                self.eng, self.sem, self.per_loop = eng, s, per_loop
                self.base, self.local, self.seg = 0, 0, "first"

            def link(self, p, ins):
                if p.seg != self.seg:
                    if self.seg == "loop":
                        assert self.local == self.per_loop, self.local
                        self.base += ROUNDS * self.local
                    else:
                        self.base += self.local
                    self.seg, self.local = p.seg, 0
                self.local += 1
                ins.then_inc(self.sem, 1)
                n = self.base + self.local
                self.eng.wait_ge(self.sem, p.r * self.per_loop + n if p.seg == "loop" else n)

        def run(eng, steps):
            for seg in ("first", "loop", "last"):
                if seg == "loop":
                    with eng.Fori(0, ROUNDS) as r:
                        for step, p in places(seg, r):
                            if step in steps:
                                steps[step](p)
                else:
                    for step, p in places(seg, 0):
                        if step in steps:
                            steps[step](p)

        def apart(eng, name):
            eng.sem_inc(waits_apart[name], 1)

        block = ctx.enter_context(nc.Block())

        flat = {0: 0, 1: 0}

        def carve(a, n):
            c = flat[a]
            flat[a] += n
            assert flat[a] <= SLOTS * 512
            return arena[a][:, c:c + n]

        nat = {}
        for name, o, i in WEIGHTS:
            nat[name] = carve(0, (o // P) * i)
        pole = carve(1, 2 * TT * 2 * NS).rearrange("p (c t d n) -> p c t d n", c=2, t=TT, d=2)
        b_nat = carve(1, TT * NS * 2).rearrange("p (t n c) -> p t n c", t=TT, c=2)
        c_nat = carve(1, B * TT * NS * 2).rearrange("p (b t n c) -> p b t n c", b=B, t=TT, c=2)
        cb_nat = carve(1, 2 * B * TT * 2 * NS).rearrange("p (c b t d n) -> p c b t d n", c=2, b=B, t=TT, d=2)
        cbT = carve(1, 2 * B * T).rearrange("p (c b t) -> p c b t", c=2, b=B)
        zp = carve(1, 8 * 2 * T).rearrange("p (k c t) -> p k c t", k=8, c=2)
        pbuf = cb_nat.rearrange("p c b t d n -> p (c b t d n)")
        pb = [pbuf[:, i * 2048:(i + 1) * 2048].rearrange("p (t b a) -> p t b a", t=TC, b=B) for i in range(2)]
        cross = [x.rearrange("p (t b a) -> p t b a", t=TC, b=B)
                 for x in (c_nat.rearrange("p b t n c -> p (b t n c)"), sb("cross1", [P, TC * B * HI])[:, :])]
        q1 = [carve(0, TC * LO).rearrange("p (t l) -> p t l", t=TC) for _ in range(2)]
        q2 = carve(1, TC * LO).rearrange("p (t l) -> p t l", t=TC)
        tmp1 = carve(0, TC * LO // 2)
        tmp2 = carve(0, TC * LO // 2)
        e1 = [sb(f"high_re{i}", [P, TC * HI])[:, :].rearrange("p (t a) -> p t a", t=TC) for i in range(2)]
        e2 = [carve(a, TC * HI).rearrange("p (t a) -> p t a", t=TC) for a in range(2)]
        etmp = [carve(0, TC * HI // 2) for _ in range(2)] + [k_in[1][:, i, 0:TC * HI // 2] for i in range(2)]
        ks = [carve(0, TC * LO) for _ in range(2)]
        work = [k_in[i // 4][:, :, :].rearrange("p t d -> p (t d)")[:, (i % 4) * P:(i % 4 + 1) * P] for i in range(8)]
        inv_nat, aim_nat = work[6], work[7]
        logdt = sb("log_dt", [P, TT])
        halfdt = sb("half_dt", [P, TT])
        sqt = [k_in[0][:, i, :] for i in range(2)]
        BH = B // 2
        br = b_nat[:, :, :, 0].unsqueeze(1).to_broadcast([P, BH, TT, NS])
        bi = b_nat[:, :, :, 1].unsqueeze(1).to_broadcast([P, BH, TT, NS])

        @block.sync
        def _(sp):
            with nc.allow_non_contiguous_dma(reason="per-token scalars"):
                sp.dma_start(logdt[:, :], t_in["L0_tok_log_dt"].rearrange("(t p) -> p t", p=P)).then_inc(inputs_in, 16)
            sp.dma_start(inv_nat.rearrange("p (t n) -> p t n", t=TT),
                         t_in["L0_tok_inv_A_real"].rearrange("(t p) n -> p t n", p=P)).then_inc(inputs_in, 16)
            sp.dma_start(aim_nat.rearrange("p (t n) -> p t n", t=TT),
                         t_in["L0_tok_A_imag"].rearrange("(t p) n -> p t n", p=P)).then_inc(inputs_in, 16)
            sp.dma_start(b_nat, t_in["L0_tok_B_ri"].rearrange("(t p) n c -> p t n c", p=P)).then_inc(inputs_in, 16)
            for tt in range(TT):
                sp.dma_start(c_nat[:, :, tt].rearrange("p b n c -> p b (n c)"),
                             t_in["x"][:, tt * P:(tt + 1) * P].rearrange("b p n c -> p b (n c)")).then_inc(c_in, 16)
            src = {"qkv": "L0_attn_qkv_w", "proj": "L0_attn_proj_w", "ffn_r": "L0_ffn_W_r", "ffn_k": "L0_ffn_W_k",
                   "ffn_v": "L0_ffn_W_v", "r": "L1_attn_W_r", "k": "L1_attn_W_k", "v": "L1_attn_W_v",
                   "g": "L1_attn_W_g", "o": "L1_attn_W_o", "gate": "L1_ffn_w_gate", "up": "L1_ffn_w_up",
                   "down": "L1_ffn_w_down"}
            for (name, o, i), s in zip(WEIGHTS, weights_in):
                dst = nat[name].bitcast(i32) if name in ("gate", "up", "down") else nat[name]
                sp.dma_start(dst.rearrange("p (o i) -> p o i", i=i),
                             t_in[src[name]].rearrange("(o p) i -> p o i", p=P)).then_inc(s, 16)

            rows = ["L0_attn_norm_w", "L0_attn_norm_b", None, "L0_ffn_mu_r", "L0_ffn_mu_k", "L1_attn_time_maa_x",
                    "L1_attn_time_maa_w", "L1_attn_time_maa_k", "L1_attn_time_maa_v", "L1_attn_time_maa_r",
                    "L1_attn_time_maa_g", "L1_attn_time_decay"]
            for i, name in enumerate(rows):
                if name is None:
                    src = t_in["L0_attn_qkv_b"][2 * D:3 * D]
                elif name.startswith("L1"):
                    src = t_in[name][0, 0, :]
                else:
                    src = t_in[name]
                sp.dma_start(vec_rows[FT * i:FT * (i + 1), :], src.rearrange("(t p) -> t p", p=P)).then_inc(vec_in, 16)
            sp.dma_start(w1[:, :, :], t_in["L1_attn_time_maa_w1"].rearrange("(t p) m -> p t m", p=P)
                         ).then_inc(small_in, 16)
            w2 = t_in["L1_attn_time_maa_w2"].rearrange("f m d -> (f m) d")
            sp.dma_start(w2a[:, :], w2[0:P, :]).then_inc(small_in, 16)
            sp.dma_start(w2b[:, :], w2[P:P + MIX, :]).then_inc(small_in, 16)
            sp.dma_start(dw1[:, :, :], t_in["L1_attn_time_decay_w1"].rearrange("(t p) m -> p t m", p=P)
                         ).then_inc(small_in, 16)
            sp.dma_start(dw2[:, :], t_in["L1_attn_time_decay_w2"]).then_inc(small_in, 16)
            for dst, src in ((qk_bias, t_in["L0_attn_qkv_b"][0:2 * D]), (pj_bias, t_in["L0_attn_proj_b"]),
                             (lnw, t_in["L1_attn_ln_w"]), (lnb, t_in["L1_attn_ln_b"])):
                sp.dma_start(dst[:, :], src.partition_broadcast(P)).then_inc(small_in, 16)

            with sp.Fori(0, GEN_ROUNDS) as r:
                for c in range(2):
                    for b in (2 * c, 2 * c + 1):
                        sp.wait_ge(emptied[b], r + (USED_A[b] + 1))
                    sp.dma_start(kd[:, bass.ds((r * 2 + c) * TC, TC), :],
                                 ks[c][0:B * HI, :].rearrange("p (t l) -> p t l", t=TC)).then_inc(k_stored[c], 16)
            for c in range(2):
                sp.wait_ge(k_stored[c], 16 * (GEN_ROUNDS + 1))

            def load(g, u):
                for tt in range(TT):
                    sp.dma_start(k_in[u][:, tt, :].rearrange("p (a l) -> p a l", a=HI),
                                 kd[bass.ds(g * HI, HI), tt * P:(tt + 1) * P, :].rearrange("a p l -> p a l"))\
                      .then_inc(k_loaded[u], 16)

            def load_after(p):
                sp.wait_ge(*at("base_ready", p.g))
                load(p.g + 2, p.u)

            def store(p):
                b, v = p.result("down")
                sp.wait_ge(emptied[b], v)
                sp.dma_start(out[bass.ds(p.g, 1), :, :].rearrange("o (t p) f -> p (o t) f", p=P), out_sb[p.u][:, :, :])\
                  .then_inc(out_free[p.u], 16)

            for u in range(STREAMS):
                load(u, u)
            for step, p in places("first", 0):
                if step == "base":
                    load_after(p)
            with sp.Fori(0, ROUNDS - 1) as r:
                for step, p in places("loop", r):
                    if step == "base":
                        load_after(p)
                    if step == "down":
                        store(p)
            for step, p in places("loop", ROUNDS - 1):
                if step == "down":
                    store(p)
            for step, p in places("last", 0):
                if step == "down":
                    store(p)
            for u in range(STREAMS):
                sp.wait_ge(out_free[u], 16 * (B // STREAMS + 1))

        @block.gpsimd
        def _(pool):
            pl = nc.gpsimd
            chain = [0]

            def link(ins):
                chain[0] += 1
                ins.then_inc(pool_chain, 1)
                pool.wait_ge(pool_chain, chain[0])

            link(pl.memset(ident[:, :], 0.0))
            pl.affine_select(out=ident[:, :], in_=ident[:, :], compare_op=ALU.not_equal, fill=1.0, base=0,
                             pattern=[[-1, P]], channel_multiplier=1).then_inc(ident_made, 1)
            link(pl.memset(blockdiag[:, :], 1.0))
            bdv = blockdiag[:, :]
            link(pl.affine_select(out=bdv, in_=bdv, compare_op=ALU.is_ge, fill=0.0, base=0,
                                  pattern=[[-HD, P // HD], [0, HD]], channel_multiplier=1))
            link(pl.affine_select(out=bdv, in_=bdv, compare_op=ALU.is_ge, fill=0.0, base=HD - 1,
                                  pattern=[[HD, P // HD], [0, HD]], channel_multiplier=-1))
            link(pl.memset(above[:, :, :], 1.0))
            link(pl.affine_select(out=above[:, :, :], in_=above[:, :, :], compare_op=ALU.is_gt, fill=0.0, base=0,
                                  pattern=[[0, 2], [-1, P]], channel_multiplier=1))
            link(pl.memset(heads4[:, :], 1.0))
            link(pl.affine_select(out=heads4[:, :], in_=heads4[:, :], compare_op=ALU.is_ge, fill=0.0, base=0,
                                  pattern=[[-2 * HD, 4]], channel_multiplier=1))
            link(pl.affine_select(out=heads4[:, :], in_=heads4[:, :], compare_op=ALU.is_ge, fill=0.0, base=HD - 1,
                                  pattern=[[2 * HD, 4]], channel_multiplier=-1))
            link(pl.memset(ones[:, :], 1.0))
            link(pl.memset(head_sel[:, :, :, :], 0.0))
            link(pl.memset(head_sel[:, 0, 0, :], 1.0))
            link(pl.memset(head_sel[:, 1, 1, :], 1.0))
            for u in range(STREAMS):
                link(pl.memset(xT[u][:, :, :], 0.0))
            pl.memset(neg_half[:, :], -0.5).then_inc(consts_made, 1)
            pool.wait_ge(inputs_in, 64)
            pool.wait_ge(c_in, 32)
            v_ = [x[:, 0:512].rearrange("p (b t n) -> p b t n", b=BH, t=TT) for x in ks]
            for b0 in range(0, B, BH):
                pl.tensor_tensor(v_[0], c_nat[:, b0:b0 + BH, :, :, 0], bi, ALU.mult)
                link(pl.tensor_tensor(v_[1], c_nat[:, b0:b0 + BH, :, :, 1], br, ALU.mult))
                for d in range(2):
                    last = pl.tensor_tensor(cb_nat[:, 1, b0:b0 + BH, :, d, :], v_[0], v_[1], ALU.add)
                if b0 == 0:
                    link(last)
            last.then_inc(cb_made[1], 1)
            pool.wait_ge(cb_made[1], 1)
            for q in (q1[0], q1[1], q2):
                link(pl.memset(q[:, :, 0:1], 0.0))
            for q in (e1[0], e1[1], e2[0], e2[1]):
                link(pl.memset(q[:, :, 0:1], 0.0))
            for q in q1:
                link(pl.memset(q[0:NS, :, 0:1], 2.0))
            link(pl.memset(q2[NS:P, :, 0:1], 2.0))
            for q in e1:
                link(pl.memset(q[0:NS, :, 0:1], 1.0))
            for q in e2:
                link(pl.memset(q[NS:P, :, 0:1], 1.0))
            pl.memset(ks[0], 0.0).then_inc(k_stored[0], 16)
            pl.memset(ks[1], 0.0).then_inc(k_stored[1], 16)
            for u in range(STREAMS):
                pl.memset(out_sb[u][:, :, :], 0.0).then_inc(out_free[u], 16)
            link(pl.memset(etmp[0], 0.0))
            pl.memset(etmp[1], 0.0).then_inc(q_start, 1)
            pool.wait_ge(q_start, 1)

            pool.wait_ge(powers_made, 1)
            for c in range(2 * B * TT // 4):
                n = PRE_POLE + c
                pool.wait_ge(emptied[n % NB], n // NB + 1)
            gen_base = chain[0]
            GEN_LINKS = 2 * 5
            with pool.Fori(0, GEN_ROUNDS) as r:
                local = [0]

                def glink(ins):
                    local[0] += 1
                    ins.then_inc(pool_chain, 1)
                    pool.wait_ge(pool_chain, r * GEN_LINKS + (gen_base + local[0]))
                    apart(pool, "pool")

                for c in range(2):
                    t0 = (r * 2 + c) * TC
                    pool.wait_ge(p_made, (r * 2 + c) + 1)
                    apart(pool, "pool")
                    for lv, m in enumerate((1, 2, 4)):
                        zr = zp[:, 5 + lv, 0, bass.ds(t0, TC)].unsqueeze(2).to_broadcast([P, TC, m])
                        zi = zp[:, 5 + lv, 1, bass.ds(t0, TC)].unsqueeze(2).to_broadcast([P, TC, m])
                        ta, tb, tc_, td = (x[:, 0:TC * m].rearrange("p (t a) -> p t a", t=TC) for x in etmp)
                        pl.tensor_tensor(ta, e1[c][:, :, 0:m], zr, ALU.mult)
                        pl.tensor_tensor(tb, e2[c][:, :, 0:m], zi, ALU.mult)
                        pl.tensor_tensor(tc_, e2[c][:, :, 0:m], zr, ALU.mult)
                        glink(pl.tensor_tensor(td, e1[c][:, :, 0:m], zi, ALU.mult))
                        pl.tensor_tensor(e1[c][:, :, m:2 * m], ta, tb, ALU.add)
                        last = pl.tensor_tensor(e2[c][:, :, m:2 * m], tc_, td, ALU.subtract)
                        if lv < 2:
                            glink(last)
                        else:
                            last.then_inc(hi_made, 1)
                            pool.wait_ge(hi_made, (r * 2 + c) + 1)
                    for b in (2 * c, 2 * c + 1):
                        pool.wait_ge(full[b], r + USED_A[b])
                    apart(pool, "pool")
                    pl.tensor_tensor(cross[c], cbT[:, 1, :, bass.ds(t0, TC)].rearrange("p b t -> p t b").unsqueeze(3)
                                     .to_broadcast([P, TC, B, HI]),
                                     e2[c].unsqueeze(2).to_broadcast([P, TC, B, HI]), ALU.mult).then_inc(cross_made, 1)
                assert local[0] == GEN_LINKS, local[0]
            pool.wait_ge(weights_in[0], 16)

            for n in range(PRE_ALL):
                pool.wait_ge(emptied[n % NB], n // NB + 1)
            chain_ = Chain(pool, main_pool_chain, 2 * (5 * 2 + 1))

            def rstd_of(p, n):
                u, v = norm_at(p, n)
                pool.wait_ge(var_ready[u], v)
                apart(pool, "pool")
                pl.tensor_scalar(shift[u][:, :], meanvar[u][:, :, 0], -1.0, 1.0, ALU.mult, ALU.mult)
                chain_.link(p, pl.tensor_scalar(rstd[u][:, :], meanvar[u][:, :, 1], LN_EPS, 1.0, ALU.add, ALU.mult))
                chain_.link(p, pl.tensor_tensor(rstd[u][:, :], rstd[u][:, :], neg_half[:, 0:TT], ALU.pow))
                pl.tensor_tensor(shift[u][:, :], shift[u][:, :], rstd[u][:, :], ALU.mult).then_inc(rstd_ready[u], 1)

            def norm0(p):
                rstd_of(p, 0)

            def norm1(p):
                rstd_of(p, 1)

            def base(p):
                u = p.u
                pool.wait_ge(normed[norm_at(p, 0)[0]], norm_at(p, 0)[1])
                chain_.link(p, pl.tensor_tensor(two(u, BASE), k_in[u][:, :, :], two(u, TN), ALU.add))
                pl.tensor_tensor(two(u, BASE), two(u, BASE), pj_bias[:, :].unsqueeze(1).to_broadcast([P, TT, D]),
                                 ALU.add).then_inc(at("base_ready", p.g)[0], 1)

            def attn_out(p):
                rstd_of(p, 2)

            def xT0(p):
                b, v = p.result("xT0")
                pool.wait_ge(emptied[b], v)
                pl.tensor_tensor(two(p.u, DIFF), xT[p.u][:, :, 1:T + 1], xT[p.u][:, :, 0:T], ALU.subtract)\
                  .then_inc(at("diff_ready", p.g)[0], 1)

            def ffn_v(p):
                rstd_of(p, 3)

            def mix(step):
                def f_(p):
                    u = p.u
                    for i, f in enumerate(MIXES[step]):
                        b, v = p.result(step, i)
                        pool.wait_ge(emptied[b], v)
                        pl.tensor_tensor(two(u, XF + f), two(u, TMP[f % 2]), xT[u][:, :, 1:T + 1], ALU.add)\
                          .then_inc(at("mixed", p.g)[0], 1)
                return f_

            def decay(p):
                pool.wait_ge(*at("cs_ready", p.g))
                pl.tensor_tensor(two(p.u, CSB), two(p.u, CS), two(p.u, EW), ALU.add)\
                  .then_inc(at("csb_ready", p.g)[0], 1)

            def factors(p):
                u = p.u
                b, v = p.result("query")
                pool.wait_ge(emptied[b], v)
                apart(pool, "pool")
                for e in range(2):
                    last = pl.tensor_scalar(
                        slot(u, RBM, 2).rearrange("p (d j e i) -> p d j e i", d=FT, j=TT, e=2)[:, :, :, e, :],
                        slot(u, RB).rearrange("p (d j i) -> p d j i", d=FT, j=TT),
                        parity[:, e:e + 1], 1.0, ALU.mult, ALU.mult)
                last.then_inc(at("rbm_ready", p.g)[0], 1)

            def values(p):
                u = p.u
                b, v = p.result("gate")
                pool.wait_ge(emptied[b], v)
                for dst, row in ((GW, lnw), (GB, lnb)):
                    last = pl.tensor_tensor(two(u, dst), two(u, G2), row[:, :].unsqueeze(1).to_broadcast([P, TT, D]),
                                            ALU.mult)
                last.then_inc(at("affine_ready", p.g)[0], 1)
                b, v = p.result("value")
                pool.wait_ge(emptied[b], v)
                pl.tensor_tensor(slot(u, VE, 2).rearrange("p (h e d) -> p h e d", h=TT * NH // 2, e=2),
                                 slot(u, VV).rearrange("p (h d) -> p h d", h=TT * NH // 2).unsqueeze(2)
                                 .to_broadcast([P, TT * NH // 2, 2, 2 * HD]),
                                 head_sel[:, :, :, :].rearrange("p e f d -> p e (f d)").unsqueeze(1)
                                 .to_broadcast([P, TT * NH // 2, 2, 2 * HD]), ALU.mult)\
                  .then_inc(at("ve_ready", p.g)[0], 1)

            def mix_out(p):
                rstd_of(p, 4)

            run(pool, {"norm0": norm0, "norm1": norm1, "base": base, "attn_out": attn_out, "xT0": xT0, "ffn_v": ffn_v,
                       "mixA": mix("mixA"), "mixB": mix("mixB"), "decay": decay, "values": values, "factors": factors,
                       "mix_out": mix_out})

        @block.scalar
        def _(act):
            ac = nc.scalar
            act.wait_ge(inputs_in, 64)
            ac.activation(halfdt[:, :], logdt[:, :], ACT.Exp).then_inc(act_dt, 1)
            ac.activation(work[0], inv_nat, ACT.Exp).then_inc(act_dt, 1)

            def copy_out(dst, b, v, src=None):
                act.wait_ge(full[b], v)
                ac.activation(dst, banks[b][:, :] if src is None else src, ACT.Copy).then_inc(emptied[b], 1)

            n = 0
            copy_out(zp[:, 0].rearrange("p c t -> p (c t)"), n % NB, n // NB + 1)
            for k in range(PRE_CB):
                n = PRE_POLE + k
                dst = (k + PRE_CB // 2) % PRE_CB
                copy_out(cbT.rearrange("p c b t -> p (c b t)")[:, dst * 512:(dst + 1) * 512], n % NB, n // NB + 1)
            for k in range(W_GROUPS):
                n = PRE_A + k
                copy_out(wt[:, k * 512:(k + 1) * 512], n % NB, n // NB + 1)
            n = PRE_ALL - 1
            act.wait_ge(full[n % NB], n // NB + 1)
            ac.activation(vec[:, :], banks[n % NB][:, 0:24], ACT.Copy).then_inc(emptied[n % NB], 1)
            with act.Fori(0, GEN_ROUNDS) as r:
                for c in range(2):
                    act.wait_ge(k_stored[c], r * 16 + 16)
                    for h in range(2):
                        b = 2 * c + h
                        act.wait_ge(full[b], r + (USED_A[b] + 1))
                        ac.activation(ks[c][0:B * HI, h * 512:(h + 1) * 512], banks[b][0:B * HI, :], ACT.Copy)\
                          .then_inc(emptied[b], 1)

            def normed_by(n, src, dst):
                def f(p):
                    k, v = norm_at(p, n)
                    act.wait_ge(rstd_ready[k], v)
                    x = k_in[p.u][:, :, :] if src is None else two(p.u, src)
                    for tt in range(TT):
                        last = ac.activation(two(p.u, dst)[:, tt, :], x[:, tt, :], ACT.Identity,
                                             bias=shift[k][:, tt:tt + 1], scale=rstd[k][:, tt:tt + 1])
                    last.then_inc(normed[k], 1)
                return f

            def transposed(step):
                def f(p):
                    b, v = p.result(step)
                    act.wait_ge(full[b], v)
                    ac.activation(xT[p.u][:, :, 1:T + 1], bank2(b), ACT.Copy).then_inc(emptied[b], 1)
                return f

            def copied(step, dst, k=0):
                def f(p):
                    b, v = p.result(step, k)
                    copy_out(slot(p.u, dst), b, v)
                return f

            def affine(p, dst, step, k, func, bias, scale=None):
                b, v = p.result(step, k)
                act.wait_ge(full[b], v)
                for ft in range(FT):
                    last = ac.activation(two(p.u, dst)[:, ft, :], bank2(b)[:, ft, :], func, bias=vcol(bias, ft),
                                         scale=1.0 if scale is None else vcol(scale, ft))
                last.then_inc(emptied[b], 1)

            def scores(p):
                u = p.u
                b, v = p.result("scores")
                act.wait_ge(*at("max_ready", p.g))
                for qt in range(FT):
                    last = ac.activation(two(u, EX)[:, qt, :], bank2(b)[:, qt, :], ACT.Exp,
                                         bias=smax[u][:, 2 + qt:3 + qt], scale=QK_SCALE,
                                         accum_out=ssum[u][:, qt:qt + 1])
                last.then_inc(emptied[b], 1)

            def ffn_kr(p):
                u = p.u
                b, v = p.result("ffn_kr", 0)
                act.wait_ge(full[b], v)
                ac.activation(slot(u, RELU), banks[b][:, :], ACT.Relu).then_inc(emptied[b], 1)
                act.wait_ge(emptied[b], v)
                ac.activation(slot(u, KSQ), slot(u, RELU), ACT.Square).then_inc(at("ksq_ready", p.g)[0], 1)
                b, v = p.result("ffn_kr", 1)
                act.wait_ge(full[b], v)
                ac.activation(slot(u, TANH), banks[b][:, :], ACT.Tanh, scale=0.5).then_inc(emptied[b], 1)

            def lowrank(p):
                b, v = p.result("lowrank")
                act.wait_ge(full[b], v)
                ac.activation(slot(p.u, XXX)[:, 0:T], banks[b][:, 0:T], ACT.Tanh)
                ac.activation(slot(p.u, XXX)[0:MIX, T:2 * T], banks[b][0:MIX, T:2 * T], ACT.Tanh)\
                  .then_inc(emptied[b], 1)
                act.wait_ge(emptied[b], v)
                act.sem_inc(at("xxx_ready", p.g)[0], 1)

            def low(p):
                b, v = p.result("low")
                act.wait_ge(full[b], v)
                ac.activation(slot(p.u, ZT)[0:DEC, 0:T], banks[b][0:DEC, 0:T], ACT.Tanh).then_inc(emptied[b], 1)

            def gate(p):
                b, v = p.result("gate")
                act.wait_ge(full[b], v)
                ac.activation(slot(p.u, THG), banks[b][:, :], ACT.Tanh, scale=0.5).then_inc(at("tanh_g", p.g)[0], 1)

            def factors(p):
                u, g = p.u, p.g
                act.wait_ge(*at("cf_ready", g))
                ac.activation(slot(u, EFN), slot(u, CF), ACT.Exp, scale=-1.0)
                ac.activation(slot(u, CF), slot(u, CF), ACT.Exp).then_inc(at("ef_ready", g)[0], 1)
                act.wait_ge(*at("cb_ready", g))
                ac.activation(slot(u, EBN), slot(u, CB), ACT.Exp, scale=-1.0)
                ac.activation(slot(u, CB), slot(u, CB), ACT.Exp).then_inc(at("eb_ready", g)[0], 1)
                act.wait_ge(*at("rf_ready", g))
                for e in range(2):
                    last = ac.activation(
                        slot(u, RFM, 2).rearrange("p (d j e i) -> p d j e i", d=FT, j=TT, e=2)[:, :, :, e, :],
                        slot(u, RF).rearrange("p (d j i) -> p d j i", d=FT, j=TT), ACT.Copy,
                        scale=parity[:, e:e + 1])
                last.then_inc(at("rfm_ready", g)[0], 1)

            def blocks(c):
                def f(p):
                    for i in range(2):
                        k = 2 * c + i
                        b, v = p.result(f"blocks{c}", i)
                        act.wait_ge(full[b], v)
                        ac.activation(slot(p.u, AB, 8)[:, k * 256:(k + 1) * 256], banks[b][:, 0:256], ACT.Copy)\
                          .then_inc(at("low_copied", p.g)[0], 1)
                return f

            def y_out(p):
                b, v = p.y_result(0)
                copy_out(slot(p.u, YF), b, v)

            def y_tokens(p):
                b, v = p.y_result(1)
                act.wait_ge(emptied[b], v)
                ac.activation(slot(p.u, SQ), slot(p.u, YC), ACT.Square).then_inc(at("squared", p.g)[0], 1)

            def gate_up(c):
                def f(p):
                    b, v = p.result(f"gate_up{c}", 0)
                    act.wait_ge(full[b], v)
                    ac.activation(slot(p.u, THF + c), banks[b][:, :], ACT.Tanh, scale=0.5)\
                      .then_inc(at("tanh_gate", p.g)[0], 1)
                return f

            run(act, {"apply0": normed_by(0, None, TN), "apply1": normed_by(1, TN, N0),
                      "apply2": normed_by(2, MID, TN), "apply3": normed_by(3, H, XN), "apply4": normed_by(4, HF, XN),
                      "hT": lambda p: affine(p, HTs, "hT", 0, ACT.Identity, "norm_b", "norm_w"),
                      "qkv": lambda p: affine(p, VT, "qkv", 2, ACT.Identity, "v_bias"), "scores": scores,
                      "probsT": copied("probsT", PT), "xT0": transposed("xT0"), "ffn_kr": ffn_kr,
                      "xT1": transposed("xT1"), "lowrank": lowrank, "low": low, "value": copied("value", VV),
                      "gate": gate, "keys": copied("keys", KTM),
                      "decay": lambda p: affine(p, EW, "decay", 0, ACT.Exp, "decay"), "factors": factors,
                      "blocks0": blocks(0), "blocks1": blocks(1), "blocks2": blocks(2), "blocks3": blocks(3),
                      "blocks4": blocks(4), "blocks5": blocks(5), "blocks6": blocks(6), "blocks7": blocks(7),
                      "y3": y_out, "yT": y_tokens, "gatedT": copied("gatedT", ZTs), "xT2": transposed("xT2"),
                      "gate_up0": gate_up(0), "gate_up1": gate_up(1), "gate_up2": gate_up(2)})

        @block.vector
        def _(dve):
            vc = nc.vector
            chain = [0]

            def link(ins):
                chain[0] += 1
                ins.then_inc(dve_chain, 1)
                dve.wait_ge(dve_chain, chain[0])

            dve.wait_ge(act_dt, 2)
            link(vc.tensor_scalar(halfdt[:, :], halfdt[:, :], 0.5, None, ALU.mult))
            hx, hy, sqx, sqy, den, num = work[0], work[1], work[2], work[3], work[4], work[5]
            for tt in range(TT):
                s = slice(tt * NS, (tt + 1) * NS)
                link(vc.tensor_scalar(hx[:, s], hx[:, s], halfdt[:, tt:tt + 1], -1.0, ALU.mult, ALU.mult))
                link(vc.tensor_scalar(hy[:, s], aim_nat[:, s], halfdt[:, tt:tt + 1], None, ALU.mult))
            link(vc.tensor_tensor(sqx, hx, hx, ALU.mult))
            link(vc.tensor_tensor(sqy, hy, hy, ALU.mult))
            link(vc.tensor_scalar(den, hx, -1.0, 1.0, ALU.mult, ALU.add))
            link(vc.tensor_tensor(den, den, den, ALU.mult))
            link(vc.tensor_tensor(den, den, sqy, ALU.add))
            link(vc.reciprocal(den, den))
            link(vc.tensor_tensor(num, sqx, sqy, ALU.add))
            link(vc.tensor_scalar(num, num, -1.0, 1.0, ALU.mult, ALU.add))

            def dup(x):
                return x.rearrange("p (t n) -> p t n", t=TT).unsqueeze(2).to_broadcast([P, TT, 2, NS])
            link(vc.tensor_tensor(pole[:, 0], dup(num), dup(den), ALU.mult))
            link(vc.tensor_scalar(hy, hy, 2.0, None, ALU.mult))
            vc.tensor_tensor(pole[:, 1], dup(hy), dup(den), ALU.mult).then_inc(poles_made, 1)

            dve.wait_ge(c_in, 32)
            v_ = [x.rearrange("p (b t n) -> p b t n", b=BH, t=TT) for x in (tmp1, tmp2)]
            for b0 in range(0, B, BH):
                vc.tensor_tensor(v_[0], c_nat[:, b0:b0 + BH, :, :, 0], br, ALU.mult)
                link(vc.tensor_tensor(v_[1], c_nat[:, b0:b0 + BH, :, :, 1], bi, ALU.mult))
                for d in range(2):
                    last = vc.tensor_tensor(cb_nat[:, 0, b0:b0 + BH, :, d, :], v_[0], v_[1], ALU.subtract)
                if b0 == 0:
                    link(last)
            last.then_inc(cb_made[0], 1)
            dve.wait_ge(cb_made[0], 1)

            n = 0
            dve.wait_ge(emptied[n % NB], n // NB + 1)
            for k in range(7):
                zr, zi = zp[:, k, 0, :], zp[:, k, 1, :]
                vc.tensor_tensor(sqt[0], zr, zi, ALU.subtract)
                vc.scalar_tensor_tensor(out=zp[:, k + 1, 1, :], in0=zr, scalar=2.0, in1=zi, op0=ALU.mult, op1=ALU.mult)
                link(vc.tensor_tensor(sqt[1], zr, zi, ALU.add))
                last = vc.tensor_tensor(zp[:, k + 1, 0, :], sqt[0], sqt[1], ALU.mult)
                if k < 6:
                    link(last)
                else:
                    last.then_inc(powers_made, 1)
                    dve.wait_ge(powers_made, 1)

            dve.wait_ge(consts_made, 1)
            link(vc.reduce_sum(parity[:, 0:1], heads4[:, :], AX.X))
            vc.tensor_scalar(parity[:, 1:2], parity[:, 0:1], -1.0, 1.0, ALU.mult, ALU.add).then_inc(parity_made, 1)
            for k, name in enumerate(("gate", "up", "down")):
                dve.wait_ge(weights_in[10 + k], 16)
                vc.tensor_scalar(nat[name], nat[name].bitcast(i32), DEQUANT, None, ALU.mult).then_inc(dequantized, 1)

            dve.wait_ge(q_start, 1)
            for k in range(PRE_CB):
                n = PRE_POLE + k
                dve.wait_ge(emptied[n % NB], n // NB + 1)
            vc.memset(tmp1, 0.0).then_inc(p_made, 1)
            vc.memset(tmp2, 0.0).then_inc(p_made, 1)
            dve.wait_ge(p_made, 2)
            gen_base = chain[0]
            GEN_LINKS = 2 * (1 + 4 * 2)
            with dve.Fori(0, GEN_ROUNDS) as r:
                local = [0]

                def glink(ins):
                    local[0] += 1
                    ins.then_inc(dve_chain, 1)
                    dve.wait_ge(dve_chain, r * GEN_LINKS + (gen_base + local[0]))

                for c in range(2):
                    t0 = (r * 2 + c) * TC
                    for b in (2 * c, 2 * c + 1):
                        dve.wait_ge(full[b], r + USED_A[b])
                    for q, rows, part, factor in ((q1[c], slice(0, NS), 0, 2.0), (q1[c], slice(NS, P), 1, -2.0),
                                                  (q2, slice(0, NS), 1, 2.0), (q2, slice(NS, P), 0, 2.0)):
                        last = vc.tensor_scalar(q[rows, :, 1], zp[rows, 0, part, bass.ds(t0, TC)], factor, None,
                                                ALU.mult)
                    glink(last)
                    for lv in range(1, 5):
                        m = 1 << lv
                        zr = zp[:, lv, 0, bass.ds(t0, TC)].unsqueeze(2).to_broadcast([P, TC, m])
                        zi = zp[:, lv, 1, bass.ds(t0, TC)].unsqueeze(2).to_broadcast([P, TC, m])
                        n = TC * m
                        ta, tb = (x[:, 0:n].rearrange("p (t a) -> p t a", t=TC) for x in (tmp1, tmp2))
                        vc.tensor_tensor(ta, q1[c][:, :, 0:m], zr, ALU.mult)
                        last = vc.tensor_tensor(tb, q2[:, :, 0:m], zi, ALU.mult)
                        if lv < 4:
                            tc_, td = (x[:, n:2 * n].rearrange("p (t a) -> p t a", t=TC) for x in (tmp1, tmp2))
                            vc.tensor_tensor(tc_, q2[:, :, 0:m], zr, ALU.mult)
                            last = vc.tensor_tensor(td, q1[c][:, :, 0:m], zi, ALU.mult)
                        glink(last)
                        last = vc.tensor_tensor(q1[c][:, :, m:2 * m], ta, tb, ALU.subtract)
                        if lv < 4:
                            last = vc.tensor_tensor(q2[:, :, m:2 * m], tc_, td, ALU.add)
                        glink(last)
                    dve.wait_ge(hi_made, (r * 2 + c) + 1)
                    vc.tensor_tensor(pb[c], cbT[:, 0, :, bass.ds(t0, TC)].rearrange("p b t -> p t b").unsqueeze(3)
                                     .to_broadcast([P, TC, B, HI]),
                                     e1[c].unsqueeze(2).to_broadcast([P, TC, B, HI]), ALU.mult).then_inc(p_made, 1)
                assert local[0] == GEN_LINKS, local[0]

            for n in range(PRE_ALL):
                dve.wait_ge(emptied[n % NB], n // NB + 1)
            for b in range(NB):
                dve.wait_ge(emptied[b], USED_M[b])
            dve.wait_ge(small_in, 16 * 9)
            chain_ = Chain(dve, main_dve_chain, 2 * 30)

            def moments(p, n, x):
                k, v = norm_at(p, n)
                vc.bn_stats(stats[k][:, 0, :], x[:, 0, :])
                chain_.link(p, vc.bn_stats(stats[k][:, 1, :], x[:, 1, :]))
                apart(dve, "dve")
                vc.bn_aggr(meanvar[k][:, 0, :], stats[k][:, 0, :])
                vc.bn_aggr(meanvar[k][:, 1, :], stats[k][:, 1, :]).then_inc(var_ready[k], 1)

            def norm0(p):
                dve.wait_ge(k_loaded[p.u], p.j * 32 + 32)
                moments(p, 0, k_in[p.u][:, :, :])

            def norm1(p):
                dve.wait_ge(normed[norm_at(p, 0)[0]], norm_at(p, 0)[1])
                moments(p, 1, two(p.u, TN))

            def qkv(p):
                for tt in range(TT):
                    b, v = p.result("qkv", tt)
                    dve.wait_ge(full[b], v)
                    vc.tensor_tensor(slot(p.u, QK + tt), banks[b][:, :], qk_bias[:, :], ALU.add).then_inc(emptied[b], 1)

            def scores(p):
                u = p.u
                b, v = p.result("scores")
                dve.wait_ge(full[b], v)
                chain_.link(p, vc.reduce_max(smax[u][:, 0:2], bank2(b), AX.X))
                vc.tensor_scalar(smax[u][:, 2:4], smax[u][:, 0:2], -QK_SCALE, None, ALU.mult)\
                  .then_inc(at("max_ready", p.g)[0], 1)

            def attT(p):
                u = p.u
                b, v = p.result("scores")
                dve.wait_ge(emptied[b], v)
                chain_.link(p, vc.reciprocal(ssum[u][:, 2:4], ssum[u][:, 0:2]))
                b, v = p.result("attT")
                dve.wait_ge(full[b], v)
                for qt in range(FT):
                    last = vc.tensor_scalar(two(u, AT_)[:, qt, :], bank2(b)[:, qt, :], ssum[u][:, 2 + qt:3 + qt],
                                            None, ALU.mult)
                last.then_inc(emptied[b], 1)

            def attn_out(p):
                u = p.u
                b, v = p.result("attn_out")
                dve.wait_ge(full[b], v)
                dve.wait_ge(*at("base_ready", p.g))
                vc.tensor_tensor(slot(u, MID), banks[b][:, :], slot(u, BASE), ALU.add).then_inc(emptied[b], 1)
                dve.wait_ge(emptied[b], v)
                moments(p, 2, two(u, MID))

            def xT0(p):
                u = p.u
                dve.wait_ge(*at("diff_ready", p.g))
                for name, dst, done in (("mu_k", XK, "xk_ready"), ("mu_r", XR, "xr_ready")):
                    for ft in range(FT):
                        last = vc.scalar_tensor_tensor(out=two(u, dst)[:, ft, :], in0=two(u, DIFF)[:, ft, :],
                                                       scalar=vcol(name, ft), in1=xT[u][:, ft, 0:T],
                                                       op0=ALU.mult, op1=ALU.add)
                    last.then_inc(at(done, p.g)[0], 1)

            def ffn_v(p):
                u = p.u
                bt, vt = p.result("ffn_kr", 1)
                dve.wait_ge(emptied[bt], vt)
                b, v = p.result("ffn_v")
                dve.wait_ge(full[b], v)
                vc.scalar_tensor_tensor(out=slot(u, GATED), in0=slot(u, TANH), scalar=1.0, in1=banks[b][:, :],
                                        op0=ALU.add, op1=ALU.mult).then_inc(emptied[b], 1)
                dve.wait_ge(emptied[b], v)
                chain_.link(p, vc.scalar_tensor_tensor(out=slot(u, H), in0=slot(u, GATED), scalar=0.5, in1=slot(u, MID),
                                                       op0=ALU.mult, op1=ALU.add))
                moments(p, 3, two(u, H))

            def xT1(p):
                u = p.u
                b, v = p.result("xT1")
                dve.wait_ge(emptied[b], v)
                chain_.link(p, vc.tensor_tensor(two(u, TMP[0]), xT[u][:, :, 0:T], xT[u][:, :, 2:T + 2], ALU.add))
                chain_.link(p, vc.scalar_tensor_tensor(out=two(u, DX), in0=two(u, TMP[0]), scalar=0.5,
                                                       in1=xT[u][:, :, 1:T + 1], op0=ALU.mult, op1=ALU.subtract))
                for ft in range(FT):
                    last = vc.scalar_tensor_tensor(out=two(u, XM)[:, ft, :], in0=two(u, DX)[:, ft, :],
                                                   scalar=vcol("maa_x", ft), in1=xT[u][:, ft, 1:T + 1],
                                                   op0=ALU.mult, op1=ALU.add)
                last.then_inc(at("xm_ready", p.g)[0], 1)

            def mix(step):
                def f_(p):
                    u = p.u
                    for i, f in enumerate(MIXES[step]):
                        name = ("maa_w", "maa_k", "maa_v", "maa_r", "maa_g")[f]
                        b, v = p.result(step, i)
                        dve.wait_ge(full[b], v)
                        if f >= 2:
                            dve.wait_ge(*at("mixed", p.g, f - 1))
                        for ft in range(FT):
                            last = vc.scalar_tensor_tensor(out=two(u, TMP[f % 2])[:, ft, :], in0=bank2(b)[:, ft, :],
                                                           scalar=vcol(name, ft), in1=two(u, DX)[:, ft, :],
                                                           op0=ALU.add, op1=ALU.mult)
                        last.then_inc(emptied[b], 1)
                return f_

            def gate(p):
                b, v = p.result("gate")
                dve.wait_ge(*at("tanh_g", p.g))
                vc.scalar_tensor_tensor(out=slot(p.u, G2), in0=slot(p.u, THG), scalar=1.0, in1=banks[b][:, :],
                                        op0=ALU.add, op1=ALU.mult).then_inc(emptied[b], 1)

            def decay(p):
                u, g = p.u, p.g
                b, v = p.result("decay")
                dve.wait_ge(emptied[b], v)
                for ft in range(FT):
                    last = vc.tensor_tensor_scan(two(u, CS)[:, ft, :], ones[:, :], two(u, EW)[:, ft, :], 0.0,
                                                 ALU.mult, ALU.subtract)
                last.then_inc(at("cs_ready", g)[0], 1)
                dve.wait_ge(*at("cs_ready", g))
                for src, dst, first, done in ((CS, CF, None, "cf_ready"), (CSB, CB, "csb_ready", "cb_ready")):
                    if first:
                        dve.wait_ge(*at(first, g))
                    for ft in range(FT):
                        last = vc.tensor_scalar(two(u, dst)[:, ft, :], two(u, src)[:, ft, :],
                                                two(u, src)[:, ft, T // 2:T // 2 + 1], CLIP, ALU.subtract, ALU.min)
                    chain_.link(p, last)
                    vc.tensor_scalar(slot(u, dst), slot(u, dst), -CLIP, None, ALU.max).then_inc(at(done, g)[0], 1)

            def factors(p):
                u, g = p.u, p.g
                br_, vr = p.result("query")
                bk, vk = p.result("key")
                dve.wait_ge(full[bk], vk)
                dve.wait_ge(full[br_], vr)
                dve.wait_ge(*at("ef_ready", g))
                vc.tensor_tensor(slot(u, RF), banks[br_][:, :], slot(u, CF), ALU.mult).then_inc(at("rf_ready", g)[0], 1)
                vc.tensor_tensor(slot(u, KF), banks[bk][:, :], slot(u, EFN), ALU.mult).then_inc(at("kf_ready", g)[0], 1)
                dve.wait_ge(*at("eb_ready", g))
                vc.tensor_tensor(slot(u, RB), banks[br_][:, :], slot(u, EBN), ALU.mult).then_inc(emptied[br_], 1)
                vc.tensor_tensor(slot(u, KB), banks[bk][:, :], slot(u, CB), ALU.mult).then_inc(emptied[bk], 1)

            def state(p):
                b, v = p.result("state")
                dve.wait_ge(full[b], v)
                vc.tensor_tensor(slot(p.u, SBD).rearrange("p (c d) -> p c d", c=4),
                                 banks[b][:, :].rearrange("p (c d) -> p c d", c=4),
                                 blockdiag[:, :].unsqueeze(1).to_broadcast([P, 4, P]), ALU.mult)\
                  .then_inc(emptied[b], 1)

            def blocks(c):
                def f(p):
                    for i in range(2):
                        k = 2 * c + i
                        b, v = p.result(f"blocks{c}", i)
                        dve.wait_ge(*at("low_copied", p.g, k + 1))
                        apart(dve, "dve")
                        vc.copy_predicated(slot(p.u, AB, 8)[:, k * 256:(k + 1) * 256],
                                           above[:, :, :].rearrange("p e i -> p (e i)").bitcast(i32),
                                           banks[b][:, 256:512]).then_inc(emptied[b], 1)
                return f

            def heads(x):
                return x.rearrange("p (h d) -> p h d", d=HD)

            def y(p):
                u = p.u
                b, v = p.y_result(1)
                dve.wait_ge(full[b], v)
                chain_.link(p, vc.reduce_sum(gn[u][:, 0, :], heads(banks[b][:, :]), AX.X))
                chain_.link(p, vc.tensor_scalar(gn[u][:, 0, :], gn[u][:, 0, :], 1.0 / HD, None, ALU.mult))
                vc.tensor_tensor(heads(slot(u, YC)), heads(banks[b][:, :]),
                                 gn[u][:, 0, :].unsqueeze(2).to_broadcast([P, TT * NH, HD]), ALU.subtract)\
                  .then_inc(emptied[b], 1)

            def head_var(p):
                u = p.u
                var, root, bits = (gn[u][:, i, :] for i in (1, 2, 0))
                dve.wait_ge(*at("squared", p.g))
                chain_.link(p, vc.reduce_sum(var, heads(slot(u, SQ)), AX.X))
                chain_.link(p, vc.tensor_scalar(var, var, 1.0 / HD, GN_EPS, ALU.mult, ALU.add))
                chain_.link(p, vc.tensor_scalar(bits.bitcast(i32), var.bitcast(i32), 1, None, ALU.logical_shift_right))
                chain_.link(p, vc.tensor_scalar(root.bitcast(i32), bits.bitcast(i32), -1.0, float(0x5f3759df),
                                                ALU.mult, ALU.add))

            def head_root(p):
                u = p.u
                var, root, sq = (gn[u][:, i, :] for i in (1, 2, 3))
                for _ in range(3):
                    chain_.link(p, vc.tensor_tensor(sq, root, root, ALU.mult))
                    chain_.link(p, vc.scalar_tensor_tensor(out=sq, in0=sq, scalar=-0.5, in1=var, op0=ALU.mult,
                                                           op1=ALU.mult))
                    chain_.link(p, vc.scalar_tensor_tensor(out=root, in0=sq, scalar=1.5, in1=root, op0=ALU.add,
                                                           op1=ALU.mult))

            def head_norm(p):
                u = p.u
                root = gn[u][:, 2, :]
                chain_.link(p, vc.tensor_tensor(heads(slot(u, ZN)), heads(slot(u, YC)),
                                                root.unsqueeze(2).to_broadcast([P, TT * NH, HD]), ALU.mult))
                dve.wait_ge(*at("affine_ready", p.g))
                chain_.link(p, vc.tensor_tensor(slot(u, ZN), slot(u, ZN), slot(u, GW), ALU.mult))
                chain_.link(p, vc.tensor_tensor(slot(u, ZN), slot(u, ZN), slot(u, GB), ALU.add))
                vc.tensor_scalar(slot(u, ZG), slot(u, ZN), 0.5, None, ALU.mult).then_inc(at("gated_ready", p.g)[0], 1)

            def mix_out(p):
                u = p.u
                b, v = p.result("mix_out")
                dve.wait_ge(full[b], v)
                vc.tensor_tensor(slot(u, HF), banks[b][:, :], slot(u, H), ALU.add).then_inc(emptied[b], 1)
                dve.wait_ge(emptied[b], v)
                moments(p, 4, two(u, HF))

            def gate_up(c):
                def f(p):
                    u = p.u
                    bg, vg = p.result(f"gate_up{c}", 0)
                    bu, vu = p.result(f"gate_up{c}", 1)
                    dve.wait_ge(*at("tanh_gate", p.g, c + 1))
                    vc.scalar_tensor_tensor(out=slot(u, SF + c), in0=slot(u, THF + c), scalar=1.0,
                                            in1=banks[bg][:, :], op0=ALU.add, op1=ALU.mult).then_inc(emptied[bg], 1)
                    dve.wait_ge(full[bu], vu)
                    dve.wait_ge(emptied[bg], vg)
                    vc.scalar_tensor_tensor(out=slot(u, HM + c), in0=slot(u, SF + c), scalar=0.5,
                                            in1=banks[bu][:, :], op0=ALU.mult, op1=ALU.mult).then_inc(emptied[bu], 1)
                return f

            def down(p):
                b, v = p.result("down")
                dve.wait_ge(full[b], v)
                dve.wait_ge(out_free[p.u], p.j * 16 + 16)
                vc.tensor_tensor(out_sb[p.u][:, :, :], bank2(b), two(p.u, HF), ALU.add).then_inc(emptied[b], 1)

            run(dve, {"norm0": norm0, "norm1": norm1, "qkv": qkv, "scores": scores, "attT": attT,
                      "attn_out": attn_out, "xT0": xT0, "ffn_v": ffn_v, "xT1": xT1, "mixA": mix("mixA"),
                      "mixB": mix("mixB"), "gate": gate, "decay": decay, "factors": factors, "state": state,
                      "blocks0": blocks(0), "blocks1": blocks(1), "blocks2": blocks(2), "blocks3": blocks(3),
                      "blocks4": blocks(4), "blocks5": blocks(5), "blocks6": blocks(6), "blocks7": blocks(7), "yT": y,
                      "head_var": head_var, "head_root": head_root, "head_norm": head_norm, "mix_out": mix_out,
                      "gate_up0": gate_up(0), "gate_up1": gate_up(1), "gate_up2": gate_up(2), "down": down})

        @block.tensor
        def _(pe):
            mm = nc.tensor.matmul

            def block_t(b, c, src, cols=P):
                return nc.tensor.transpose(banks[b][0:cols, c * P:c * P + src.shape[0]], src,
                                           ident[0:src.shape[0], 0:src.shape[0]])

            pe.wait_ge(ident_made, 1)
            n = 0
            pe.wait_ge(poles_made, 1)
            for part in range(2):
                for tt in range(TT):
                    last = block_t(n % NB, part * TT + tt, pole[:, part, tt].rearrange("p d n -> p (d n)"))
            last.then_inc(full[n % NB], 1)
            blk = 0
            for part in (1, 0):
                pe.wait_ge(cb_made[part], 1)
                for b in range(B):
                    for tt in range(TT):
                        n = PRE_POLE + blk // 4
                        if blk % 4 == 0 and n >= NB:
                            pe.wait_ge(emptied[n % NB], n // NB)
                        last = block_t(n % NB, blk % 4, cb_nat[:, part, b, tt].rearrange("p d n -> p (d n)"))
                        if blk % 4 == 3:
                            last.then_inc(full[n % NB], 1)
                        blk += 1
            blk = 0
            for k, (name, o, i) in enumerate(WEIGHTS):
                pe.wait_ge(weights_in[k], 16)
                if name in ("gate", "up", "down"):
                    pe.wait_ge(dequantized, k - 9)
                src = nat[name].rearrange("p (o i) -> p o i", i=i)
                for kt in range(i // P):
                    for ot in range(o // P):
                        n = PRE_A + blk // 4
                        if blk % 4 == 0:
                            pe.wait_ge(emptied[n % NB], n // NB)
                        last = block_t(n % NB, blk % 4, src[:, ot, kt * P:(kt + 1) * P])
                        if blk % 4 == 3:
                            last.then_inc(full[n % NB], 1)
                        blk += 1
            n = PRE_ALL - 1
            pe.wait_ge(emptied[n % NB], n // NB)
            pe.wait_ge(vec_in, 16 * 12)
            block_t(n % NB, 0, vec_rows[:, :]).then_inc(full[n % NB], 1)
            with pe.Fori(0, GEN_ROUNDS) as r:
                for c in range(2):
                    pe.wait_ge(p_made, (r * 2 + c) + 3)
                    pe.wait_ge(cross_made, (r * 2 + c) + 1)
                    for h in range(2):
                        b = 2 * c + h
                        pe.wait_ge(emptied[b], r + USED_A[b])
                        for t in range(TC // 2):
                            tl = h * (TC // 2) + t
                            for rows in (slice(0, B * HI // 2), slice(B * HI // 2, B * HI)):
                                for x, part in enumerate((pb[c], cross[c])):
                                    last = mm(banks[b][rows, t * LO:(t + 1) * LO],
                                              part[:, tl].rearrange("p b a -> p (b a)")[:, rows], q1[c][:, tl, :],
                                              start=(x == 0), stop=(x == 1))
                        last.then_inc(full[b], 1)
            pe.wait_ge(small_in, 16 * 9)

            def free_bank(p, step, k=0):
                b, v = p.result(step, k)
                pe.wait_ge(emptied[b], v - 1)
                return b

            def wait_emptied(p, step, k=0):
                b, v = p.result(step, k)
                pe.wait_ge(emptied[b], v)

            def transposes(p, step, s):
                transposed_to(free_bank(p, step), p, s)

            def transposed_to(b, p, s):
                for tt in range(TT):
                    for ft in range(FT):
                        last = nc.tensor.transpose(bank2(b)[:, ft, tt * P:(tt + 1) * P],
                                                   two(p.u, s)[:, tt, ft * P:(ft + 1) * P], ident[:, :])
                last.then_inc(full[b], 1)

            def feature_major(b, name, x, c0=0):
                for ft in range(FT):
                    for kt in range(FT):
                        last = mm(bank2(b)[:, ft, :], w(name, kt, c0 + ft * P, P), x[:, kt, :],
                                  start=(kt == 0), stop=(kt == FT - 1))
                last.then_inc(full[b], 1)

            def token_major(b, name, x, kts=FT):
                for tt in range(TT):
                    for kt in range(kts):
                        last = mm(bank2(b)[:, tt, :], x(kt, tt), w(name, kt, 0, D),
                                  start=(kt == 0), stop=(kt == kts - 1))
                last.then_inc(full[b], 1)

            def tok(u, s):
                return lambda kt, tt: two(u, s)[:, kt, tt * P:(tt + 1) * P]

            def after_norm(step, n, s):
                def f(p):
                    pe.wait_ge(normed[norm_at(p, n)[0]], norm_at(p, n)[1])
                    transposes(p, step, s)
                return f

            def qkv(p):
                u = p.u
                wait_emptied(p, "hT")
                for tt in range(TT):
                    b = free_bank(p, "qkv", tt)
                    for kt in range(FT):
                        last = mm(banks[b][:, :], two(u, HTs)[:, kt, tt * P:(tt + 1) * P],
                                  w("qkv", kt, 0, 2 * D), start=(kt == 0), stop=(kt == FT - 1))
                    last.then_inc(full[b], 1)
                feature_major(free_bank(p, "qkv", 2), "qkv", two(u, HTs), c0=2 * D)

            def scores(p):
                u = p.u
                wait_emptied(p, "qkv", 0)
                wait_emptied(p, "qkv", 1)
                b = free_bank(p, "scores")
                for qt in range(FT):
                    for tt in range(TT):
                        last = mm(bank2(b)[:, qt, :], slot(u, QK + tt)[:, qt * P:(qt + 1) * P],
                                  slot(u, QK + tt)[:, D:2 * D], start=(tt == 0), stop=(tt == TT - 1))
                last.then_inc(full[b], 1)

            def probsT(p):
                wait_emptied(p, "qkv", 2)
                wait_emptied(p, "scores")
                transposes(p, "probsT", EX)

            def attT(p):
                u = p.u
                wait_emptied(p, "probsT")
                b = free_bank(p, "attT")
                for qt in range(FT):
                    for kt in range(FT):
                        last = mm(bank2(b)[:, qt, :], two(u, PT)[:, kt, qt * P:(qt + 1) * P],
                                  two(u, VT)[:, kt, :], start=(kt == 0), stop=(kt == FT - 1))
                last.then_inc(full[b], 1)

            def attn_out(p):
                wait_emptied(p, "attT")
                token_major(free_bank(p, "attn_out"), "proj", tok(p.u, AT_))

            def ffn_kr(p):
                pe.wait_ge(*at("xk_ready", p.g))
                feature_major(free_bank(p, "ffn_kr", 0), "ffn_k", two(p.u, XK))
                pe.wait_ge(*at("xr_ready", p.g))
                token_major(free_bank(p, "ffn_kr", 1), "ffn_r", tok(p.u, XR))

            def ffn_v(p):
                pe.wait_ge(*at("ksq_ready", p.g))
                token_major(free_bank(p, "ffn_v"), "ffn_v", tok(p.u, KSQ))

            def lowrank(p):
                pe.wait_ge(*at("xm_ready", p.g))
                b = free_bank(p, "lowrank")
                for c0, cn in ((0, P), (P, MIX)):
                    for kt in range(FT):
                        last = mm(bank2(b)[0:cn, c0 // P, :], w1[:, kt, c0:c0 + cn], two(p.u, XM)[:, kt, :],
                                  start=(kt == 0), stop=(kt == FT - 1))
                last.then_inc(full[b], 1)

            def mix(step):
                def f_(p):
                    if step == "mixA":
                        pe.wait_ge(*at("xxx_ready", p.g))
                    for i, f in enumerate(MIXES[step]):
                        b = free_bank(p, step, i)
                        q = f % 4
                        for ft in range(FT):
                            lhs = (w2a if f < 4 else w2b)[MIX * q:MIX * (q + 1), ft * P:(ft + 1) * P]
                            rhs = slot(p.u, XXX)[MIX * q:MIX * (q + 1), (f // 4) * T:(f // 4 + 1) * T]
                            last = mm(bank2(b)[:, ft, :], lhs, rhs, start=True, stop=True)
                        last.then_inc(full[b], 1)
                return f_

            def low(p):
                pe.wait_ge(*at("mixed", p.g, 1))
                b = free_bank(p, "low")
                for kt in range(FT):
                    last = mm(banks[b][0:DEC, 0:T], dw1[:, kt, :], two(p.u, XF)[:, kt, :],
                              start=(kt == 0), stop=(kt == FT - 1))
                last.then_inc(full[b], 1)

            def key(p):
                pe.wait_ge(*at("mixed", p.g, 2))
                feature_major(free_bank(p, "key"), "k", two(p.u, XF + 1))

            def value(p):
                pe.wait_ge(*at("mixed", p.g, 3))
                token_major(free_bank(p, "value"), "v", tok(p.u, XF + 2))

            def query(p):
                pe.wait_ge(*at("mixed", p.g, 4))
                feature_major(free_bank(p, "query"), "r", two(p.u, XF + 3))

            def gate(p):
                pe.wait_ge(*at("mixed", p.g, 5))
                token_major(free_bank(p, "gate"), "g", tok(p.u, XF + 4))

            def decay(p):
                wait_emptied(p, "low")
                b = free_bank(p, "decay")
                for ft in range(FT):
                    last = mm(bank2(b)[:, ft, :], dw2[:, ft * P:(ft + 1) * P], slot(p.u, ZT)[0:DEC, 0:T],
                              start=True, stop=True)
                last.then_inc(full[b], 1)


            def keys(p):
                pe.wait_ge(*at("kf_ready", p.g))
                wait_emptied(p, "key")
                b = free_bank(p, "keys")
                for x, s in enumerate((KF, KB)):
                    for ft in range(FT):
                        last = nc.tensor.transpose(bank2(b)[:, x, ft * P:(ft + 1) * P],
                                                   two(p.u, s)[:, ft, x * P:(x + 1) * P], ident[:, :])
                last.then_inc(full[b], 1)

            def state(p):
                u = p.u
                wait_emptied(p, "keys")
                wait_emptied(p, "value")
                b = free_bank(p, "state")
                for x in range(2):
                    for ft in range(FT):
                        c = (x * FT + ft) * P
                        last = mm(banks[b][:, c:c + P], two(u, KTM)[:, x, ft * P:(ft + 1) * P],
                                  two(u, VV)[:, x, ft * P:(ft + 1) * P], start=True, stop=True)
                last.then_inc(full[b], 1)

            def blocks(c):
                def f(p):
                    u = p.u
                    if c == 0:
                        pe.wait_ge(*at("rfm_ready", p.g))
                        pe.wait_ge(*at("rbm_ready", p.g))
                    ft, jb = c // 4, (c // 2) % 2
                    bs = [free_bank(p, f"blocks{c}", i) for i in range(2)]
                    for x, (ks_, rs_) in enumerate(((KF, RFM), (KB, RBM))):
                        for i in range(2):
                            q = 2 * (c % 2) + i
                            rows = slice(32 * q, 32 * q + 32)
                            last = mm(banks[bs[i]][:, x * 256:(x + 1) * 256],
                                      two(u, ks_)[rows, ft, jb * P:(jb + 1) * P],
                                      slot(u, rs_, 2)[rows, (ft * 2 + jb) * 256:(ft * 2 + jb + 1) * 256],
                                      start=True, stop=True)
                            if x == 1:
                                last.then_inc(full[bs[i]], 1)
                return f

            def y(part):
                def f(p):
                    u = p.u
                    if part == 0:
                        wait_emptied(p, "state")
                        pe.wait_ge(*at("ve_ready", p.g))
                        b, v = p.y_result(0)
                        pe.wait_ge(emptied[b], v - 1)
                        for x, (s, tt) in enumerate(((RF, 1), (RB, 0))):
                            for ft in range(FT):
                                c = (x * FT + ft) * P
                                mm(bank2(b)[:, ft, tt * P:(tt + 1) * P], slot(u, SBD)[:, c:c + P],
                                   two(u, s)[:, ft, tt * P:(tt + 1) * P], start=(x == 0 and ft == 0), stop=False,
                                   skip_group_check=True)
                    else:
                        b, _ = p.y_result(0)
                    ft, jb = part // 2, part % 2
                    for q in range(4):
                        wait_emptied(p, f"blocks{2 * part + q // 2}", q % 2)
                        for e in range(2):
                            c = (((jb * NH // 2) + ft * 4 + q) * 2 + e) * 2 * HD
                            last = mm(bank2(b)[2 * HD * q:2 * HD * (q + 1), ft, jb * P:(jb + 1) * P],
                                      slot(u, VE, 2)[:, c:c + 2 * HD],
                                      slot(u, AB, 8)[:, (4 * part + q) * 256 + e * P:(4 * part + q) * 256 + (e + 1) * P],
                                      start=False, stop=(part == 3 and q == 3 and e == 1), skip_group_check=True)
                    if part == 3:
                        last.then_inc(full[b], 1)
                return f

            def yT(p):
                b, v = p.y_result(1)
                pe.wait_ge(emptied[b], v - 1)
                transposed_to(b, p, YF)

            def gatedT(p):
                pe.wait_ge(*at("gated_ready", p.g))
                transposes(p, "gatedT", ZG)

            def mix_out(p):
                wait_emptied(p, "gatedT")
                token_major(free_bank(p, "mix_out"), "o", tok(p.u, ZTs))

            def gate_up(c):
                def f(p):
                    if c == 0:
                        wait_emptied(p, "xT2")
                    x = xT[p.u][:, :, 1:T + 1]
                    feature_major(free_bank(p, f"gate_up{c}", 0), "gate", x, c0=2 * c * P)
                    feature_major(free_bank(p, f"gate_up{c}", 1), "up", x, c0=2 * c * P)
                return f

            def down(p):
                for c in range(3):
                    wait_emptied(p, f"gate_up{c}", 1)
                token_major(free_bank(p, "down"), "down",
                            lambda kt, tt: two(p.u, HM + kt // 2)[:, kt % 2, tt * P:(tt + 1) * P], kts=HT)

            run(pe, {"hT": after_norm("hT", 1, N0), "qkv": qkv, "scores": scores, "probsT": probsT, "attT": attT,
                     "attn_out": attn_out, "xT0": after_norm("xT0", 2, TN), "ffn_kr": ffn_kr, "ffn_v": ffn_v,
                     "xT1": after_norm("xT1", 3, XN), "lowrank": lowrank, "mixA": mix("mixA"), "mixB": mix("mixB"),
                     "low": low, "key": key, "value": value, "query": query, "gate": gate, "decay": decay,
                     "keys": keys, "state": state, "blocks0": blocks(0), "blocks1": blocks(1), "blocks2": blocks(2),
                     "blocks3": blocks(3), "blocks4": blocks(4), "blocks5": blocks(5), "blocks6": blocks(6),
                     "blocks7": blocks(7), "y0": y(0), "y1": y(1), "y2": y(2), "y3": y(3), "yT": yT, "gatedT": gatedT,
                     "mix_out": mix_out, "xT2": after_norm("xT2", 4, XN), "gate_up0": gate_up(0),
                     "gate_up1": gate_up(1), "gate_up2": gate_up(2), "down": down})



_INS = ['x', 'L0_tok_log_dt', 'L0_tok_inv_A_real', 'L0_tok_A_imag', 'L0_tok_B_ri', 'L0_attn_norm_w', 'L0_attn_norm_b',
        'L0_attn_qkv_w', 'L0_attn_qkv_b', 'L0_attn_proj_w', 'L0_attn_proj_b', 'L0_ffn_W_r', 'L0_ffn_W_k', 'L0_ffn_W_v',
        'L0_ffn_mu_r', 'L0_ffn_mu_k', 'L1_attn_time_maa_x', 'L1_attn_time_maa_w', 'L1_attn_time_maa_k',
        'L1_attn_time_maa_v', 'L1_attn_time_maa_r', 'L1_attn_time_maa_g', 'L1_attn_time_maa_w1', 'L1_attn_time_maa_w2',
        'L1_attn_time_decay', 'L1_attn_time_decay_w1', 'L1_attn_time_decay_w2', 'L1_attn_W_r', 'L1_attn_W_k',
        'L1_attn_W_v', 'L1_attn_W_g', 'L1_attn_W_o', 'L1_attn_ln_w', 'L1_attn_ln_b', 'L1_ffn_w_gate', 'L1_ffn_w_up',
        'L1_ffn_w_down']


def kernel(**inputs):
    import numpy as _np
    import concourse.bacc as _bacc
    from concourse import mybir as _mybir
    from concourse.bass_utils import run_bass_kernel_spmd as _run

    nc = _bacc.Bacc("TRN2", target_bir_lowering=False, num_devices=1)
    arrays, t_in = {}, {}
    for name in _INS:
        a = _np.ascontiguousarray(inputs[name])
        arrays[f"in_{name}"] = a
        t_in[name] = nc.dram_tensor(f"in_{name}", a.shape, _mybir.dt.from_np(a.dtype), kind="ExternalInput").ap()
    out = nc.dram_tensor("out_0", (B, T, D), f32, kind="ExternalOutput").ap()
    mk_vit_tower(nc, t_in, out)
    r = _run(nc, [arrays], core_ids=[0])
    return r.results[0]["out_0"]
```
